# Optimizing a Trainium2 kernel written in Bass

```python
import numpy as np
import jax
import jax.numpy as jnp

def _softmax(x, axis=-1):
    return jax.nn.softmax(x, axis=axis)

def _gelu(x):
    return jax.nn.gelu(x, approximate=True)

def _silu(x):
    return jax.nn.silu(x)

def _sigmoid(x):
    return jax.nn.sigmoid(x)

def _layernorm(x, axis=-1, eps=1e-05):
    m = jnp.mean(x, axis=axis, keepdims=True)
    v = jnp.var(x, axis=axis, keepdims=True)
    return (x - m) / jnp.sqrt(v + eps)

def _scatter_add(tgt, idx, src, axis=0):
    return tgt.at[idx].add(src)

def _segment_sum(src, seg, n):
    return jax.ops.segment_sum(src, seg, n)
kernel_name = 'mk_seq_preln_d2_jaxref_r8_228978'

def setup_inputs(seed: int=0):
    np.random.seed(seed)
    _w = jnp.asarray

    def _L0_attn_setup():
        import jax, jax.numpy as jnp
        import numpy as np
        RMS_EPS = 1e-05

        def _l2norm(t):
            return t / jnp.linalg.norm(t, axis=-1, keepdims=True)

        def _delta_rule(q, k, v, beta):
            B, H, N, Dk = q.shape
            Dv = v.shape[-1]
            qT = jnp.moveaxis(q, 2, 0)
            kT = jnp.moveaxis(k, 2, 0)
            vT = jnp.moveaxis(v, 2, 0)
            bT = jnp.moveaxis(beta, 2, 0)

            def step(S, inp):
                q_t, k_t, v_t, b_t = inp
                pred = jnp.einsum('bhk,bhkv->bhv', k_t, S)
                err = (v_t - pred) * b_t[..., None]
                S = S + jnp.einsum('bhk,bhv->bhkv', k_t, err)
                o_t = jnp.einsum('bhk,bhkv->bhv', q_t, S)
                return (S, o_t)
            S0 = jnp.zeros((B, H, Dk, Dv), q.dtype)
            _, oT = jax.lax.scan(step, S0, (qT, kT, vT, bT))
            return jnp.moveaxis(oT, 0, 2)
        key = jax.random.key(seed)
        ks = jax.random.split(key, 7)
        B, N, D, H = (8, 128, 128, 4)
        Dv = D // H
        s = lambda k, shp, fan: jax.random.normal(k, shp, jnp.float32) * (1.0 / np.sqrt(fan))
        return {'x': jax.random.normal(ks[0], (B, N, D), jnp.float32), 'Wq': s(ks[1], (D, D), D), 'Wk': s(ks[2], (D, D), D), 'Wv': s(ks[3], (D, D), D), 'Wbeta': s(ks[4], (D, H), D), 'Wo': s(ks[5], (D, D), D), 'g_norm': jnp.ones((Dv,), jnp.float32)}
    _L0_attn_in = _L0_attn_setup()

    def _L0_ffn_setup():
        import jax, jax.numpy as jnp
        import numpy as np
        B, S, H, NH, E, F = (4, 128, 128, 16, 8, 512)
        D = H // NH
        EPS = 1e-05

        def _layernorm(x, g, b):
            mu = jnp.mean(x, axis=-1, keepdims=True)
            var = jnp.var(x, axis=-1, keepdims=True)
            return (x - mu) * jax.lax.rsqrt(var + EPS) * g + b
        key = jax.random.key(seed)
        ks = jax.random.split(key, 16)
        s = 0.02
        return {'x': jax.random.normal(ks[0], (B, S, H), jnp.float32), 'ln1_g': jnp.ones((H,), jnp.float32), 'ln1_b': jnp.zeros((H,), jnp.float32), 'ln2_g': jnp.ones((H,), jnp.float32), 'ln2_b': jnp.zeros((H,), jnp.float32), 'wq': jax.random.normal(ks[1], (H, H), jnp.float32) * s, 'bq': jnp.zeros((H,), jnp.float32), 'wk': jax.random.normal(ks[2], (H, H), jnp.float32) * s, 'bk': jnp.zeros((H,), jnp.float32), 'wv': jax.random.normal(ks[3], (H, H), jnp.float32) * s, 'bv': jnp.zeros((H,), jnp.float32), 'wo': jax.random.normal(ks[4], (H, H), jnp.float32) * s, 'bo': jnp.zeros((H,), jnp.float32), 'gate_w': jax.random.normal(ks[5], (H, E), jnp.float32) * s, 'gate_b': jnp.zeros((E,), jnp.float32), 'w1': jax.random.normal(ks[6], (E, H, F), jnp.float32) * s, 'b1': jnp.zeros((E, F), jnp.float32), 'w2': jax.random.normal(ks[7], (E, F, H), jnp.float32) * s, 'b2': jnp.zeros((E, H), jnp.float32)}
    _L0_ffn_in = _L0_ffn_setup()

    def _L1_attn_setup():
        import jax, jax.numpy as jnp
        import numpy as np
        HEADS = 32
        DIM_HEAD = 32
        EPS = 1e-06
        key = jax.random.key(seed)
        k1, k2, k3 = jax.random.split(key, 3)
        b, n, dim = (2, 256, 128)
        x = jax.random.normal(k1, (b, n, dim), dtype=jnp.float32)
        w_qkv = jax.random.normal(k2, (dim, 3 * HEADS * DIM_HEAD), dtype=jnp.float32) * dim ** (-0.5)
        w_out = jax.random.normal(k3, (HEADS * DIM_HEAD, dim), dtype=jnp.float32) * dim ** (-0.5)
        b_out = jnp.zeros((dim,), dtype=jnp.float32)
        ln_gamma = jnp.ones((dim,), dtype=jnp.float32)
        ln_beta = jnp.zeros((dim,), dtype=jnp.float32)
        return {'x': x, 'w_qkv': w_qkv, 'w_out': w_out, 'b_out': b_out, 'ln_gamma': ln_gamma, 'ln_beta': ln_beta}
    _L1_attn_in = _L1_attn_setup()

    def _L1_ffn_setup():
        import jax, jax.numpy as jnp
        import numpy as np
        B, N, D = (4, 256, 128)
        SPARSITY = 0.01
        key = jax.random.key(seed)
        k1, k2, k3 = jax.random.split(key, 3)
        x = jax.random.normal(k1, (B, N, D), dtype=jnp.float32)
        spatial = jax.random.normal(k2, (D, D), dtype=jnp.float32) * 0.02
        freq = jnp.fft.fft(spatial, axis=-1)
        k = int(D * SPARSITY)
        mag = jnp.abs(freq)
        kth = jax.lax.top_k(mag, k)[0][:, -1:]
        w_sparse = jnp.where(mag >= kth, freq, 0.0 + 0j)
        bias = jax.random.normal(k3, (D,), dtype=jnp.float32) * 0.01
        return {'x': x, 'w_freq_real': jnp.real(w_sparse).astype(jnp.float32), 'w_freq_imag': jnp.imag(w_sparse).astype(jnp.float32), 'bias': bias}
    _L1_ffn_in = _L1_ffn_setup()
    _d = {'L0_attn_x': _L0_attn_in['x'], 'L0_attn_Wq': _L0_attn_in['Wq'], 'L0_attn_Wk': _L0_attn_in['Wk'], 'L0_attn_Wv': _L0_attn_in['Wv'], 'L0_attn_Wbeta': _L0_attn_in['Wbeta'], 'L0_attn_Wo': _L0_attn_in['Wo'], 'L0_attn_g_norm': _L0_attn_in['g_norm'], 'L0_ffn_ln1_g': _L0_ffn_in['ln1_g'], 'L0_ffn_ln1_b': _L0_ffn_in['ln1_b'], 'L0_ffn_ln2_g': _L0_ffn_in['ln2_g'], 'L0_ffn_ln2_b': _L0_ffn_in['ln2_b'], 'L0_ffn_wq': _L0_ffn_in['wq'], 'L0_ffn_bq': _L0_ffn_in['bq'], 'L0_ffn_wk': _L0_ffn_in['wk'], 'L0_ffn_bk': _L0_ffn_in['bk'], 'L0_ffn_wv': _L0_ffn_in['wv'], 'L0_ffn_bv': _L0_ffn_in['bv'], 'L0_ffn_wo': _L0_ffn_in['wo'], 'L0_ffn_bo': _L0_ffn_in['bo'], 'L0_ffn_gate_w': _L0_ffn_in['gate_w'], 'L0_ffn_gate_b': _L0_ffn_in['gate_b'], 'L0_ffn_w1': _L0_ffn_in['w1'], 'L0_ffn_b1': _L0_ffn_in['b1'], 'L0_ffn_w2': _L0_ffn_in['w2'], 'L0_ffn_b2': _L0_ffn_in['b2'], 'L1_attn_w_qkv': _L1_attn_in['w_qkv'], 'L1_attn_w_out': _L1_attn_in['w_out'], 'L1_attn_b_out': _L1_attn_in['b_out'], 'L1_attn_ln_gamma': _L1_attn_in['ln_gamma'], 'L1_attn_ln_beta': _L1_attn_in['ln_beta'], 'L1_ffn_w_freq_real': _L1_ffn_in['w_freq_real'], 'L1_ffn_w_freq_imag': _L1_ffn_in['w_freq_imag'], 'L1_ffn_bias': _L1_ffn_in['bias']}
    _x0 = _d['L0_attn_x']
    _d['L0_attn_x'] = jax.random.normal(jax.random.fold_in(jax.random.key(seed), 1), (8, 512, 128), dtype=_x0.dtype)
    del _x0
    return _d

def reference(L0_attn_x, L0_attn_Wq, L0_attn_Wk, L0_attn_Wv, L0_attn_Wbeta, L0_attn_Wo, L0_attn_g_norm, L0_ffn_ln1_g, L0_ffn_ln1_b, L0_ffn_ln2_g, L0_ffn_ln2_b, L0_ffn_wq, L0_ffn_bq, L0_ffn_wk, L0_ffn_bk, L0_ffn_wv, L0_ffn_bv, L0_ffn_wo, L0_ffn_bo, L0_ffn_gate_w, L0_ffn_gate_b, L0_ffn_w1, L0_ffn_b1, L0_ffn_w2, L0_ffn_b2, L1_attn_w_qkv, L1_attn_w_out, L1_attn_b_out, L1_attn_ln_gamma, L1_attn_ln_beta, L1_ffn_w_freq_real, L1_ffn_w_freq_imag, L1_ffn_bias):

    def _L0_attn_ref(x, Wq, Wk, Wv, Wbeta, Wo, g_norm):
        import jax, jax.numpy as jnp
        import numpy as np
        RMS_EPS = 1e-05

        def _l2norm(t):
            return t / jnp.linalg.norm(t, axis=-1, keepdims=True)

        def _delta_rule(q, k, v, beta):
            B, H, N, Dk = q.shape
            Dv = v.shape[-1]
            qT = jnp.moveaxis(q, 2, 0)
            kT = jnp.moveaxis(k, 2, 0)
            vT = jnp.moveaxis(v, 2, 0)
            bT = jnp.moveaxis(beta, 2, 0)

            def step(S, inp):
                q_t, k_t, v_t, b_t = inp
                pred = jnp.einsum('bhk,bhkv->bhv', k_t, S)
                err = (v_t - pred) * b_t[..., None]
                S = S + jnp.einsum('bhk,bhv->bhkv', k_t, err)
                o_t = jnp.einsum('bhk,bhkv->bhv', q_t, S)
                return (S, o_t)
            S0 = jnp.zeros((B, H, Dk, Dv), q.dtype)
            _, oT = jax.lax.scan(step, S0, (qT, kT, vT, bT))
            return jnp.moveaxis(oT, 0, 2)
        B, N, D = x.shape
        H = Wbeta.shape[1]
        Dk = Wq.shape[1] // H
        Dv = Wv.shape[1] // H
        split = lambda t, d: t.reshape(B, N, H, d).transpose(0, 2, 1, 3)
        q = _l2norm(split(x @ Wq, Dk))
        k = _l2norm(split(x @ Wk, Dk))
        v = split(x @ Wv, Dv)
        beta = jax.nn.sigmoid(x @ Wbeta).transpose(0, 2, 1)
        o = _delta_rule(q, k, v, beta)
        o = o * jax.lax.rsqrt(jnp.mean(o * o, axis=-1, keepdims=True) + RMS_EPS) * g_norm
        o = o.transpose(0, 2, 1, 3).reshape(B, N, H * Dv)
        return o @ Wo

    def _L0_ffn_ref(x, ln1_g, ln1_b, ln2_g, ln2_b, wq, bq, wk, bk, wv, bv, wo, bo, gate_w, gate_b, w1, b1, w2, b2):
        import jax, jax.numpy as jnp
        import numpy as np
        B, S, H, NH, E, F = (4, 128, 128, 16, 8, 512)
        D = H // NH
        EPS = 1e-05

        def _layernorm(x, g, b):
            mu = jnp.mean(x, axis=-1, keepdims=True)
            var = jnp.var(x, axis=-1, keepdims=True)
            return (x - mu) * jax.lax.rsqrt(var + EPS) * g + b
        b, s, h = x.shape
        hn = _layernorm(x, ln1_g, ln1_b)
        q = (hn @ wq + bq).reshape(b, s, NH, D).transpose(0, 2, 1, 3)
        k = (hn @ wk + bk).reshape(b, s, NH, D).transpose(0, 2, 1, 3)
        v = (hn @ wv + bv).reshape(b, s, NH, D).transpose(0, 2, 1, 3)
        scores = jnp.einsum('bhqd,bhkd->bhqk', q, k) / jnp.sqrt(jnp.float32(D))
        attn = jax.nn.softmax(scores, axis=-1)
        o = jnp.einsum('bhqk,bhkd->bhqd', attn, v)
        o = o.transpose(0, 2, 1, 3).reshape(b, s, h)
        x = x + (o @ wo + bo)
        hn2 = _layernorm(x, ln2_g, ln2_b).reshape(-1, h)
        logits = hn2 @ gate_w + gate_b
        idx = jnp.argmax(logits, axis=-1)
        mid = jax.nn.relu(jnp.einsum('th,ehf->etf', hn2, w1) + b1[:, None, :])
        y = jnp.einsum('etf,efh->eth', mid, w2) + b2[:, None, :]
        moe = y[idx, jnp.arange(hn2.shape[0])]
        return x + moe.reshape(b, s, h)

    def _L1_attn_ref(x, w_qkv, w_out, b_out, ln_gamma, ln_beta):
        import jax, jax.numpy as jnp
        import numpy as np
        HEADS = 32
        DIM_HEAD = 32
        EPS = 1e-06
        b, n, dim = x.shape
        scale = DIM_HEAD ** (-0.5)
        qkv = x @ w_qkv
        qkv = qkv.reshape(b, n, 3, HEADS, DIM_HEAD)
        qkv = jnp.transpose(qkv, (2, 0, 3, 1, 4))
        q, k, v = (qkv[0], qkv[1], qkv[2])
        dots = jnp.einsum('bhnd,bhmd->bhnm', q, k) * scale
        attn = jax.nn.softmax(dots, axis=-1)
        out = jnp.einsum('bhnm,bhmd->bhnd', attn, v)
        out = jnp.transpose(out, (0, 2, 1, 3)).reshape(b, n, HEADS * DIM_HEAD)
        out = out @ w_out + b_out
        mu = jnp.mean(out, axis=-1, keepdims=True)
        var = jnp.mean((out - mu) ** 2, axis=-1, keepdims=True)
        out = (out - mu) / jnp.sqrt(var + EPS) * ln_gamma + ln_beta
        return out

    def _L1_ffn_ref(x, w_freq_real, w_freq_imag, bias):
        import jax, jax.numpy as jnp
        import numpy as np
        B, N, D = (4, 256, 128)
        SPARSITY = 0.01
        w = jax.lax.complex(w_freq_real, w_freq_imag)
        x_freq = jnp.fft.fft(x, axis=-1)
        y_freq = jnp.einsum('bnd,do->bno', x_freq, w)
        y = jnp.real(jnp.fft.ifft(y_freq, axis=-1))
        return y + bias
    x = L0_attn_x
    x = x + _L0_attn_ref(_layernorm(x, axis=-1), L0_attn_Wq, L0_attn_Wk, L0_attn_Wv, L0_attn_Wbeta, L0_attn_Wo, L0_attn_g_norm)
    x = x + _L0_ffn_ref(_layernorm(x, axis=-1), L0_ffn_ln1_g, L0_ffn_ln1_b, L0_ffn_ln2_g, L0_ffn_ln2_b, L0_ffn_wq, L0_ffn_bq, L0_ffn_wk, L0_ffn_bk, L0_ffn_wv, L0_ffn_bv, L0_ffn_wo, L0_ffn_bo, L0_ffn_gate_w, L0_ffn_gate_b, L0_ffn_w1, L0_ffn_b1, L0_ffn_w2, L0_ffn_b2)
    x = x + _L1_attn_ref(_layernorm(x, axis=-1), L1_attn_w_qkv, L1_attn_w_out, L1_attn_b_out, L1_attn_ln_gamma, L1_attn_ln_beta)
    x = x + _L1_ffn_ref(_layernorm(x, axis=-1), L1_ffn_w_freq_real, L1_ffn_w_freq_imag, L1_ffn_bias)
    return x

_drawn_inputs = setup_inputs


def setup_inputs(seed=0):
    import zlib

    import numpy as np

    out = dict(_drawn_inputs(seed))
    spreads = {'L0_attn_g_norm': (1.0, 0.2),
     'L0_ffn_ln1_g': (1.0, 0.6),
     'L0_ffn_ln1_b': (0.0, 0.8),
     'L0_ffn_ln2_g': (1.0, 0.56),
     'L0_ffn_ln2_b': (0.0, 0.482),
     'L0_ffn_bq': (0.0, 0.8),
     'L0_ffn_bk': (0.0, 0.8),
     'L0_ffn_bv': (0.0, 0.294),
     'L0_ffn_bo': (0.0, 0.1),
     'L0_ffn_gate_b': (0.0, 0.1),
     'L0_ffn_b1': (0.0, 0.458),
     'L0_ffn_b2': (0.0, 0.1),
     'L1_attn_b_out': (0.0, 0.1),
     'L1_attn_ln_gamma': (1.0, 0.2),
     'L1_attn_ln_beta': (0.0, 0.1)}
    factors = {'L0_ffn_wq': 8.0, 'L0_ffn_wk': 8.0, 'L0_ffn_wv': 6.508, 'L1_ffn_bias': 8.0}
    for name, (base, spread) in spreads.items():
        noise = np.random.default_rng([zlib.crc32(name.encode()), seed]).standard_normal(out[name].shape)
        drawn = base * np.exp(spread * noise) if base else spread * noise
        out[name] = jnp.asarray(drawn.astype(out[name].dtype))
    for name, factor in factors.items():
        out[name] = (out[name] * factor).astype(out[name].dtype)
    return out
```

```python
from contextlib import ExitStack

import numpy as np
import concourse.bass as bass
from concourse import mybir

F32 = mybir.dt.float32
F16 = mybir.dt.float16
ALU = mybir.AluOpType
ACT = mybir.ActivationFunctionType
AX = mybir.AxisListType.X

P = 128
B, N, D = 8, 512, 128
NT = N // P
T = B * NT


def phase_semaphores(nc, ctx, tag):
    held = []

    def clear():
        nc.clear_and_free_semaphores(held)
        nc.all_engine_barrier()

    def new(name):
        held.append(nc.alloc_semaphore(name=name + tag))
        return held[-1]

    ctx.callback(clear)
    return new


def wait_ge(eng, sem, value, apart=None):
    eng.wait_ge(sem, value)
    if apart is not None:
        eng.sem_inc(apart, 1)


class Shared:
    pass


class Product:

    def __init__(self, sem, per, credit=0, unit=1):
        self.sem, self.per, self.credit, self.unit = sem, per, credit, unit

    def made(self, it, k):
        return (it * self.per + (k + 1 + self.credit)) * self.unit

    def made_before(self, it, k, ago=1):
        assert self.credit >= ago * self.per
        return (it * self.per + (k + 1 + self.credit - ago * self.per)) * self.unit


class Own:

    def __init__(self, eng, sem, per, it):
        self.eng, self.sem, self.per, self.it, self.n = eng, sem, per, it, 0

    def did(self, ins):
        ins.then_inc(self.sem, 1)
        self.n += 1

    def settle(self, apart=None):
        wait_ge(self.eng, self.sem, self.it * self.per + self.n, apart)

    def close(self):
        assert self.n == self.per, (self.n, self.per)


def bc(ap, n):
    return ap.unsqueeze(len(ap.shape)).broadcast_to([*ap.shape, n])


HA, DA = 4, 32
W_A = 3 * D + HA
LB = 16
GB = P // LB
RHS, Q_, K_, KT_, QT_, LT_ = 0, 2 * D, 3 * D, 4 * D, 5 * D, 6 * D
W_PACK = 6 * D + HA * P
LN_EPS = 1e-5
RMS_EPS = 1e-5


def setup(nc, g, ins):
    with ExitStack() as ctx:
        sem = phase_semaphores(nc, ctx, "_setup")
        filled, ident_ready, eye_built, mask_built, loaded = (
            sem("filled"), sem("ident_ready"), sem("eye_built"), sem("mask_built"), sem("loaded"))
        block = ctx.enter_context(nc.Block())

        @block.sync
        def _(sp):
            sp.dma_start(g.x[:, 0:T, :], ins["L0_attn_x"].rearrange("b (k p) d -> p (b k) d", p=P)).then_inc(loaded, 16)
            sp.wait_ge(loaded, 16)

        @block.gpsimd
        def _(pool):
            pool.memset(g.ident[:, :], 0.0).then_inc(filled, 1)
            pool.memset(g.head_mask[:, :], 1.0).then_inc(filled, 1)
            pool.memset(g.minus_half[:, :], -0.5).then_inc(filled, 1)
            pool.wait_ge(filled, 3)
            pool.affine_select(out=g.ident[:, :], in_=g.ident[:, :], compare_op=ALU.not_equal, fill=1.0,
                               base=0, pattern=[[-1, P]], channel_multiplier=1).then_inc(ident_ready, 1)
            pool.affine_select(out=g.head_mask[:, :], in_=g.head_mask[:, :], compare_op=ALU.is_ge, fill=0.0,
                               base=0, pattern=[[-DA, HA]], channel_multiplier=1).then_inc(mask_built, 1)
            pool.wait_ge(mask_built, 1)
            pool.affine_select(out=g.head_mask[:, :], in_=g.head_mask[:, :], compare_op=ALU.is_ge, fill=0.0,
                               base=DA - 1, pattern=[[DA, HA]], channel_multiplier=-1).then_inc(mask_built, 1)

        @block.vector
        def _(dve):
            dve.wait_ge(ident_ready, 1)
            for h in range(HA):
                last = dve.tensor_scalar(g.two_eye[:, h, :], g.ident[:, :], 2.0, None, ALU.mult)
            last.then_inc(eye_built, 1)
            dve.wait_ge(mask_built, 2)
            dve.tensor_scalar(g.fg_mask[:, 1, :, :], bc(g.head_mask[:, :], DA), 1.0, None, ALU.mult)
            dve.tensor_scalar(g.fg_mask[:, 0, :, :], bc(g.head_mask[:, :], DA), -1.0, None,
                              ALU.mult).then_inc(eye_built, 1)
            dve.wait_ge(eye_built, 2)



class TilePack:

    def __init__(self, pack, s, k):
        a = pack[:, s, k, :]
        by_head = lambda at: a[:, at:at + D].rearrange("p (h d) -> p h d", d=DA)
        self.rhs = a[:, RHS:RHS + 2 * D].rearrange("p (s h d) -> p s h d", s=2, d=DA)
        self.q, self.k = by_head(Q_), by_head(K_)
        self.kT, self.qT = a[:, KT_:KT_ + P], a[:, QT_:QT_ + P]
        self.lt = a[:, LT_:LT_ + HA * P].rearrange("p (h d) -> p h d", d=P)


def delta_front(nc, g, ins, scratch):
    with ExitStack() as ctx:
        sb = lambda name, shape: ctx.enter_context(nc.sbuf_tensor(name, shape, F32))
        sem = phase_semaphores(nc, ctx, "_a")
        ps = [[ctx.enter_context(nc.psum_tensor(f"fps{k}{j}", [P, 512], F32)) for j in range(2)] for k in range(NT)]
        w = sb("w_a", [P, W_A])
        xn = sb("xn_a", [P, NT, P])
        xnT = sb("xnT_a", [P, NT, P])
        squares = sb("squares", [P, NT, 2 * D])
        stats = sb("stats_a", [P, NT, 6])
        mv = sb("mv_a", [P, NT, 2])
        var_eps = sb("var_eps_a", [P, NT])
        rstd = sb("rstd_a", [P, NT])
        norm2 = sb("norm2", [P, NT, 2 * HA])
        inv_norm = sb("inv_norm", [P, NT, 2 * HA])
        beta = sb("beta", [P, NT, HA])
        bk_heads = sb("bk_heads", [P, NT, HA, P])
        pack = sb("pack_a", [P, 2, NT, W_PACK])

        own = sem("dve_own")
        w_loaded = sem("w_a_loaded")
        moments = Product(sem("moments"), 1)
        rstd_ready = Product(sem("rstd_ready"), 1)
        norm2_ready = Product(sem("norm2_ready"), 1)
        inv_norm_ready = Product(sem("inv_norm_ready"), 1)
        xn_ready = Product(sem("xn_ready"), NT)
        xnT_ps = Product(sem("xnT_ps"), NT, credit=NT)
        xnT_sb = Product(sem("xnT_sb"), NT)
        proj_ps = Product(sem("proj_ps"), NT)
        squared = Product(sem("squared"), NT)
        beta_exp = Product(sem("beta_exp"), NT)
        normed = Product(sem("normed"), NT)
        kqT_ps = Product(sem("kqT_ps"), NT)
        kT_sb = Product(sem("kT_sb"), NT)
        qT_sb = Product(sem("qT_sb"), NT)
        bk_ready = Product(sem("bk_ready"), NT)
        lt_ps = Product(sem("lt_ps"), NT)
        lt_sb = Product(sem("lt_sb"), NT, credit=NT)
        lt_masked = Product(sem("lt_masked"), 2 * NT)
        stored = [[sem(f"stored{s}{k}") for k in range(NT)] for s in range(2)]

        block = ctx.enter_context(nc.Block())

        @block.sync
        def _(sp):
            for n, name in enumerate(("L0_attn_Wq", "L0_attn_Wk", "L0_attn_Wv", "L0_attn_Wbeta")):
                sp.dma_start(w[:, n * D:n * D + ins[name].shape[1]], ins[name]).then_inc(w_loaded, 16)
            for s in range(2):
                for k in range(NT):
                    sp.sem_inc(stored[s][k], 16)
            with sp.Fori(0, B // 2) as pair:
                for s in range(2):
                    b = pair * 2 + s
                    for k in range(NT):
                        wait_ge(sp, lt_masked.sem, lt_masked.made(b, NT + k), g.passed)
                        sp.wait_ge(qT_sb.sem, qT_sb.made(b, k))
                        sp.dma_start(scratch.packs[b * NT + k], pack[:, s, k, :]).then_inc(stored[s][k], 16)
            for s in range(2):
                for k in range(NT):
                    sp.wait_ge(stored[s][k], 16 * (B // 2 + 1))

        @block.vector
        def _(dve):
            with dve.Fori(0, B // 2) as pair:
                for s in range(2):
                    b = pair * 2 + s
                    tiles = [TilePack(pack, s, k) for k in range(NT)]
                    me = Own(dve, own, 3 * NT + 2, b)
                    for k in range(NT):
                        me.did(dve.bn_stats(stats[:, k, :], g.x[:, b * NT + k, :]))
                    me.settle(g.passed)
                    for k in range(NT):
                        me.did(dve.bn_aggr(mv[:, k, :], stats[:, k, :]))
                    me.settle()
                    dve.tensor_scalar(var_eps[:, :], mv[:, :, 1], LN_EPS, None, ALU.add).then_inc(moments.sem, 1)
                    dve.wait_ge(rstd_ready.sem, rstd_ready.made(b, 0))
                    for k in range(NT):
                        dve.wait_ge(xnT_ps.sem, xnT_ps.made_before(b, k))
                        dve.tensor_scalar(xn[:, k, :], g.x[:, b * NT + k, :], mv[:, k, 0:1], rstd[:, k:k + 1],
                                          ALU.subtract, ALU.mult).then_inc(xn_ready.sem, 1)
                    dve.wait_ge(beta_exp.sem, beta_exp.made(b, NT - 1))
                    me.did(dve.tensor_scalar(beta[:, :, :], beta[:, :, :], 1.0, None, ALU.add))
                    dve.wait_ge(squared.sem, squared.made(b, NT - 1))
                    dve.tensor_reduce(norm2[:, :, :], squares[:, :, :].rearrange("p k (h d) -> p (k h) d", d=DA),
                                      AX, ALU.add).then_inc(norm2_ready.sem, 1)
                    me.settle()
                    me.did(dve.reciprocal(beta[:, :, :], beta[:, :, :]))
                    me.settle()
                    dve.wait_ge(inv_norm_ready.sem, inv_norm_ready.made(b, 0))
                    for k in range(NT):
                        qkv = ps[k][1][:, 0:3 * D].rearrange("p (h d) -> p h d", d=DA)
                        dve.wait_ge(stored[s][k], 16 * pair + 16)
                        dve.tensor_tensor(tiles[k].q, qkv[:, 0:HA, :], bc(inv_norm[:, k, 0:HA], DA), ALU.mult)
                        dve.tensor_tensor(tiles[k].rhs[:, 0, :, :], qkv[:, 2 * HA:, :], bc(beta[:, k, :], DA), ALU.mult)
                        me.did(dve.tensor_tensor(tiles[k].k, qkv[:, HA:2 * HA, :], bc(inv_norm[:, k, HA:], DA), ALU.mult))
                    me.settle()
                    for k in range(NT):
                        dve.tensor_tensor(tiles[k].rhs[:, 1, :, :], tiles[k].k, bc(beta[:, k, :], DA),
                                          ALU.mult).then_inc(normed.sem, 1)
                    for k in range(NT):
                        dve.wait_ge(kqT_ps.sem, kqT_ps.made(b, k))
                        dve.tensor_tensor(bk_heads[:, k, :, :], ps[k][0][:, 2 * P:3 * P].unsqueeze(1).broadcast_to([P, HA, P]),
                                          bc(g.head_mask[:, :], P), ALU.mult).then_inc(bk_ready.sem, 1)
                    me.close()

        @block.scalar
        def _(act):
            act.sem_inc(lt_sb.sem, NT)
            with act.Fori(0, B // 2) as pair:
                for s in range(2):
                    b = pair * 2 + s
                    for k in range(NT):
                        act.wait_ge(xnT_ps.sem, xnT_ps.made(b, k))
                        act.copy(xnT[:, k, :], ps[k][0][:, 0:P]).then_inc(xnT_sb.sem, 1)
                    for k in range(NT):
                        act.wait_ge(proj_ps.sem, proj_ps.made(b, k))
                        act.activation(beta[:, k, :], ps[k][1][:, 3 * D:W_A], ACT.Exp, scale=-1.0).then_inc(beta_exp.sem, 1)
                        act.activation(squares[:, k, :], ps[k][1][:, 0:2 * D], ACT.Square).then_inc(squared.sem, 1)
                    for k in range(NT):
                        tile = TilePack(pack, s, k)
                        act.wait_ge(bk_ready.sem, bk_ready.made(b, k))
                        act.copy(tile.kT, ps[k][0][:, P:2 * P]).then_inc(kT_sb.sem, 1)
                        act.copy(tile.qT, ps[k][0][:, 0:P]).then_inc(qT_sb.sem, 1)
                    for k in range(NT):
                        act.wait_ge(lt_ps.sem, lt_ps.made(b, k))
                        act.copy(TilePack(pack, s, k).lt, ps[k][1][:, :].rearrange("p (h i) -> p h i", h=HA)).then_inc(lt_sb.sem, 1)

        @block.gpsimd
        def _(pool):
            with pool.Fori(0, B // 2) as pair:
                for s in range(2):
                    b = pair * 2 + s
                    pool.wait_ge(moments.sem, moments.made(b, 0))
                    pool.tensor_tensor(rstd[:, :], var_eps[:, :], g.minus_half[:, 0:NT], ALU.pow).then_inc(rstd_ready.sem, 1)
                    pool.wait_ge(norm2_ready.sem, norm2_ready.made(b, 0))
                    pool.tensor_tensor(inv_norm[:, :, :], norm2[:, :, :], g.minus_half[:, 0:NT * 2 * HA].rearrange("p (k h) -> p k h", k=NT),
                                       ALU.pow).then_inc(inv_norm_ready.sem, 1)
                    for k in range(NT):
                        lt = TilePack(pack, s, k).lt
                        wait_ge(pool, lt_sb.sem, lt_sb.made(b, k), g.passed)
                        pool.affine_select(out=lt, in_=lt, compare_op=ALU.is_gt, fill=0.0, base=0,
                                           pattern=[[0, HA], [1, P]], channel_multiplier=-1).then_inc(lt_masked.sem, 1)
                    for k in range(NT):
                        lt = TilePack(pack, s, k).lt
                        wait_ge(pool, lt_masked.sem, lt_masked.made(b, k), g.passed)
                        pool.affine_select(out=lt, in_=lt, compare_op=ALU.not_equal, fill=1.0, base=0,
                                           pattern=[[0, HA], [1, P]], channel_multiplier=-1).then_inc(lt_masked.sem, 1)

        @block.tensor
        def _(pe):
            pe.sem_inc(xnT_ps.sem, NT)
            pe.wait_ge(w_loaded, 64)
            with pe.Fori(0, B // 2) as pair:
                for s in range(2):
                    b = pair * 2 + s
                    for k in range(NT):
                        pe.wait_ge(xn_ready.sem, xn_ready.made(b, k))
                        pe.transpose(ps[k][0][:, 0:P], xn[:, k, :], g.ident[:, :]).then_inc(xnT_ps.sem, 1)
                    for k in range(NT):
                        pe.wait_ge(xnT_sb.sem, xnT_sb.made(b, k))
                        pe.wait_ge(lt_sb.sem, lt_sb.made_before(b, k))
                        pe.matmul(ps[k][1][:, 0:W_A], xnT[:, k, :], w[:, :], start=True, stop=True).then_inc(proj_ps.sem, 1)
                    for k in range(NT):
                        tile = TilePack(pack, s, k)
                        pe.wait_ge(normed.sem, normed.made(b, k))
                        pe.transpose(ps[k][0][:, 0:P], tile.q, g.ident[:, :])
                        pe.transpose(ps[k][0][:, P:2 * P], tile.k, g.ident[:, :])
                        pe.transpose(ps[k][0][:, 2 * P:3 * P], tile.rhs[:, 1, :, :], g.ident[:, :]).then_inc(kqT_ps.sem, 1)
                    for k in range(NT):
                        pe.wait_ge(kT_sb.sem, kT_sb.made(b, k))
                        pe.matmul(ps[k][1][:, :], TilePack(pack, s, k).kT, bk_heads[:, k, :, :], start=True,
                                  stop=True).then_inc(lt_ps.sem, 1)


def delta_invert(nc, g, scratch):
    n_blocks = T * HA * GB // P
    assert T * HA == P and n_blocks == GB
    with ExitStack() as ctx:
        sb = lambda name, shape: ctx.enter_context(nc.sbuf_tensor(name, shape, F32))
        sem = phase_semaphores(nc, ctx, "_inv")
        ltb = sb("lt_blocks", [P, GB, LB, LB])
        inv = sb("inv_blocks", [P, GB, LB, LB])
        terms = sb("terms", [P, GB, LB, LB])
        loaded, own, stored, zeroed, eye = (
            sem("blocks_loaded"), sem("dve_own"), sem("blocks_stored"), sem("inv_zeroed"), sem("inv_eye"))
        block = ctx.enter_context(nc.Block())

        @block.sync
        def _(sp):
            per_block = scratch.packs[:, :, LT_:].rearrange("t (g j) (h q) -> g t h j q", g=GB, h=HA)
            for n in range(GB):
                for h in range(HA):
                    sp.dma_start(ltb[h::HA, n, :, :], per_block[n, :, h, :, n * LB:(n + 1) * LB]).then_inc(loaded, 16)
            sp.wait_ge(own, 2 * (LB - 1))
            sp.dma_start(scratch.inv, inv[:, :, :, :]).then_inc(stored, 16)
            sp.wait_ge(stored, 16)

        @block.gpsimd
        def _(pool):
            pool.memset(inv[:, :, :, :], 0.0).then_inc(zeroed, 1)

        @block.vector
        def _(dve):
            dve.wait_ge(zeroed, 1)
            dve.memset(inv[:, :, :, :].rearrange("p g i c -> p g (i c)")[:, :, 0::LB + 1], 1.0).then_inc(eye, 1)
            dve.wait_ge(eye, 1)
            dve.wait_ge(loaded, 16 * 4 * GB)
            for i in range(1, LB):
                for_j = bc(ltb[:, :, 0:i, i], i).rearrange("p g j c -> p g c j")
                dve.tensor_tensor(terms[:, :, 0:i, 0:i], for_j, inv[:, :, 0:i, 0:i].rearrange("p g j c -> p g c j"),
                                  ALU.mult).then_inc(own, 1)
                dve.wait_ge(own, 2 * i - 1)
                dve.tensor_reduce(inv[:, :, i, 0:i], terms[:, :, 0:i, 0:i], AX, ALU.add, negate=True).then_inc(own, 1)
                dve.wait_ge(own, 2 * i)


def delta_back(nc, g, ins, scratch):
    with ExitStack() as ctx:
        sb = lambda name, shape: ctx.enter_context(nc.sbuf_tensor(name, shape, F32))
        sem = phase_semaphores(nc, ctx, "_b")
        ps = [[ctx.enter_context(nc.psum_tensor(f"bps{k}{j}", [P, 512], F32)) for j in range(2)] for k in range(NT)]
        by_head = lambda bank: bank[:, :].rearrange("p (h i) -> p h i", h=HA)
        pack = sb("pack_b", [P, 2, NT, W_PACK])
        inv = sb("inv_b", [P, 2, NT, HA, P])
        invT = sb("invT_b", [P, NT, HA, P])
        resid = sb("newton_residual", [P, NT, HA, P])
        grown = sb("grown_b", [P, NT, HA, P])
        grownT = sb("grownT_b", [P, NT, HA, P])
        q_heads = sb("q_heads", [P, NT, HA, P])
        y0 = sb("y0", [P, NT, 2, HA, DA])
        err = sb("err", [P, NT, 2, HA, DA])
        uw = sb("uw", [P, NT, 2, HA, DA])
        within = sb("within", [P, NT, HA, DA])
        qt = sb("q_tilde", [P, NT, HA, DA])
        qtT = sb("q_tildeT", [P, NT, P])
        fg = sb("fg", [P, NT, 2, P])
        state = sb("state", [P, NT, P])
        o = sb("o_a", [P, NT, HA, DA])
        o2 = sb("o2_a", [P, NT, HA, DA])
        ms = sb("ms_a", [P, NT, HA])
        inv_rms = sb("inv_rms", [P, NT, HA])
        oT = sb("oT_a", [P, NT, P])
        wo = sb("wo_a", [P, P])
        g_col = sb("g_col", [P, 1])

        w_loaded, own, cleared, wo_ready = sem("wo_a_loaded"), sem("dve_own"), sem("inv_cleared"), sem("wo_a_ready")
        pack_in = [[sem(f"pack_in{s}{k}") for k in range(NT)] for s in range(2)]
        inv_in = [sem(f"inv_in{s}") for s in range(2)]
        made = lambda name, per=NT, credit=0: Product(sem(name), per, credit)
        q_heads_ready = made("q_heads_ready")
        qk_ps, qk_sb, qk_masked = made("qk_ps"), made("qk_sb"), made("qk_masked")
        invT_ready = made("invT_ready")
        lt0_ps, r0_ready = made("lt0_ps"), made("r0_ready")
        t1_ps, t1_sb = made("t1_ps"), made("t1_sb")
        t1T_ps, t1T_sb = made("t1T_ps"), made("t1T_sb")
        lt1_ps, r1_ready = made("lt1_ps"), made("r1_ready")
        t2T_ps, t2T_sb = made("t2T_ps"), made("t2T_sb")
        y0_ps, y0_sb = made("y0_ps"), made("y0_sb")
        ly_ps, err_ready = made("ly_ps"), made("err_ready")
        dy_ps, uw_ready = made("dy_ps"), made("uw_ready")
        muw_ps, qt_ready = made("muw_ps"), made("qt_ready")
        fg_ps, fg_masked = made("fg_ps"), made("fg_masked")
        qtT_ps, qtT_sb = made("qtT_ps"), made("qtT_sb")
        f_ready = made("f_ready")
        state_ps, state_ready = made("state_ps", NT - 2), made("state_ready", NT - 1)
        cross_ps, o_ready = made("cross_ps", NT - 1), made("o_ready")
        o2_ready, ms_ready, inv_rms_ready, on_ready = made("o2_ready"), made("ms_ready", 1), made("inv_rms_ready", 1), made("on_ready")
        oT_ps, oT_sb = made("oT_ps"), made("oT_sb")
        out_ps = made("out_ps", credit=2 * NT)
        added = made("added", credit=NT)

        block = ctx.enter_context(nc.Block())

        @block.sync
        def _(sp):
            sp.dma_start(wo[:, :], ins["L0_attn_Wo"]).then_inc(w_loaded, 16)
            for h in range(HA):
                sp.dma_start(g_col[h * DA:(h + 1) * DA, :], ins["L0_attn_g_norm"].rearrange("(d a) -> d a", a=1)).then_inc(w_loaded, 16)
            sp.wait_ge(cleared, 2)
            blocks = scratch.inv.rearrange("(t h) g i c -> g i t h c", h=HA)
            with sp.Fori(0, B // 2) as pair:
                for s in range(2):
                    b = pair * 2 + s
                    for k in range(NT):
                        sp.wait_ge(out_ps.sem, out_ps.made_before(b, k, 2))
                        sp.dma_start(pack[:, s, k, :], scratch.packs[b * NT + k]).then_inc(pack_in[s][k], 16)
                    for n in range(GB):
                        for h in range(HA):
                            sp.dma_start(inv[n * LB:(n + 1) * LB, s, :, h, n * LB:(n + 1) * LB],
                                         blocks[n, :, bass.ds(b * NT, NT), h, :]).then_inc(inv_in[s], 16)

        @block.gpsimd
        def _(pool):
            for s in range(2):
                pool.memset(inv[:, s, :, :, :], 0.0).then_inc(cleared, 1)
            pool.wait_ge(w_loaded, 16 * (1 + HA))
            pool.tensor_scalar(wo[:, :], wo[:, :], g_col[:, 0:1], None, ALU.mult).then_inc(wo_ready, 1)
            with pool.Fori(0, B // 2) as pair:
                for s in range(2):
                    b = pair * 2 + s
                    tiles = [TilePack(pack, s, k) for k in range(NT)]
                    for k in range(NT):
                        pool.wait_ge(pack_in[s][k], 16 * pair + 16)
                        pool.tensor_tensor(q_heads[:, k, :, :], tiles[k].qT.unsqueeze(1).broadcast_to([P, HA, P]),
                                           bc(g.head_mask[:, :], P), ALU.mult).then_inc(q_heads_ready.sem, 1)
                    for k in range(NT):
                        wait_ge(pool, qk_sb.sem, qk_sb.made(b, k), g.passed)
                        pool.affine_select(out=resid[:, k, :, :], in_=resid[:, k, :, :], compare_op=ALU.is_ge, fill=0.0,
                                           base=0, pattern=[[0, HA], [1, P]], channel_multiplier=-1).then_inc(qk_masked.sem, 1)
                    for k in range(NT):
                        pool.wait_ge(fg_masked.sem, fg_masked.made(b, k))
                        pool.tensor_tensor(fg[:, k, 0, :], fg[:, k, 0, :], g.ident[:, :], ALU.add).then_inc(f_ready.sem, 1)
                    for k in range(NT):
                        pool.wait_ge(o_ready.sem, o_ready.made(b, k))
                        pool.tensor_tensor(o2[:, k, :, :], o[:, k, :, :], o[:, k, :, :], ALU.mult).then_inc(o2_ready.sem, 1)
                    pool.wait_ge(ms_ready.sem, ms_ready.made(b, 0))
                    pool.tensor_tensor(inv_rms[:, :, :], ms[:, :, :], g.minus_half[:, 0:NT * HA].rearrange("p (k h) -> p k h", k=NT),
                                       ALU.pow).then_inc(inv_rms_ready.sem, 1)

        @block.vector
        def _(dve):
            dve.sem_inc(added.sem, NT)
            with dve.Fori(0, B // 2) as pair:
                for s in range(2):
                    b = pair * 2 + s
                    tiles = [TilePack(pack, s, k) for k in range(NT)]
                    me = Own(dve, own, 1, b)
                    dve.wait_ge(inv_in[s], (16 * GB * HA) * pair + 16 * GB * HA)
                    for k in range(NT):
                        dve.transpose(invT[:, k, :, :], inv[:, s, k, :, :]).then_inc(invT_ready.sem, 1)
                    for k in range(NT):
                        dve.wait_ge(lt0_ps.sem, lt0_ps.made(b, k))
                        dve.scalar_tensor_tensor(out=resid[:, k, :, :], in0=by_head(ps[k][0]), scalar=-1.0,
                                                 in1=g.two_eye[:, :, :], op0=ALU.mult, op1=ALU.add).then_inc(r0_ready.sem, 1)
                    for k in range(NT):
                        dve.wait_ge(lt1_ps.sem, lt1_ps.made(b, k))
                        dve.scalar_tensor_tensor(out=resid[:, k, :, :], in0=by_head(ps[k][1]), scalar=-1.0,
                                                 in1=g.two_eye[:, :, :], op0=ALU.mult, op1=ALU.add).then_inc(r1_ready.sem, 1)
                    half = lambda bank: bank[:, 0:2 * D].rearrange("p (s h d) -> p s h d", s=2, d=DA)
                    for k in range(NT):
                        dve.wait_ge(ly_ps.sem, ly_ps.made(b, k))
                        dve.tensor_tensor(err[:, k, :, :, :], tiles[k].rhs, half(ps[k][0]), ALU.subtract).then_inc(err_ready.sem, 1)
                    for k in range(NT):
                        dve.wait_ge(dy_ps.sem, dy_ps.made(b, k))
                        dve.wait_ge(y0_sb.sem, y0_sb.made(b, k))
                        dve.tensor_tensor(uw[:, k, :, :, :], half(ps[k][1]), y0[:, k, :, :, :], ALU.add).then_inc(uw_ready.sem, 1)
                    for k in range(NT):
                        dve.wait_ge(fg_ps.sem, fg_ps.made(b, k))
                        dve.tensor_tensor(fg[:, k, :, :], ps[k][1][:, 0:2 * P].rearrange("p (s c) -> p s c", s=2),
                                          g.fg_mask[:, :, :, :].rearrange("p s h d -> p s (h d)"), ALU.mult).then_inc(fg_masked.sem, 1)
                    for k in range(NT):
                        dve.wait_ge(muw_ps.sem, muw_ps.made(b, k))
                        dve.tensor_copy(within[:, k, :, :], half(ps[k][0])[:, 0, :, :])
                        dve.tensor_tensor(qt[:, k, :, :], tiles[k].q, half(ps[k][0])[:, 1, :, :], ALU.subtract).then_inc(qt_ready.sem, 1)
                    dve.wait_ge(fg_masked.sem, fg_masked.made(b, NT - 1))
                    dve.wait_ge(qt_ready.sem, qt_ready.made(b, NT - 1))
                    dve.tensor_copy(state[:, 1, :], fg[:, 0, 1, :]).then_inc(state_ready.sem, 1)
                    dve.tensor_copy(o[:, 0, :, :], within[:, 0, :, :]).then_inc(o_ready.sem, 1)
                    for k in range(1, NT):
                        if k < NT - 1:
                            dve.wait_ge(state_ps.sem, state_ps.made(b, k - 1))
                            dve.tensor_tensor(state[:, k + 1, :], ps[k][1][:, 0:P], fg[:, k, 1, :], ALU.add).then_inc(state_ready.sem, 1)
                        dve.wait_ge(cross_ps.sem, cross_ps.made(b, k - 1))
                        dve.tensor_tensor(o[:, k, :, :], ps[k][0][:, 0:P].rearrange("p (h d) -> p h d", d=DA), within[:, k, :, :],
                                          ALU.add).then_inc(o_ready.sem, 1)
                    dve.wait_ge(o2_ready.sem, o2_ready.made(b, NT - 1))
                    me.did(dve.tensor_reduce(ms[:, :, :], o2[:, :, :, :], AX, ALU.add))
                    me.settle()
                    dve.tensor_scalar(ms[:, :, :], ms[:, :, :], 1.0 / DA, RMS_EPS, ALU.mult, ALU.add).then_inc(ms_ready.sem, 1)
                    dve.wait_ge(inv_rms_ready.sem, inv_rms_ready.made(b, 0))
                    for k in range(NT):
                        dve.tensor_tensor(o[:, k, :, :], o[:, k, :, :], bc(inv_rms[:, k, :], DA), ALU.mult).then_inc(on_ready.sem, 1)
                    for k in range(NT):
                        dve.wait_ge(out_ps.sem, out_ps.made(b, k))
                        dve.tensor_tensor(g.x[:, b * NT + k, :], g.x[:, b * NT + k, :], ps[k][0][:, 0:P], ALU.add).then_inc(added.sem, 1)
                    me.close()

        @block.scalar
        def _(act):
            with act.Fori(0, B // 2) as pair:
                for s in range(2):
                    b = pair * 2 + s

                    def evacuate(source, bank_of, target, ready):
                        for k in range(NT):
                            act.wait_ge(source.sem, source.made(b, k))
                            act.copy(target(k), bank_of(k)).then_inc(ready.sem, 1)

                    evacuate(t1_ps, lambda k: by_head(ps[k][1]), lambda k: grown[:, k, :, :], t1_sb)
                    evacuate(t1T_ps, lambda k: by_head(ps[k][0]), lambda k: grownT[:, k, :, :], t1T_sb)
                    evacuate(t2T_ps, lambda k: by_head(ps[k][0]), lambda k: invT[:, k, :, :], t2T_sb)
                    evacuate(y0_ps, lambda k: ps[k][1][:, 0:2 * D].rearrange("p (s h d) -> p s h d", s=2, d=DA),
                             lambda k: y0[:, k, :, :, :], y0_sb)
                    evacuate(qk_ps, lambda k: by_head(ps[k][1]), lambda k: resid[:, k, :, :], qk_sb)
                    evacuate(qtT_ps, lambda k: ps[k][0][:, 0:P], lambda k: qtT[:, k, :], qtT_sb)
                    evacuate(oT_ps, lambda k: ps[k][1][:, 0:P], lambda k: oT[:, k, :], oT_sb)

        @block.tensor
        def _(pe):
            pe.sem_inc(out_ps.sem, 2 * NT)
            pe.wait_ge(wo_ready, 1)
            with pe.Fori(0, B // 2) as pair:
                for s in range(2):
                    b = pair * 2 + s
                    tiles = [TilePack(pack, s, k) for k in range(NT)]

                    def heads(bank, k, lhsT, rhs, ready):
                        for h in range(HA):
                            last = pe.matmul(bank(h), lhsT(h), rhs(h), start=True, stop=True)
                        last.then_inc(ready.sem, 1)

                    full = lambda k, j: lambda h: by_head(ps[k][j])[:, h, :]
                    pair_of = lambda k, j: lambda h: ps[k][j][:, 0:2 * D].rearrange("p (s h d) -> p s h d", s=2, d=DA)[:, :, h, :]
                    for k in range(NT):
                        pe.wait_ge(pack_in[s][k], 16 * pair + 16)
                        if k == 0:
                            pe.wait_ge(inv_in[s], (16 * GB * HA) * pair + 16 * GB * HA)
                        pe.wait_ge(added.sem, added.made_before(b, k))
                        heads(full(k, 0), k, lambda h: tiles[k].lt[:, h, :], lambda h: inv[:, s, k, h, :], lt0_ps)
                    for k in range(NT):
                        pe.wait_ge(invT_ready.sem, invT_ready.made(b, k))
                        pe.wait_ge(r0_ready.sem, r0_ready.made(b, k))
                        heads(full(k, 1), k, lambda h: invT[:, k, h, :], lambda h: resid[:, k, h, :], t1_ps)
                    for k in range(NT):
                        heads(full(k, 0), k, lambda h: resid[:, k, h, :], lambda h: invT[:, k, h, :], t1T_ps)
                    for k in range(NT):
                        pe.wait_ge(t1_sb.sem, t1_sb.made(b, k))
                        heads(full(k, 1), k, lambda h: tiles[k].lt[:, h, :], lambda h: grown[:, k, h, :], lt1_ps)
                    for k in range(NT):
                        pe.wait_ge(t1T_sb.sem, t1T_sb.made(b, k))
                        pe.wait_ge(r1_ready.sem, r1_ready.made(b, k))
                        heads(full(k, 0), k, lambda h: resid[:, k, h, :], lambda h: grownT[:, k, h, :], t2T_ps)
                    for k in range(NT):
                        pe.wait_ge(t2T_sb.sem, t2T_sb.made(b, k))
                        heads(pair_of(k, 1), k, lambda h: invT[:, k, h, :], lambda h: tiles[k].rhs[:, :, h, :], y0_ps)
                    for k in range(NT):
                        pe.wait_ge(y0_sb.sem, y0_sb.made(b, k))
                        heads(pair_of(k, 0), k, lambda h: tiles[k].lt[:, h, :], lambda h: y0[:, k, :, h, :], ly_ps)
                    for k in range(NT):
                        pe.wait_ge(q_heads_ready.sem, q_heads_ready.made(b, k))
                        pe.matmul(ps[k][1][:, :], tiles[k].kT, q_heads[:, k, :, :], start=True, stop=True).then_inc(qk_ps.sem, 1)
                    for k in range(NT):
                        pe.wait_ge(err_ready.sem, err_ready.made(b, k))
                        pe.wait_ge(qk_sb.sem, qk_sb.made(b, k))
                        heads(pair_of(k, 1), k, lambda h: invT[:, k, h, :], lambda h: err[:, k, :, h, :], dy_ps)
                    for k in range(NT):
                        pe.wait_ge(uw_ready.sem, uw_ready.made(b, k))
                        pe.wait_ge(qk_masked.sem, qk_masked.made(b, k))
                        heads(pair_of(k, 0), k, lambda h: resid[:, k, h, :], lambda h: uw[:, k, :, h, :], muw_ps)
                    for k in range(NT):
                        pe.matmul(ps[k][1][:, 0:P], uw[:, k, 1, :, :], tiles[k].k, start=True, stop=True)
                        pe.matmul(ps[k][1][:, P:2 * P], tiles[k].k, uw[:, k, 0, :, :], start=True, stop=True).then_inc(fg_ps.sem, 1)
                    for k in range(NT):
                        pe.wait_ge(qt_ready.sem, qt_ready.made(b, k))
                        pe.transpose(ps[k][0][:, 0:P], qt[:, k, :, :], g.ident[:, :]).then_inc(qtT_ps.sem, 1)
                    for k in range(1, NT):
                        pe.wait_ge(state_ready.sem, state_ready.made(b, k - 1))
                        if k < NT - 1:
                            pe.wait_ge(f_ready.sem, f_ready.made(b, k))
                            pe.matmul(ps[k][1][:, 0:P], fg[:, k, 0, :], state[:, k, :], start=True, stop=True).then_inc(state_ps.sem, 1)
                        pe.wait_ge(qtT_sb.sem, qtT_sb.made(b, k))
                        pe.matmul(ps[k][0][:, 0:P], qtT[:, k, :], state[:, k, :], start=True, stop=True).then_inc(cross_ps.sem, 1)
                    for k in range(NT):
                        pe.wait_ge(on_ready.sem, on_ready.made(b, k))
                        pe.transpose(ps[k][1][:, 0:P], o[:, k, :, :], g.ident[:, :]).then_inc(oT_ps.sem, 1)
                    for k in range(NT):
                        pe.wait_ge(oT_sb.sem, oT_sb.made(b, k))
                        pe.matmul(ps[k][0][:, 0:P], oT[:, k, :], wo[:, :], start=True, stop=True).then_inc(out_ps.sem, 1)


class Attention:

    def __init__(self, name, heads, width, pairs):
        self.name, self.heads, self.width, self.pairs = name, heads, width, pairs
        self.parts = 1 + max(max(p) for p in pairs)
        self.groups = heads // HG
        self.total = B * self.groups
        self.scale = float(width) ** -0.5
        assert len(pairs) * width <= SHIFT_ROW and HG * HEAD_ROWS == P and width <= HEAD_ROWS


HG = 4
HEAD_ROWS = P // HG
SHIFT_ROW = 96
RING = 4
EXP_LAG, PV_LAG, OUT_LAG = 2, 3, 4
TILES = HG * NT
L0_ATT = Attention("l0", 16, 8, ((0, 0), (0, 1), (0, 2), (1, 0), (1, 1), (2, 0)))
L1_ATT = Attention("l1", 32, 32, ((0, 0), (0, 1), (1, 0)))


def attention(nc, g, a, scratch, w_out, out, addend):
    W, M, U = a.width, a.total, a.groups
    with ExitStack() as ctx:
        sb = lambda name, shape, dt=F32: ctx.enter_context(nc.sbuf_tensor(f"{name}_{a.name}", shape, dt))
        sem = phase_semaphores(nc, ctx, "_" + a.name)
        pb = lambda name: ctx.enter_context(nc.psum_tensor(f"{name}_{a.name}", [P, N], F32))
        max_ps, exp_ps = [pb(f"max{i}") for i in range(2)], [pb(f"exp{i}") for i in range(3)]
        pv_bank, sums_bank, y_bank = pb("pv_bank"), pb("sums_bank"), pb("y_bank")
        qs, ks = sb("q_stack", [P, RING, HG, N], F16), sb("k_stack", [P, RING, HG, N], F16)
        vs = sb("v_ring", [P, RING, NT, HG, W])
        probs = sb("probs", [P, 2, HG, NT, N])
        part_sums = sb("part_sums", [P, 2, HG, 2, N])
        ones = sb("ones", [P, HEAD_ROWS])
        maxima = sb("maxima", [P, 2, NT, HG])
        shift = sb("shift", [HG, 2, N], F16)
        sums, oT_raw, oT = sb("sums", [P, N]), sb("oT_raw", [P, N]), sb("oT", [P, 2, N])
        inv_sums, inv_rows = sb("inv_sums", [P, NT, HG]), sb("inv_rows", [P, NT, HG, HEAD_ROWS])

        cleared, shift_rows = sem("cleared"), sem("shift_rows")
        loaded = [sem(f"loaded{s}") for s in range(RING)]
        v_loaded = [sem(f"v_loaded{s}") for s in range(RING)]
        shifted = [sem(f"shifted{s}") for s in range(RING)]
        n_loads = 2 * len(a.pairs)
        made = lambda name, per=1: Product(sem(name), per)
        max_tile = made("max_tile", TILES)
        max_taken = made("max_taken", TILES)
        maxT_ps, shift_ready = made("maxT_ps"), made("shift_ready")
        score_tile = made("score_tile", TILES)
        prob_tile = made("prob_tile", TILES)
        pair_sum, key_sum, key_sum2 = made("pair_sum", HG), made("key_sum", HG // 2), made("key_sum2", HG // 2)
        sums_ps, sums_sb, sumsT_ps, inv_ready, inv_rows_ready, inv_ps, pv_sb, pv_ps, oT_ready, y_ps, y_taken = (
            made("sums_ps"), made("sums_sb"), made("sumsT_ps"), made("inv_ready"), made("inv_rows_ready"), made("inv_ps"), made("pv_sb"), made("pv_ps"), made("oT_ready"), made("y_ps"), made("y_taken"))

        def exists(turn, s, lag):
            return not isinstance(turn, int) or 0 <= turn * U + s - lag < M

        def stream(eng, step):
            for s in range(U):
                step(0, s)
            with eng.Fori(1, B) as turn:
                for s in range(U):
                    step(turn, s)
            for s in range(OUT_LAG):
                step(B, s)

        def nth(turn, s, unit):
            return (turn * (U // RING) + s // RING + 1) * unit

        def exp_bank(s, at):
            return (at + s % 2) % 3

        block = ctx.enter_context(nc.Block())

        @block.sync
        def _(sp):
            sp.wait_ge(cleared, 3)

            def load(turn, s):
                slot = s % RING
                if exists(turn, s, RING):
                    wait_ge(sp, score_tile.sem, score_tile.made(turn * U + s - RING, TILES - 1), g.passed)
                for r, parts in enumerate(a.pairs):
                    for side, stack in enumerate((qs, ks)):
                        sp.dma_start(stack[r * W:(r + 1) * W, slot, :, :],
                                     scratch.qk[side, parts[side], turn * U + s].rearrange("h d t -> d h t")).then_inc(loaded[slot], 16)

            def step(turn, s, more=True):
                if more:
                    load(turn, s + 1)
                if exists(turn, s, 0):
                    if exists(turn, s, RING):
                        wait_ge(sp, pv_ps.sem, pv_ps.made(turn * U + s - RING, 0), g.passed)
                    sp.dma_start(vs[:, s % RING, :, :, :], scratch.v[turn * U + s]).then_inc(v_loaded[s % RING], 16)
                if exists(turn, s, 1):
                    wait_ge(sp, shift_ready.sem, shift_ready.made(turn * U + s - 1, 0), g.passed)
                    sp.dma_start(qs[SHIFT_ROW:SHIFT_ROW + HG, (s - 1) % RING, :, :],
                                 shift[:, (s - 1) % 2, :].unsqueeze(1).broadcast_to([HG, HG, N])).then_inc(shifted[(s - 1) % RING], 16)

            load(0, 0)
            for s in range(U):
                step(0, s)
            with sp.Fori(1, B - 1) as turn:
                for s in range(U):
                    step(turn, s)
            for s in range(U):
                step(B - 1, s, s + 1 < U)
            step(B, 0, False)

        @block.gpsimd
        def _(pool):
            pool.memset(qs[:, :, :, :], 0.0).then_inc(shift_rows, 1)
            pool.wait_ge(shift_rows, 1)
            rows = ks[SHIFT_ROW:SHIFT_ROW + HG, :, :, :]
            pool.memset(rows, 0.0).then_inc(shift_rows, 1)
            pool.wait_ge(shift_rows, 2)
            pool.affine_select(out=rows, in_=rows, compare_op=ALU.not_equal, fill=1.0, base=0,
                               pattern=[[0, RING], [-1, HG], [0, N]], channel_multiplier=1).then_inc(cleared, 1)

            def step(turn, s):
                if not exists(turn, s, EXP_LAG):
                    return
                m, i = turn * U + s - EXP_LAG, (s - EXP_LAG) % 2
                for h in range(HG):
                    pool.wait_ge(prob_tile.sem, prob_tile.made(m, h * NT + NT - 1))
                    pool.tensor_tensor(part_sums[:, i, h, :, :], probs[:, i, h, 0:2, :], probs[:, i, h, 2:4, :], ALU.add).then_inc(pair_sum.sem, 1)
                    pool.wait_ge(pair_sum.sem, pair_sum.made(m, h))
                    if h < HG // 2:
                        both = part_sums[:, i, h, :, :]
                        pool.tensor_tensor(both[:, 0, :], both[:, 0, :], both[:, 1, :], ALU.add).then_inc(key_sum.sem, 1)
                        pool.wait_ge(key_sum.sem, key_sum.made(m, h))

            stream(pool, step)

        @block.vector
        def _(dve):
            dve.memset(ks[0:SHIFT_ROW, :, :, :], 0.0).then_inc(cleared, 1)
            dve.memset(ones[:, :], 1.0)
            dve.sem_inc(y_taken.sem, 1)
            dve.memset(pv_bank[:, :], 0.0).then_inc(cleared, 1)

            def step(turn, s):
                n = turn * U + s
                for at in range(TILES):
                    if exists(turn, s, 0):
                        dve.wait_ge(max_tile.sem, max_tile.made(n, at))
                        dve.reduce_max(maxima[:, s % 2, at % NT, at // NT:at // NT + 1], max_ps[at % 2][:, :], AX).then_inc(max_taken.sem, 1)
                    if at in (2, 5) and exists(turn, s, PV_LAG):
                        h = HG // 2 + at // 5
                        dve.wait_ge(pair_sum.sem, pair_sum.made(n - PV_LAG, h))
                        both = part_sums[:, (s - PV_LAG) % 2, h, :, :]
                        dve.tensor_tensor(both[:, 0, :], both[:, 0, :], both[:, 1, :], ALU.add).then_inc(key_sum2.sem, 1)
                    if at == 11 and exists(turn, s, PV_LAG):
                        dve.wait_ge(sumsT_ps.sem, sumsT_ps.made(n - PV_LAG, 0))
                        by_token = sums_bank[:, :].rearrange("p (k h r) -> p k h r", k=NT, h=HG)
                        dve.reciprocal(inv_sums[:, :, :], by_token[:, :, :, 0]).then_inc(inv_ready.sem, 1)
                        dve.wait_ge(inv_ready.sem, inv_ready.made(n - PV_LAG, 0))
                        dve.tensor_copy(inv_rows[:, :, :, :], bc(inv_sums[:, :, :], HEAD_ROWS)).then_inc(inv_rows_ready.sem, 1)
                    if at == 0 and exists(turn, s, OUT_LAG):
                        dve.wait_ge(inv_ps.sem, inv_ps.made(n - OUT_LAG, 0))
                        dve.wait_ge(pv_sb.sem, pv_sb.made(n - OUT_LAG, 0))
                        dve.tensor_tensor(oT[:, s % 2, :], oT_raw[:, :], sums_bank[:, :], ALU.mult).then_inc(oT_ready.sem, 1)
                    if at == TILES - 1 and s == OUT_LAG - 1 and exists(turn, s, OUT_LAG):
                        dve.wait_ge(y_ps.sem, y_ps.made(n - OUT_LAG, 0))
                        tiles = bass.ds((turn - 1) * NT, NT)
                        dve.tensor_tensor(out[:, tiles, :], y_bank[:, :].rearrange("p (k d) -> p k d", k=NT), addend(tiles),
                                          ALU.add).then_inc(y_taken.sem, 1)

            stream(dve, step)

        @block.scalar
        def _(act):
            def step(turn, s):
                n = turn * U + s
                for at in range(TILES):
                    if exists(turn, s, EXP_LAG):
                        m, i = n - EXP_LAG, (s - EXP_LAG) % 2
                        act.wait_ge(score_tile.sem, score_tile.made(m, at))
                        if at == 0 and exists(turn, s, EXP_LAG + 2):
                            act.wait_ge(pv_ps.sem, pv_ps.made(m - 2, 0))
                        act.activation(probs[:, i, at // NT, at % NT, :], exp_ps[exp_bank(s, at)][:, :], ACT.Exp,
                                       scale=a.scale).then_inc(prob_tile.sem, 1)
                    if at == 8 and exists(turn, s, PV_LAG):
                        act.wait_ge(sums_ps.sem, sums_ps.made(n - PV_LAG, 0))
                        act.copy(sums[:, :], sums_bank[:, :]).then_inc(sums_sb.sem, 1)
                    if at == 13 and exists(turn, s, PV_LAG):
                        act.wait_ge(pv_ps.sem, pv_ps.made(n - PV_LAG, 0))
                        if exists(turn, s, OUT_LAG):
                            act.wait_ge(oT_ready.sem, oT_ready.made(n - OUT_LAG, 0))
                        act.copy(oT_raw[:, :], pv_bank[:, :]).then_inc(pv_sb.sem, 1)
                    if at == 4 and exists(turn, s, 1):
                        act.wait_ge(maxT_ps.sem, maxT_ps.made(n - 1, 0))
                        act.activation(shift[:, (s - 1) % 2, :], sums_bank[0:HG, :], ACT.Copy, scale=-1.0).then_inc(shift_ready.sem, 1)

            stream(act, step)

        @block.tensor
        def _(pe):
            pe.wait_ge(cleared, 3)

            def step(turn, s):
                n = turn * U + s
                for at in range(TILES):
                    h, k = at // NT, at % NT
                    if exists(turn, s, 0):
                        if at == 0:
                            pe.wait_ge(loaded[s % RING], nth(turn, s, 16 * n_loads))
                        if at >= 2:
                            pe.wait_ge(max_taken.sem, max_taken.made(n, at - 2))
                        elif exists(turn, s, 1):
                            pe.wait_ge(max_taken.sem, max_taken.made(n - 1, TILES + at - 2))
                        pe.matmul(max_ps[at % 2][:, :], qs[0:SHIFT_ROW, s % RING, h, k * P:(k + 1) * P],
                                  ks[0:SHIFT_ROW, s % RING, h, :], start=True, stop=True).then_inc(max_tile.sem, 1)
                    if exists(turn, s, EXP_LAG):
                        m, slot = n - EXP_LAG, (s - EXP_LAG) % RING
                        if at == 0:
                            pe.wait_ge(shifted[slot], nth(turn, s - EXP_LAG, 16))
                        before = [t for t in range(at) if exp_bank(s, t) == exp_bank(s, at)]
                        if before:
                            pe.wait_ge(prob_tile.sem, prob_tile.made(m, before[-1]))
                        elif exists(turn, s, EXP_LAG + 1):
                            before = [t for t in range(TILES) if exp_bank(s - 1, t) == exp_bank(s, at)]
                            pe.wait_ge(prob_tile.sem, prob_tile.made(m - 1, before[-1]))
                        pe.matmul(exp_ps[exp_bank(s, at)][:, :], ks[0:SHIFT_ROW + HG, slot, h, k * P:(k + 1) * P],
                                  qs[0:SHIFT_ROW + HG, slot, h, :], start=True, stop=True).then_inc(score_tile.sem, 1)
                    if at == 3 and exists(turn, s, 1):
                        pe.wait_ge(max_taken.sem, max_taken.made(n - 1, TILES - 1))
                        if exists(turn, s, OUT_LAG):
                            pe.wait_ge(oT_ready.sem, oT_ready.made(n - OUT_LAG, 0))
                        for j in range(NT):
                            ins = pe.transpose(sums_bank[0:HG, j * P:(j + 1) * P], maxima[:, (s - 1) % 2, j, :], g.ident[:, :])
                        ins.then_inc(maxT_ps.sem, 1)
                    if at in (4, 15) and exists(turn, s, OUT_LAG):
                        group = (s - OUT_LAG) % U
                        if at == 4:
                            pe.wait_ge(oT_ready.sem, oT_ready.made(n - OUT_LAG, 0))
                            if group == 0:
                                pe.wait_ge(y_taken.sem, turn + (s - OUT_LAG) // U + 1)
                        for j in ((0, 1) if at == 4 else (2, 3)):
                            ins = pe.matmul(y_bank[:, j * D:(j + 1) * D], oT[:, s % 2, j * P:(j + 1) * P], w_out[:, group, :],
                                            start=(group == 0 and j == 0), stop=(group == U - 1 and j == NT - 1))
                        if at == 15:
                            ins.then_inc(y_ps.sem, 1)
                    if not exists(turn, s, PV_LAG):
                        continue
                    m, i, slot = n - PV_LAG, (s - PV_LAG) % 2, (s - PV_LAG) % RING
                    if at in (1, 5, 9, 12):
                        j = at // 4 if at < 12 else 3
                        if j == 0:
                            pe.wait_ge(v_loaded[slot], nth(turn, s - PV_LAG, 16))
                            pe.wait_ge(prob_tile.sem, prob_tile.made(m, TILES - 1))
                            if exists(turn, s, OUT_LAG):
                                pe.wait_ge(pv_sb.sem, pv_sb.made(m - 1, 0))
                        for hh in range(HG):
                            ins = pe.matmul(pv_bank[hh * HEAD_ROWS:hh * HEAD_ROWS + W, :], vs[:, slot, j, hh, :],
                                            probs[:, i, hh, j, :], start=(j == 0), stop=(j == NT - 1))
                        if j == NT - 1:
                            ins.then_inc(pv_ps.sem, 1)
                    if at == 7:
                        pe.wait_ge(key_sum.sem, key_sum.made(m, HG // 2 - 1))
                        pe.wait_ge(key_sum2.sem, key_sum2.made(m, HG // 2 - 1))
                        if exists(turn, s, 1):
                            pe.wait_ge(shift_ready.sem, shift_ready.made(n - 1, 0))
                        for hh in range(HG):
                            ins = pe.matmul(sums_bank[hh * HEAD_ROWS:(hh + 1) * HEAD_ROWS, :], ones[:, :], part_sums[:, i, hh, 0, :],
                                            start=True, stop=True)
                        ins.then_inc(sums_ps.sem, 1)
                    if at == 10:
                        pe.wait_ge(sums_sb.sem, sums_sb.made(m, 0))
                        for j in range(NT):
                            ins = pe.transpose(sums_bank[:, j * P:(j + 1) * P], sums[:, j * P:(j + 1) * P], g.ident[:, :])
                        ins.then_inc(sumsT_ps.sem, 1)
                    if at == 14:
                        pe.wait_ge(inv_rows_ready.sem, inv_rows_ready.made(m, 0))
                        for j in range(NT):
                            ins = pe.transpose(sums_bank[:, j * P:(j + 1) * P], inv_rows[:, j, :, :].rearrange("p h r -> p (h r)"), g.ident[:, :])
                        ins.then_inc(inv_ps.sem, 1)

            stream(pe, step)


def prep_l0(nc, g, ins, scratch):
    a = L0_ATT
    with ExitStack() as ctx:
        sb = lambda name, shape, dt=F32: ctx.enter_context(nc.sbuf_tensor(name + "_c", shape, dt))
        sem = phase_semaphores(nc, ctx, "_c")
        pb = lambda name: ctx.enter_context(nc.psum_tensor(name + "_ps_c", [P, N], F32))
        znT_bank, qk_bank, v_bank = pb("znT"), [pb("q"), pb("k")], pb("v")
        w = sb("w", [P, 3, D])
        col = sb("col", [P, 4])
        bv = sb("bv", [P, D])
        stats, mv, var_eps, rstd = sb("stats", [P, NT, 6]), sb("mv", [P, NT, 2]), sb("var_eps", [P, 2, NT]), sb("rstd", [P, 2, NT])
        zn, hT = sb("zn", [P, NT, D]), sb("hT", [P, N])
        qk = sb("qk", [P, 2, N])
        parts = sb("parts", [P, 2, 3, N], F16)
        v = sb("v", [P, a.groups, NT, HG, a.width])
        bo, wo_filled = sb("bo", [P, D]), sem("wo_filled")
        bo_added = Product(sem("bo_added"), NT)

        own, own2, w_loaded = sem("own"), sem("own2"), sem("w_loaded")
        made = lambda name, per=1, credit=0, unit=1: Product(sem(name), per, credit, unit)
        moments, rstd_ready = made("moments", 2), made("rstd_ready", 2)
        zn_ready, znT_ps, hT_ready = made("zn_ready", NT), made("znT_ps", 1), made("hT_ready", 1)
        qk_ps, v_ps = made("qk_ps", 2), made("v_ps", 1)
        qk_sb, part0, rest, part1, part2 = made("qk_sb", 2), made("part0"), made("rest"), made("part1"), made("part2")
        v_ready = made("v_ready", NT, NT)
        parts_stored, v_stored = made("parts_stored", 2, 2, 16), made("v_stored", 1, 1, 16)
        block = ctx.enter_context(nc.Block())

        @block.sync
        def _(sp):
            for n, name in enumerate(("wq", "wk", "wv")):
                sp.dma_start(w[:, n, :], ins["L0_ffn_" + name]).then_inc(w_loaded, 16)
            for n, name in enumerate(("ln1_g", "ln1_b", "bq", "bk")):
                sp.dma_start(col[:, n:n + 1], ins["L0_ffn_" + name].rearrange("(p a) -> p a", a=1)).then_inc(w_loaded, 16)
            sp.dma_start(bv[:, :], ins["L0_ffn_bv"].partition_broadcast(P)).then_inc(w_loaded, 16)
            sp.dma_start(bo[:, :], ins["L0_ffn_bo"].partition_broadcast(P)).then_inc(w_loaded, 16)
            sp.wait_ge(wo_filled, 1)
            wo = ins["L0_ffn_wo"].rearrange("(g h d) c -> h d g c", h=HG, d=a.width)
            for h in range(HG):
                sp.dma_start(g.wo[h * HEAD_ROWS:h * HEAD_ROWS + a.width, :, :], wo[h]).then_inc(wo_filled, 16)
            sp.sem_inc(parts_stored.sem, 32)
            sp.sem_inc(v_stored.sem, 16)
            with sp.Fori(0, B) as b:
                sp.wait_ge(v_ready.sem, v_ready.made(b, NT - 1))
                sp.dma_start(scratch.v.rearrange("(b g) p k h c -> b p g (k h c)", b=B)[b],
                             v[:, :, :, :, :].rearrange("p g k h c -> p g (k h c)")).then_inc(v_stored.sem, 16)
                wait_ge(sp, part2.sem, part2.made(b, 0), g.passed)
                for s in range(2):
                    sp.dma_start(scratch.qk[s].rearrange("r (b g) h d t -> b (g h d) r t", b=B)[b],
                                 parts[:, s, :, :]).then_inc(parts_stored.sem, 16)
            sp.wait_ge(wo_filled, 16 * HG + 1)
            sp.wait_ge(v_stored.sem, v_stored.made(B - 1, 0))
            sp.wait_ge(parts_stored.sem, parts_stored.made(B - 1, 1))

        @block.gpsimd
        def _(pool):
            pool.memset(g.wo[:, :, :], 0.0).then_inc(wo_filled, 1)
            pool.wait_ge(w_loaded, 16 * 9)
            with pool.Fori(0, B) as b:
                for i in range(2):
                    pool.wait_ge(moments.sem, moments.made(b, i))
                    pool.tensor_tensor(rstd[:, i, :], var_eps[:, i, :], g.minus_half[:, 0:NT], ALU.pow).then_inc(rstd_ready.sem, 1)
                for k in range(NT):
                    pool.wait_ge(zn_ready.sem, zn_ready.made(b, k))
                    pool.tensor_tensor(g.z[:, b * NT + k, :], g.z[:, b * NT + k, :], bo[:, :], ALU.add).then_inc(bo_added.sem, 1)
                    pool.wait_ge(bo_added.sem, bo_added.made(b, k))

        @block.vector
        def _(dve):
            dve.wait_ge(w_loaded, 16 * 9)
            dve.sem_inc(v_ready.sem, NT)

            def moments_of(rows, me, b, i):
                for k in range(NT):
                    me.did(dve.bn_stats(stats[:, k, :], rows(k)))
                me.settle(g.passed)
                for k in range(NT):
                    me.did(dve.bn_aggr(mv[:, k, :], stats[:, k, :]))
                me.settle()
                dve.tensor_scalar(var_eps[:, i, :], mv[:, :, 1], LN_EPS, None, ALU.add).then_inc(moments.sem, 1)
                dve.wait_ge(rstd_ready.sem, rstd_ready.made(b, i))

            def normalise(b):
                me = Own(dve, own, 3 * NT, b)
                moments_of(lambda k: g.x[:, b * NT + k, :], me, b, 0)
                for k in range(NT):
                    me.did(dve.tensor_scalar(g.z[:, b * NT + k, :], g.x[:, b * NT + k, :], mv[:, k, 0:1], rstd[:, 0, k:k + 1],
                                             ALU.subtract, ALU.mult))
                me.settle(g.passed)
                me.close()

            def normalise_again(b, first):
                me = Own(dve, own2, 2 * NT, b)
                moments_of(lambda k: g.z[:, b * NT + k, :], me, b, 1)
                if not first:
                    dve.wait_ge(znT_ps.sem, znT_ps.made(b - 1, 0))
                for k in range(NT):
                    dve.tensor_scalar(zn[:, k, :], g.z[:, b * NT + k, :], mv[:, k, 0:1], rstd[:, 1, k:k + 1],
                                      ALU.subtract, ALU.mult).then_inc(zn_ready.sem, 1)
                me.close()

            def step(b, ahead):
                dve.wait_ge(znT_ps.sem, znT_ps.made(b, 0))
                dve.tensor_scalar(hT[:, :], znT_bank[:, :], col[:, 0:1], col[:, 1:2], ALU.mult, ALU.add).then_inc(hT_ready.sem, 1)
                if ahead:
                    normalise(b + 1)
                for s in range(2):
                    dve.wait_ge(qk_ps.sem, qk_ps.made(b, s))
                    dve.tensor_scalar(qk[:, s, :], qk_bank[s][:, :], col[:, 2 + s:3 + s], None, ALU.add).then_inc(qk_sb.sem, 1)
                dve.wait_ge(v_ps.sem, v_ps.made(b, 0))
                dve.wait_ge(v_stored.sem, v_stored.made_before(b, 0))
                for k in range(NT):
                    split = lambda ap: ap.rearrange("p (g h d) -> p g h d", h=HG, d=a.width)
                    dve.tensor_tensor(v[:, :, k, :, :], split(v_bank[:, k * D:(k + 1) * D]), split(bv[:, :]),
                                      ALU.add).then_inc(v_ready.sem, 1)
                if ahead:
                    normalise_again(b + 1, False)
                dve.wait_ge(part0.sem, part0.made(b, 0))
                dve.tensor_tensor(qk[:, :, :], qk[:, :, :], parts[:, :, 0, :], ALU.subtract).then_inc(rest.sem, 1)
                dve.wait_ge(part1.sem, part1.made(b, 0))
                dve.tensor_tensor(parts[:, :, 2, :], qk[:, :, :], parts[:, :, 1, :], ALU.subtract).then_inc(part2.sem, 1)

            normalise(0)
            normalise_again(0, True)
            with dve.Fori(0, B - 1) as b:
                step(b, True)
            step(B - 1, False)

        @block.scalar
        def _(act):
            with act.Fori(0, B) as b:
                act.wait_ge(qk_sb.sem, qk_sb.made(b, 1))
                act.wait_ge(parts_stored.sem, parts_stored.made_before(b, 1))
                act.copy(parts[:, :, 0, :], qk[:, :, :]).then_inc(part0.sem, 1)
                act.wait_ge(rest.sem, rest.made(b, 0))
                act.copy(parts[:, :, 1, :], qk[:, :, :]).then_inc(part1.sem, 1)

        @block.tensor
        def _(pe):
            pe.wait_ge(w_loaded, 16 * 9)

            def transposes(b):
                for k in range(NT):
                    pe.wait_ge(zn_ready.sem, zn_ready.made(b, k))
                    ins = pe.transpose(znT_bank[:, k * P:(k + 1) * P], zn[:, k, :], g.ident[:, :])
                ins.then_inc(znT_ps.sem, 1)

            def projections(b):
                pe.wait_ge(hT_ready.sem, hT_ready.made(b, 0))
                for s in range(2):
                    pe.matmul(qk_bank[s][:, :], w[:, s, :], hT[:, :], start=True, stop=True).then_inc(qk_ps.sem, 1)
                pe.wait_ge(v_ready.sem, v_ready.made_before(b, NT - 1))
                for k in range(NT):
                    ins = pe.matmul(v_bank[:, k * D:(k + 1) * D], hT[:, k * P:(k + 1) * P], w[:, 2, :], start=True, stop=True)
                ins.then_inc(v_ps.sem, 1)

            transposes(0)
            with pe.Fori(0, B - 1) as b:
                projections(b)
                transposes(b + 1)
            projections(B - 1)


E_, F_ = 8, 512
FT = F_ // P


def moe_prep(nc, g, ins):
    with ExitStack() as ctx:
        sb = lambda name, shape, dt=F32: ctx.enter_context(nc.sbuf_tensor(name + "_e", shape, dt))
        sem = phase_semaphores(nc, ctx, "_e")
        pb = lambda name: ctx.enter_context(nc.psum_tensor(name + "_ps_e", [P, N], F32))
        znT_bank, logit_bank, choiceT_bank, b2_bank = pb("znT"), pb("logit"), pb("choiceT"), pb("b2")
        gate_w, gate_b, b2, col = sb("gate_w", [P, E_]), sb("gate_b", [P, E_]), sb("b2", [E_, D]), sb("col", [P, 2])
        rank, ranks_built = sb("rank", [P, NT, E_]), sem("ranks_built")
        stats, mv, var_eps, rstd = sb("stats", [P, NT, 6]), sb("mv", [P, NT, 2]), sb("var_eps", [P, NT]), sb("rstd", [P, NT])
        zn, hT = sb("zn", [P, NT, D]), sb("hT", [P, N])
        logits, best = sb("logits", [P, NT, E_]), sb("best", [P, NT])
        choice, choiceT = sb("choice", [P, NT, E_]), sb("choiceT", [E_, N])
        b1_rows, b1_bank, b1_loaded, b1T_ps, b1_kept = sb("b1_rows", [E_ * FT, P]), pb("b1T"), sem("b1_loaded"), sem("b1T_ps"), sem("b1_kept")
        own, w_loaded = sem("own"), sem("w_loaded")
        made = lambda name, per=1, credit=0: Product(sem(name), per, credit)
        moments, rstd_ready, zn_ready, znT_ps, hT_ready = made("moments"), made("rstd_ready"), made("zn_ready", NT), made("znT_ps"), made("hT_ready")
        hT_kept = made("hT_kept", 1, 1)
        logits_ps, chosen, choiceT_ps, choiceT_sb, b2_ps = made("logits_ps"), made("chosen"), made("choiceT_ps"), made("choiceT_sb"), made("b2_ps")
        x_added = made("x_added", NT, NT)
        block = ctx.enter_context(nc.Block())

        @block.sync
        def _(sp):
            sp.dma_start(gate_w[:, :], ins["L0_ffn_gate_w"]).then_inc(w_loaded, 16)
            sp.dma_start(gate_b[:, :], ins["L0_ffn_gate_b"].partition_broadcast(P)).then_inc(w_loaded, 16)
            sp.dma_start(b2[:, :], ins["L0_ffn_b2"]).then_inc(w_loaded, 16)
            for n, name in enumerate(("ln2_g", "ln2_b")):
                sp.dma_start(col[:, n:n + 1], ins["L0_ffn_" + name].rearrange("(p a) -> p a", a=1)).then_inc(w_loaded, 16)
            sp.dma_start(b1_rows[:, :], ins["L0_ffn_b1"].rearrange("e (f p) -> (e f) p", p=P)).then_inc(b1_loaded, 16)
            sp.dma_start(g.w1[:, :, :], ins["L0_ffn_w1"].rearrange("e p f -> p e f")).then_inc(g.experts_in, 16)
            sp.dma_start(g.w2[:, :, :, :], ins["L0_ffn_w2"].rearrange("e (f p) d -> p e f d", p=P)).then_inc(g.experts_in, 16)

        @block.gpsimd
        def _(pool):
            for e in range(E_):
                pool.memset(rank[:, :, e:e + 1], float(E_ - e)).then_inc(ranks_built, 1)
                pool.wait_ge(ranks_built, e + 1)
            with pool.Fori(0, B) as b:
                pool.wait_ge(moments.sem, moments.made(b, 0))
                pool.tensor_tensor(rstd[:, :], var_eps[:, :], g.minus_half[:, 0:NT], ALU.pow).then_inc(rstd_ready.sem, 1)

        @block.vector
        def _(dve):
            dve.wait_ge(w_loaded, 16 * 5)
            dve.wait_ge(ranks_built, E_)
            dve.sem_inc(x_added.sem, NT)
            with dve.Fori(0, B) as b:
                me = Own(dve, own, 3 * NT + 5, b)
                for k in range(NT):
                    me.did(dve.bn_stats(stats[:, k, :], g.z[:, b * NT + k, :]))
                me.settle(g.passed)
                for k in range(NT):
                    me.did(dve.bn_aggr(mv[:, k, :], stats[:, k, :]))
                me.settle()
                dve.tensor_scalar(var_eps[:, :], mv[:, :, 1], LN_EPS, None, ALU.add).then_inc(moments.sem, 1)
                dve.wait_ge(rstd_ready.sem, rstd_ready.made(b, 0))
                for k in range(NT):
                    dve.tensor_scalar(zn[:, k, :], g.z[:, b * NT + k, :], mv[:, k, 0:1], rstd[:, k:k + 1],
                                      ALU.subtract, ALU.mult).then_inc(zn_ready.sem, 1)
                for k in range(NT):
                    me.did(dve.tensor_tensor(g.x[:, b * NT + k, :], g.x[:, b * NT + k, :], g.z[:, b * NT + k, :], ALU.add))
                dve.wait_ge(znT_ps.sem, znT_ps.made(b, 0))
                dve.wait_ge(hT_kept.sem, hT_kept.made_before(b, 0))
                dve.tensor_scalar(hT[:, :], znT_bank[:, :], col[:, 0:1], col[:, 1:2], ALU.mult, ALU.add).then_inc(hT_ready.sem, 1)
                dve.wait_ge(logits_ps.sem, logits_ps.made(b, 0))
                gate_b4 = gate_b[:, :].unsqueeze(1).broadcast_to([P, NT, E_])
                me.did(dve.tensor_tensor(logits[:, :, :], logit_bank[:, 0:NT * E_].rearrange("p (k e) -> p k e", k=NT), gate_b4, ALU.add))
                me.settle()
                me.did(dve.tensor_reduce(best[:, :], logits[:, :, :], AX, ALU.max))
                me.settle()
                me.did(dve.tensor_tensor(logits[:, :, :], logits[:, :, :], bc(best[:, :], E_), ALU.is_equal))
                me.settle()
                me.did(dve.tensor_tensor(logits[:, :, :], logits[:, :, :], rank[:, :, :], ALU.mult))
                me.settle()
                me.did(dve.tensor_reduce(best[:, :], logits[:, :, :], AX, ALU.max))
                me.settle()
                dve.tensor_tensor(g.choice[:, bass.ds(b * NT, NT), :], logits[:, :, :], bc(best[:, :], E_), ALU.is_equal)
                dve.tensor_tensor(choice[:, :, :], logits[:, :, :], bc(best[:, :], E_), ALU.is_equal).then_inc(chosen.sem, 1)
                dve.wait_ge(choiceT_ps.sem, choiceT_ps.made(b, 0))
                dve.tensor_copy(choiceT[:, :], choiceT_bank[0:E_, :]).then_inc(choiceT_sb.sem, 1)
                dve.wait_ge(b2_ps.sem, b2_ps.made(b, 0))
                for k in range(NT):
                    dve.tensor_tensor(g.x[:, b * NT + k, :], g.x[:, b * NT + k, :], b2_bank[:, k * D:(k + 1) * D],
                                      ALU.add).then_inc(x_added.sem, 1)
                me.close()

        @block.scalar
        def _(act):
            act.sem_inc(hT_kept.sem, 1)
            act.wait_ge(b1T_ps, 1)
            act.copy(g.b1[:, :, :], b1_bank[:, 0:E_ * FT].rearrange("p (e f) -> p e f", e=E_)).then_inc(b1_kept, 1)
            with act.Fori(0, B) as b:
                act.wait_ge(hT_ready.sem, hT_ready.made(b, 0))
                act.copy(g.hT[:, b, :], hT[:, :]).then_inc(hT_kept.sem, 1)

        @block.tensor
        def _(pe):
            pe.wait_ge(b1_loaded, 16)
            pe.transpose(b1_bank[:, 0:E_ * FT], b1_rows[:, :], g.ident[0:E_ * FT, 0:E_ * FT]).then_inc(b1T_ps, 1)
            pe.wait_ge(w_loaded, 16 * 5)
            with pe.Fori(0, B) as b:
                for k in range(NT):
                    pe.wait_ge(zn_ready.sem, zn_ready.made(b, k))
                    ins_ = pe.transpose(znT_bank[:, k * P:(k + 1) * P], zn[:, k, :], g.ident[:, :])
                ins_.then_inc(znT_ps.sem, 1)
                pe.wait_ge(hT_ready.sem, hT_ready.made(b, 0))
                for k in range(NT):
                    ins_ = pe.matmul(logit_bank[:, k * E_:(k + 1) * E_], hT[:, k * P:(k + 1) * P], gate_w[:, :], start=True, stop=True)
                ins_.then_inc(logits_ps.sem, 1)
                pe.wait_ge(chosen.sem, chosen.made(b, 0))
                for k in range(NT):
                    ins_ = pe.transpose(choiceT_bank[0:E_, k * P:(k + 1) * P], choice[:, k, :], g.ident[:, :])
                ins_.then_inc(choiceT_ps.sem, 1)
                pe.wait_ge(choiceT_sb.sem, choiceT_sb.made(b, 0))
                pe.wait_ge(x_added.sem, x_added.made_before(b, NT - 1))
                for k in range(NT):
                    ins_ = pe.matmul(b2_bank[:, k * D:(k + 1) * D], choiceT[:, k * P:(k + 1) * P], b2[:, :], start=True, stop=True)
                ins_.then_inc(b2_ps.sem, 1)


def moe(nc, g):
    M = B * E_
    with ExitStack() as ctx:
        sb = lambda name, shape, dt=F32: ctx.enter_context(nc.sbuf_tensor(name + "_f", shape, dt))
        sem = phase_semaphores(nc, ctx, "_f")
        pb = lambda name: ctx.enter_context(nc.psum_tensor(name + "_ps_f", [P, N], F32))
        mid_bank, y_bank = [pb(f"mid{i}") for i in range(4)], [pb(f"y{i}") for i in range(2)]
        mid = sb("mid", [P, 2, FT, N])
        made = lambda name, per=1: Product(sem(name), per)
        mid_ps, mid_sb, y_ps, y_added = made("mid_ps", FT), made("mid_sb", FT), made("y_ps"), made("y_added", NT)
        block = ctx.enter_context(nc.Block())

        @block.vector
        def _(dve):
            def step(n, b, e, first):
                dve.wait_ge(y_ps.sem, y_ps.made(n, 0))
                for k in range(NT):
                    if not first:
                        dve.wait_ge(y_added.sem, y_added.made(n - 1, k))
                    dve.scalar_tensor_tensor(out=g.x[:, b * NT + k, :], in0=y_bank[e % 2][:, k * D:(k + 1) * D],
                                             scalar=g.choice[:, b * NT + k, e:e + 1], in1=g.x[:, b * NT + k, :],
                                             op0=ALU.mult, op1=ALU.add).then_inc(y_added.sem, 1)

            for e in range(E_):
                step(e, 0, e, e == 0)
            with dve.Fori(1, B) as b:
                for e in range(E_):
                    step(b * E_ + e, b, e, False)

        @block.scalar
        def _(act):
            act.wait_ge(g.experts_in, 32)

            def step(n, e, reuse):
                for f in range(FT):
                    act.wait_ge(mid_ps.sem, mid_ps.made(n, f))
                    if reuse and f == 0:
                        act.wait_ge(y_ps.sem, y_ps.made(n - 2, 0))
                    act.activation(mid[:, e % 2, f, :], mid_bank[f][:, :], ACT.Relu, bias=g.b1[:, e, f:f + 1]).then_inc(mid_sb.sem, 1)

            for e in range(E_):
                step(e, e, e >= 2)
            with act.Fori(1, B) as b:
                for e in range(E_):
                    step(b * E_ + e, e, True)

        @block.tensor
        def _(pe):
            pe.wait_ge(g.experts_in, 32)

            def first_product(n, b, e, reuse):
                for f in range(FT):
                    if reuse:
                        pe.wait_ge(mid_sb.sem, mid_sb.made(n - 1, f))
                    pe.matmul(mid_bank[f][:, :], g.w1[:, e, f * P:(f + 1) * P], g.hT[:, b, :], start=True, stop=True).then_inc(mid_ps.sem, 1)

            def second_product(n, e, reuse):
                pe.wait_ge(mid_sb.sem, mid_sb.made(n, FT - 1))
                if reuse:
                    pe.wait_ge(y_added.sem, y_added.made(n - 2, NT - 1))
                for k in range(NT):
                    for f in range(FT):
                        ins = pe.matmul(y_bank[e % 2][:, k * D:(k + 1) * D], mid[:, e % 2, f, k * P:(k + 1) * P], g.w2[:, e, f, :],
                                        start=(f == 0), stop=(f == FT - 1))
                ins.then_inc(y_ps.sem, 1)

            for e in range(E_):
                first_product(e, 0, e, e > 0)
                if e:
                    second_product(e - 1, e - 1, e >= 3)
            with pe.Fori(1, B) as b:
                for e in range(E_):
                    first_product(b * E_ + e, b, e, True)
                    second_product(b * E_ + e - 1, (e - 1) % E_, True)
            second_product(M - 1, E_ - 1, True)


QK_TILES = 2 * L1_ATT.heads * L1_ATT.width // P
V_HALVES = L1_ATT.heads * L1_ATT.width // N


def prep_l1(nc, g, ins, scratch):
    a = L1_ATT
    with ExitStack() as ctx:
        sb = lambda name, shape, dt=F32: ctx.enter_context(nc.sbuf_tensor(name + "_g", shape, dt))
        sem = phase_semaphores(nc, ctx, "_g")
        pb = lambda name: ctx.enter_context(nc.psum_tensor(name + "_ps_g", [P, N], F32))
        xnT_bank, bank = pb("xnT"), [pb(f"ring{i}") for i in range(4)]
        w = sb("w", [P, 3 * a.heads * a.width])
        stats, mv, var_eps, rstd = sb("stats", [P, NT, 6]), sb("mv", [P, NT, 2]), sb("var_eps", [P, NT]), sb("rstd", [P, NT])
        xn, xnT = sb("xn", [P, NT, D]), sb("xnT", [P, 2, N])
        parts = sb("parts", [P, QK_TILES, 2, N], F16)
        v = sb("v", [P, a.groups, NT, HG, a.width])
        v_cols = NT * V_HALVES
        own, w_loaded, out_loaded = sem("own"), sem("w_loaded"), sem("out_loaded")
        made = lambda name, per=1, credit=0, unit=1: Product(sem(name), per, credit, unit)
        moments, rstd_ready, zn_ready = made("moments"), made("rstd_ready"), made("xn_ready", NT, NT)
        xnT_ps, xnT_sb = made("xnT_ps", 1, 1), made("xnT_sb")
        tile_ps, part0, part1 = made("tile_ps", QK_TILES), made("part0", QK_TILES), made("part1", QK_TILES, QK_TILES)
        v_ps, v_sb = made("v_ps", v_cols), made("v_sb", v_cols, v_cols)
        parts_stored = [made(f"parts_stored{i}", 1, 1, 16) for i in range(QK_TILES)]
        v_stored = made("v_stored", 1, 1, 16)
        block = ctx.enter_context(nc.Block())

        @block.sync
        def _(sp):
            sp.dma_start(w[:, :], ins["L1_attn_w_qkv"]).then_inc(w_loaded, 16)
            sp.dma_start(g.w_out[:, :, :], ins["L1_attn_w_out"].rearrange("(c p) d -> p c d", p=P)).then_inc(out_loaded, 16)
            sp.dma_start(g.b_out[:, :], ins["L1_attn_b_out"].partition_broadcast(P)).then_inc(out_loaded, 16)
            for i in range(QK_TILES):
                sp.sem_inc(parts_stored[i].sem, 16)
            sp.sem_inc(v_stored.sem, 16)
            with sp.Fori(0, B) as b:
                for i in range(QK_TILES):
                    sp.wait_ge(part1.sem, part1.made(b, i))
                    s, j = i // (QK_TILES // 2), i % (QK_TILES // 2)
                    per = P // (HG * a.width)
                    sp.dma_start(scratch.qk[s].rearrange("r (b j g) h d t -> b j (g h d) r t", b=B, g=per)[b, j],
                                 parts[:, i, :, :]).then_inc(parts_stored[i].sem, 16)
                wait_ge(sp, v_sb.sem, v_sb.made(b, v_cols - 1), g.passed)
                sp.dma_start(scratch.v.rearrange("(b g) p k h c -> b p g (k h c)", b=B)[b],
                             v[:, :, :, :, :].rearrange("p g k h c -> p g (k h c)")).then_inc(v_stored.sem, 16)
            for i in range(QK_TILES):
                sp.wait_ge(parts_stored[i].sem, parts_stored[i].made(B - 1, 0))
            sp.wait_ge(v_stored.sem, v_stored.made(B - 1, 0))
            sp.wait_ge(out_loaded, 32)

        @block.gpsimd
        def _(pool):
            with pool.Fori(0, B) as b:
                pool.wait_ge(moments.sem, moments.made(b, 0))
                pool.tensor_tensor(rstd[:, :], var_eps[:, :], g.minus_half[:, 0:NT], ALU.pow).then_inc(rstd_ready.sem, 1)

        @block.vector
        def _(dve):
            dve.sem_inc(part1.sem, QK_TILES)

            def normalise(b, it):
                me = Own(dve, own, 2 * NT, it)
                for k in range(NT):
                    me.did(dve.bn_stats(stats[:, k, :], g.x[:, b * NT + k, :]))
                me.settle(g.passed)
                for k in range(NT):
                    me.did(dve.bn_aggr(mv[:, k, :], stats[:, k, :]))
                me.settle()
                dve.tensor_scalar(var_eps[:, :], mv[:, :, 1], LN_EPS, None, ALU.add).then_inc(moments.sem, 1)
                dve.wait_ge(rstd_ready.sem, rstd_ready.made(it, 0))
                dve.wait_ge(xnT_ps.sem, xnT_ps.made_before(it, 0))
                for k in range(NT):
                    dve.tensor_scalar(xn[:, k, :], g.x[:, b * NT + k, :], mv[:, k, 0:1], rstd[:, k:k + 1],
                                      ALU.subtract, ALU.mult).then_inc(zn_ready.sem, 1)

            with dve.Fori(0, B) as b:
                normalise(b, b)
                for i in range(QK_TILES):
                    dve.wait_ge(part0.sem, part0.made(b, i))
                    dve.tensor_tensor(parts[:, i, 1, :], bank[i % 4][:, :], parts[:, i, 0, :], ALU.subtract).then_inc(part1.sem, 1)

        @block.scalar
        def _(act):
            act.sem_inc(v_sb.sem, v_cols)
            with act.Fori(0, B) as b:
                act.wait_ge(xnT_ps.sem, xnT_ps.made(b, 0))
                act.copy(xnT[:, 0, :], xnT_bank[:, :]).then_inc(xnT_sb.sem, 1)
                for i in range(QK_TILES):
                    act.wait_ge(tile_ps.sem, tile_ps.made(b, i))
                    act.wait_ge(parts_stored[i].sem, parts_stored[i].made_before(b, 0))
                    act.copy(parts[:, i, 0, :], bank[i % 4][:, :]).then_inc(part0.sem, 1)
                act.wait_ge(v_stored.sem, v_stored.made_before(b, 0))
                for i in range(v_cols):
                    k, half = i // V_HALVES, i % V_HALVES
                    gs = slice(half * a.groups // V_HALVES, (half + 1) * a.groups // V_HALVES)
                    act.wait_ge(v_ps.sem, v_ps.made(b, i))
                    act.copy(v[:, gs, k, :, :],
                             bank[i % 4][:, :].rearrange("p (g h d) -> p g h d", h=HG, d=a.width)).then_inc(v_sb.sem, 1)

        @block.tensor
        def _(pe):
            pe.wait_ge(w_loaded, 16)
            pe.sem_inc(xnT_ps.sem, 1)
            with pe.Fori(0, B) as b:
                pe.wait_ge(zn_ready.sem, b * NT + NT)
                for k in range(NT):
                    ins_ = pe.transpose(xnT_bank[:, k * P:(k + 1) * P], xn[:, k, :], g.ident[:, :])
                ins_.then_inc(xnT_ps.sem, 1)
                pe.wait_ge(xnT_sb.sem, xnT_sb.made(b, 0))
                for i in range(QK_TILES):
                    if i < 4:
                        pe.wait_ge(v_sb.sem, v_sb.made_before(b, v_cols - 4 + i))
                    else:
                        pe.wait_ge(part1.sem, part1.made(b, i - 4))
                    pe.matmul(bank[i % 4][:, :], w[:, i * P:(i + 1) * P], xnT[:, 0, :], start=True, stop=True).then_inc(tile_ps.sem, 1)
                for i in range(v_cols):
                    k, half = i // V_HALVES, i % V_HALVES
                    if i < 4:
                        pe.wait_ge(part1.sem, part1.made(b, QK_TILES - 4 + i))
                    else:
                        pe.wait_ge(v_sb.sem, v_sb.made(b, i - 4))
                    at = QK_TILES * P + half * N
                    pe.matmul(bank[i % 4][:, :], xnT[:, 0, k * P:(k + 1) * P], w[:, at:at + N], start=True, stop=True).then_inc(v_ps.sem, 1)


L1_EPS = 1e-6


def post_l1(nc, g, ins, out):
    with ExitStack() as ctx:
        sb = lambda name, shape, dt=F32: ctx.enter_context(nc.sbuf_tensor(name + "_h", shape, dt))
        sem = phase_semaphores(nc, ctx, "_h")
        pb = lambda name: ctx.enter_context(nc.psum_tensor(name + "_ps_h", [P, N], F32))
        xnT_bank, f_bank = pb("xnT"), pb("f")
        rows = sb("rows", [P, 3, D])
        fourier, wf, filt, half = sb("fourier", [P, 3, D]), sb("wf", [P, 2, D]), sb("filter", [P, D]), sb("half", [P, 2, D])
        stats, mv, var_eps, rstd = sb("stats", [P, NT, 6]), sb("mv", [P, NT, 2]), sb("var_eps", [P, 2, NT]), sb("rstd", [P, 2, NT])
        xn, xnT, res = sb("xn", [P, NT, D]), sb("xnT", [P, N]), sb("res", [P, 2, NT, D])
        own, w_loaded = sem("own"), sem("w_loaded")
        half_ps, half_sb, filt_ps, filt_sb = sem("half_ps"), sem("half_sb"), sem("filt_ps"), sem("filt_sb")
        made = lambda name, per=1, credit=0: Product(sem(name), per, credit)
        moments, rstd_ready = made("moments", 2), made("rstd_ready", 2)
        xn_ready, xnT_ps, xnT_sb, f_ps, res_ready = made("xn_ready", NT), made("xnT_ps"), made("xnT_sb"), made("f_ps"), made("res_ready", 1, 1)
        stored = [sem(f"stored{s}") for s in range(2)]
        block = ctx.enter_context(nc.Block())

        @block.sync
        def _(sp):
            for n, name in enumerate(("L1_attn_ln_gamma", "L1_attn_ln_beta", "L1_ffn_bias")):
                sp.dma_start(rows[:, n, :], ins[name].partition_broadcast(P)).then_inc(w_loaded, 16)
            for n, name in enumerate(("L1_ffn_w_freq_real", "L1_ffn_w_freq_imag")):
                sp.dma_start(wf[:, n, :], ins[name]).then_inc(w_loaded, 16)
            sp.dma_start(fourier[:, :, :], ins["fourier"]).then_inc(w_loaded, 16)
            for s in range(2):
                sp.sem_inc(stored[s], 16)

            with sp.Fori(0, B // 2) as pair:
                for s in range(2):
                    b = pair * 2 + s
                    sp.wait_ge(res_ready.sem, res_ready.made(b, 0))
                    sp.dma_start(out.rearrange("b (k p) d -> b p k d", p=P)[b], res[:, s, :, :]).then_inc(stored[s], 16)
            for s in range(2):
                sp.wait_ge(stored[s], 16 * (B // 2 + 1))

        @block.gpsimd
        def _(pool):
            with pool.Fori(0, B) as b:
                for i in range(2):
                    pool.wait_ge(moments.sem, moments.made(b, i))
                    pool.tensor_tensor(rstd[:, i, :], var_eps[:, i, :], g.minus_half[:, 0:NT], ALU.pow).then_inc(rstd_ready.sem, 1)

        @block.vector
        def _(dve):
            dve.wait_ge(w_loaded, 16 * 6)
            dve.wait_ge(half_ps, 1)
            dve.tensor_copy(half[:, :, :], f_bank[:, 0:2 * D].rearrange("p (s d) -> p s d", s=2)).then_inc(half_sb, 1)
            dve.wait_ge(filt_ps, 1)
            dve.tensor_scalar(filt[:, :], f_bank[:, 0:D], 1.0 / D, None, ALU.mult).then_inc(filt_sb, 1)
            dve.sem_inc(res_ready.sem, 1)
            with dve.Fori(0, B // 2) as pair:
                for s in range(2):
                    b = pair * 2 + s
                    me = Own(dve, own, 8 * NT + 1, b)
                    row = lambda n: rows[:, n, :].unsqueeze(1).broadcast_to([P, NT, D])
                    x = lambda k: g.x[:, b * NT + k, :]

                    def moments_of(source, i, eps):
                        for k in range(NT):
                            me.did(dve.bn_stats(stats[:, k, :], source(k)))
                        me.settle(g.passed)
                        for k in range(NT):
                            me.did(dve.bn_aggr(mv[:, k, :], stats[:, k, :]))
                        me.settle()
                        dve.tensor_scalar(var_eps[:, i, :], mv[:, :, 1], eps, None, ALU.add).then_inc(moments.sem, 1)
                        dve.wait_ge(rstd_ready.sem, rstd_ready.made(b, i))

                    y = g.y[:, bass.ds(b * NT, NT), :]
                    moments_of(lambda k: g.y[:, b * NT + k, :], 0, L1_EPS)
                    for k in range(NT):
                        me.did(dve.tensor_scalar(g.y[:, b * NT + k, :], g.y[:, b * NT + k, :], mv[:, k, 0:1], rstd[:, 0, k:k + 1], ALU.subtract, ALU.mult))
                    me.settle()
                    for k in range(NT):
                        me.did(dve.tensor_tensor(g.y[:, b * NT + k, :], g.y[:, b * NT + k, :], rows[:, 0, :], ALU.mult))
                    me.settle()
                    for k in range(NT):
                        me.did(dve.tensor_tensor(g.y[:, b * NT + k, :], g.y[:, b * NT + k, :], x(k), ALU.add))
                    me.settle()
                    me.did(dve.tensor_tensor(y, y, row(1), ALU.add))
                    me.settle(g.passed)
                    moments_of(lambda k: g.y[:, b * NT + k, :], 1, LN_EPS)
                    for k in range(NT):
                        dve.tensor_scalar(xn[:, k, :], g.y[:, b * NT + k, :], mv[:, k, 0:1], rstd[:, 1, k:k + 1],
                                          ALU.subtract, ALU.mult).then_inc(xn_ready.sem, 1)
                    for k in range(NT):
                        me.did(dve.tensor_tensor(g.y[:, b * NT + k, :], g.y[:, b * NT + k, :], rows[:, 2, :], ALU.add))
                    me.settle()
                    dve.wait_ge(f_ps.sem, f_ps.made(b, 0))
                    dve.wait_ge(stored[s], 16 * pair + 16)
                    dve.tensor_tensor(res[:, s, :, :], f_bank[:, :].rearrange("p (k d) -> p k d", k=NT), y, ALU.add).then_inc(res_ready.sem, 1)
                    me.close()

        @block.scalar
        def _(act):
            with act.Fori(0, B) as b:
                act.wait_ge(xnT_ps.sem, xnT_ps.made(b, 0))
                act.copy(xnT[:, :], xnT_bank[:, :]).then_inc(xnT_sb.sem, 1)

        @block.tensor
        def _(pe):
            pe.wait_ge(w_loaded, 16 * 6)
            cos, sin, msin = (fourier[:, i, :] for i in range(3))
            pe.matmul(f_bank[:, 0:D], wf[:, 0, :], cos, start=True, stop=False)
            pe.matmul(f_bank[:, 0:D], wf[:, 1, :], sin, start=False, stop=True)
            pe.matmul(f_bank[:, D:2 * D], wf[:, 1, :], cos, start=True, stop=False)
            pe.matmul(f_bank[:, D:2 * D], wf[:, 0, :], msin, start=False, stop=True).then_inc(half_ps, 1)
            pe.wait_ge(half_sb, 1)
            pe.matmul(f_bank[:, 0:D], half[:, 0, :], cos, start=True, stop=False)
            pe.matmul(f_bank[:, 0:D], half[:, 1, :], msin, start=False, stop=True).then_inc(filt_ps, 1)
            pe.wait_ge(filt_sb, 1)
            with pe.Fori(0, B // 2) as pair:
                for s in range(2):
                    b = pair * 2 + s
                    for k in range(NT):
                        pe.wait_ge(xn_ready.sem, xn_ready.made(b, k))
                        ins_ = pe.transpose(xnT_bank[:, k * P:(k + 1) * P], xn[:, k, :], g.ident[:, :])
                    ins_.then_inc(xnT_ps.sem, 1)
                    pe.wait_ge(xnT_sb.sem, xnT_sb.made(b, 0))
                    pe.wait_ge(res_ready.sem, res_ready.made_before(b, 0))
                    for k in range(NT):
                        ins_ = pe.matmul(f_bank[:, k * D:(k + 1) * D], xnT[:, k * P:(k + 1) * P], filt[:, :], start=True, stop=True)
                    ins_.then_inc(f_ps.sem, 1)


def program(nc, ins, out):
    with ExitStack() as ctx:
        g = Shared()
        sb = lambda name, shape: ctx.enter_context(nc.sbuf_tensor(name, shape, F32))
        dram = lambda name, shape, dt=F32: nc.dram_tensor("scratch_" + name, shape, dt, kind="Internal").ap()
        g.x = sb("x_res", [P, T, D])
        g.ident = sb("ident", [P, P])
        g.minus_half = sb("minus_half", [P, 64])
        g.passed = ctx.enter_context(nc.semaphore("passed"))
        with ExitStack() as delta:
            sb_delta = lambda name, shape: delta.enter_context(nc.sbuf_tensor(name, shape, F32))
            g.head_mask = sb_delta("head_mask", [P, HA])
            g.two_eye = sb_delta("two_eye", [P, HA, P])
            g.fg_mask = sb_delta("fg_mask", [P, 2, HA, DA])
            scratch = Shared()
            scratch.packs, scratch.inv = dram("packs", (T, P, W_PACK)), dram("inv", (P, GB, LB, LB))
            setup(nc, g, ins)
            delta_front(nc, g, ins, scratch)
            delta_invert(nc, g, scratch)
            delta_back(nc, g, ins, scratch)

        def att_scratch(a):
            s = Shared()
            s.qk = dram("qk_" + a.name, (2, a.parts, a.total, HG, a.width, N), F16)
            s.v = dram("v_" + a.name, (a.total, P, NT, HG, a.width))
            return s

        with ExitStack() as ffn:
            sb_ffn = lambda name, shape: ffn.enter_context(nc.sbuf_tensor(name, shape, F32))
            g.z = sb_ffn("z_res", [P, T, D])
            g.wo = sb_ffn("wo", [P, L0_ATT.groups, D])
            scratch = att_scratch(L0_ATT)
            prep_l0(nc, g, ins, scratch)
            attention(nc, g, L0_ATT, scratch, g.wo, g.z, lambda tiles: g.z[:, tiles, :])
            g.experts_in = ffn.enter_context(nc.semaphore("experts_in"))
            g.w1, g.w2, g.b1 = sb_ffn("w1", [P, E_, F_]), sb_ffn("w2", [P, E_, FT, D]), sb_ffn("b1", [P, E_, FT])
            g.hT, g.choice = sb_ffn("hT_all", [P, B, N]), sb_ffn("choice_all", [P, T, E_])
            moe_prep(nc, g, ins)
            moe(nc, g)
        scratch = att_scratch(L1_ATT)
        g.y = sb("y", [P, T, D])
        g.w_out, g.b_out = sb("w_out", [P, L1_ATT.groups, D]), sb("b_out", [P, D])
        prep_l1(nc, g, ins, scratch)
        attention(nc, g, L1_ATT, scratch, g.w_out, g.y, lambda tiles: g.b_out[:, :].unsqueeze(1).broadcast_to([P, NT, D]))
        post_l1(nc, g, ins, out)


_INS = ['L0_attn_x', 'L0_attn_Wq', 'L0_attn_Wk', 'L0_attn_Wv', 'L0_attn_Wbeta', 'L0_attn_Wo', 'L0_attn_g_norm',
        'L0_ffn_ln1_g', 'L0_ffn_ln1_b', 'L0_ffn_ln2_g', 'L0_ffn_ln2_b', 'L0_ffn_wq', 'L0_ffn_bq', 'L0_ffn_wk',
        'L0_ffn_bk', 'L0_ffn_wv', 'L0_ffn_bv', 'L0_ffn_wo', 'L0_ffn_bo', 'L0_ffn_gate_w', 'L0_ffn_gate_b',
        'L0_ffn_w1', 'L0_ffn_b1', 'L0_ffn_w2', 'L0_ffn_b2', 'L1_attn_w_qkv', 'L1_attn_w_out', 'L1_attn_b_out',
        'L1_attn_ln_gamma', 'L1_attn_ln_beta', 'L1_ffn_w_freq_real', 'L1_ffn_w_freq_imag', 'L1_ffn_bias']


def fourier_rows():
    angle = 2.0 * np.pi * (np.outer(np.arange(D), np.arange(D)) % D) / D
    return np.ascontiguousarray(np.stack([np.cos(angle), np.sin(angle), -np.sin(angle)], axis=1).astype(np.float32))


def kernel(**inputs):
    import concourse.bacc as _bacc
    from concourse.bass_utils import run_bass_kernel_spmd as _run

    nc = _bacc.Bacc("TRN2", target_bir_lowering=False, num_devices=1)
    arrays = {f"in_{name}_dram": np.ascontiguousarray(inputs[name]) for name in _INS}
    arrays["in_fourier_dram"] = fourier_rows()
    ins = {name: nc.dram_tensor(f"in_{name}_dram", arrays[f"in_{name}_dram"].shape, F32, kind="ExternalInput").ap()
           for name in _INS + ["fourier"]}
    out = nc.dram_tensor("out_0_dram", (B, N, D), F32, kind="ExternalOutput").ap()
    program(nc, ins, out)
    r = _run(nc, [arrays], core_ids=[0])
    return r.results[0]["out_0_dram"]
```

```python
from contextlib import ExitStack

import numpy as np
import concourse.bass as bass
from concourse import mybir

F32 = mybir.dt.float32
F16 = mybir.dt.float16
ALU = mybir.AluOpType
ACT = mybir.ActivationFunctionType
AX = mybir.AxisListType.X

P = 128
B, N, D = 8, 512, 128
NT = N // P
T = B * NT


def phase_semaphores(nc, ctx, tag):
    held = []

    def clear():
        nc.clear_and_free_semaphores(held)
        nc.all_engine_barrier()

    def new(name):
        held.append(nc.alloc_semaphore(name=name + tag))
        return held[-1]

    ctx.callback(clear)
    return new


def wait_ge(eng, sem, value, apart=None):
    eng.wait_ge(sem, value)
    if apart is not None:
        eng.sem_inc(apart, 1)


class Shared:
    pass


class Product:

    def __init__(self, sem, per, credit=0, unit=1):
        self.sem, self.per, self.credit, self.unit = sem, per, credit, unit

    def made(self, it, k):
        return (it * self.per + (k + 1 + self.credit)) * self.unit

    def made_before(self, it, k, ago=1):
        assert self.credit >= ago * self.per
        return (it * self.per + (k + 1 + self.credit - ago * self.per)) * self.unit


class Own:

    def __init__(self, eng, sem, per, it):
        self.eng, self.sem, self.per, self.it, self.n = eng, sem, per, it, 0

    def did(self, ins):
        ins.then_inc(self.sem, 1)
        self.n += 1

    def settle(self, apart=None):
        wait_ge(self.eng, self.sem, self.it * self.per + self.n, apart)

    def close(self):
        assert self.n == self.per, (self.n, self.per)


def bc(ap, n):
    return ap.unsqueeze(len(ap.shape)).broadcast_to([*ap.shape, n])


HA, DA = 4, 32
W_A = 3 * D + HA
LB = 16
GB = P // LB
RHS, Q_, K_, KT_, QT_, LT_ = 0, 2 * D, 3 * D, 4 * D, 5 * D, 6 * D
W_PACK = 6 * D + HA * P
LN_EPS = 1e-5
RMS_EPS = 1e-5


def setup(nc, g, ins):
    with ExitStack() as ctx:
        sem = phase_semaphores(nc, ctx, "_setup")
        filled, ident_ready, eye_built, mask_built, loaded = (
            sem("filled"), sem("ident_ready"), sem("eye_built"), sem("mask_built"), sem("loaded"))
        block = ctx.enter_context(nc.Block())

        @block.sync
        def _(sp):
            sp.dma_start(g.x[:, 0:T, :], ins["L0_attn_x"].rearrange("b (k p) d -> p (b k) d", p=P)).then_inc(loaded, 16)
            sp.wait_ge(loaded, 16)

        @block.gpsimd
        def _(pool):
            pool.memset(g.ident[:, :], 0.0).then_inc(filled, 1)
            pool.memset(g.head_mask[:, :], 1.0).then_inc(filled, 1)
            pool.memset(g.minus_half[:, :], -0.5).then_inc(filled, 1)
            pool.wait_ge(filled, 3)
            pool.affine_select(out=g.ident[:, :], in_=g.ident[:, :], compare_op=ALU.not_equal, fill=1.0,
                               base=0, pattern=[[-1, P]], channel_multiplier=1).then_inc(ident_ready, 1)
            pool.affine_select(out=g.head_mask[:, :], in_=g.head_mask[:, :], compare_op=ALU.is_ge, fill=0.0,
                               base=0, pattern=[[-DA, HA]], channel_multiplier=1).then_inc(mask_built, 1)
            pool.wait_ge(mask_built, 1)
            pool.affine_select(out=g.head_mask[:, :], in_=g.head_mask[:, :], compare_op=ALU.is_ge, fill=0.0,
                               base=DA - 1, pattern=[[DA, HA]], channel_multiplier=-1).then_inc(mask_built, 1)

        @block.vector
        def _(dve):
            dve.wait_ge(ident_ready, 1)
            for h in range(HA):
                last = dve.tensor_scalar(g.two_eye[:, h, :], g.ident[:, :], 2.0, None, ALU.mult)
            last.then_inc(eye_built, 1)
            dve.wait_ge(mask_built, 2)
            dve.tensor_scalar(g.fg_mask[:, 1, :, :], bc(g.head_mask[:, :], DA), 1.0, None, ALU.mult)
            dve.tensor_scalar(g.fg_mask[:, 0, :, :], bc(g.head_mask[:, :], DA), -1.0, None,
                              ALU.mult).then_inc(eye_built, 1)
            dve.wait_ge(eye_built, 2)


class TilePack:

    def __init__(self, pack, s, k):
        a = pack[:, s, k, :]
        by_head = lambda at: a[:, at:at + D].rearrange("p (h d) -> p h d", d=DA)
        self.rhs = a[:, RHS:RHS + 2 * D].rearrange("p (s h d) -> p s h d", s=2, d=DA)
        self.q, self.k = by_head(Q_), by_head(K_)
        self.kT, self.qT = a[:, KT_:KT_ + P], a[:, QT_:QT_ + P]
        self.lt = a[:, LT_:LT_ + HA * P].rearrange("p (h d) -> p h d", d=P)


def delta_front(nc, g, ins, scratch):
    with ExitStack() as ctx:
        sb = lambda name, shape: ctx.enter_context(nc.sbuf_tensor(name, shape, F32))
        sem = phase_semaphores(nc, ctx, "_a")
        ps = [[ctx.enter_context(nc.psum_tensor(f"fps{k}{j}", [P, 512], F32)) for j in range(2)] for k in range(NT)]
        w = sb("w_a", [P, W_A])
        xn = sb("xn_a", [P, NT, P])
        xnT = sb("xnT_a", [P, NT, P])
        squares = sb("squares", [P, NT, 2 * D])
        stats = sb("stats_a", [P, NT, 6])
        mv = sb("mv_a", [P, NT, 2])
        var_eps = sb("var_eps_a", [P, NT])
        rstd = sb("rstd_a", [P, NT])
        norm2 = sb("norm2", [P, NT, 2 * HA])
        inv_norm = sb("inv_norm", [P, NT, 2 * HA])
        beta = sb("beta", [P, NT, HA])
        bk_heads = sb("bk_heads", [P, NT, HA, P])
        pack = sb("pack_a", [P, 2, NT, W_PACK])

        own, own_heads = sem("own"), sem("own_heads")
        w_loaded = sem("w_a_loaded")
        moments = Product(sem("moments"), 1)
        rstd_ready = Product(sem("rstd_ready"), 1)
        norm2_ready = Product(sem("norm2_ready"), 2)
        inv_norm_ready = Product(sem("inv_norm_ready"), 2)
        xn_ready = Product(sem("xn_ready"), NT)
        xnT_ps = Product(sem("xnT_ps"), NT)
        xnT_sb = Product(sem("xnT_sb"), NT)
        proj_ps = Product(sem("proj_ps"), NT)
        squared = Product(sem("squared"), NT)
        beta_exp = Product(sem("beta_exp"), NT)
        normed = Product(sem("normed"), NT)
        kqT_ps = Product(sem("kqT_ps"), NT)
        kT_sb = Product(sem("kT_sb"), NT)
        qT_sb = Product(sem("qT_sb"), NT)
        bk_ready = Product(sem("bk_ready"), NT)
        lt_ps = Product(sem("lt_ps"), NT)
        lt_sb = Product(sem("lt_sb"), NT, credit=NT)
        lt_masked = Product(sem("lt_masked"), 2 * NT)
        stored = [[sem(f"stored{s}{k}") for k in range(NT)] for s in range(2)]

        block = ctx.enter_context(nc.Block())

        @block.sync
        def _(sp):
            for n, name in enumerate(("L0_attn_Wq", "L0_attn_Wk", "L0_attn_Wv", "L0_attn_Wbeta")):
                sp.dma_start(w[:, n * D:n * D + ins[name].shape[1]], ins[name]).then_inc(w_loaded, 16)
            for s in range(2):
                for k in range(NT):
                    sp.sem_inc(stored[s][k], 16)
            with sp.Fori(0, B // 2) as pair:
                for s in range(2):
                    b = pair * 2 + s
                    for k in range(NT):
                        wait_ge(sp, lt_masked.sem, lt_masked.made(b, NT + k), g.passed)
                        sp.wait_ge(qT_sb.sem, qT_sb.made(b, k))
                        sp.dma_start(scratch.packs[b * NT + k], pack[:, s, k, :]).then_inc(stored[s][k], 16)
            for s in range(2):
                for k in range(NT):
                    sp.wait_ge(stored[s][k], 16 * (B // 2 + 1))

        @block.vector
        def _(dve):
            def take_moments(b):
                me = Own(dve, own, 2 * NT, b)
                for k in range(NT):
                    me.did(dve.bn_stats(stats[:, k, :], g.x[:, b * NT + k, :]))
                me.settle(g.passed)
                for k in range(NT):
                    me.did(dve.bn_aggr(mv[:, k, :], stats[:, k, :]))
                me.settle()
                dve.tensor_scalar(var_eps[:, :], mv[:, :, 1], LN_EPS, None, ALU.add).then_inc(moments.sem, 1)
                me.close()

            def normalise(b, first=False):
                dve.wait_ge(rstd_ready.sem, rstd_ready.made(b, 0))
                for k in range(NT):
                    if not first:
                        dve.wait_ge(xnT_ps.sem, xnT_ps.made(b - 1, k))
                    dve.tensor_scalar(xn[:, k, :], g.x[:, b * NT + k, :], mv[:, k, 0:1], rstd[:, k:k + 1],
                                      ALU.subtract, ALU.mult).then_inc(xn_ready.sem, 1)

            def step(pair, s, ahead):
                b = pair * 2 + s
                tiles = [TilePack(pack, s, k) for k in range(NT)]
                me = Own(dve, own_heads, NT + 2, b)
                dve.wait_ge(beta_exp.sem, beta_exp.made(b, NT - 1))
                me.did(dve.tensor_scalar(beta[:, :, :], beta[:, :, :], 1.0, None, ALU.add))
                dve.wait_ge(squared.sem, squared.made(b, NT - 1))
                for half in range(2):
                    ks = slice(half * NT // 2, (half + 1) * NT // 2)
                    dve.tensor_reduce(norm2[:, ks, :], squares[:, ks, :].rearrange("p k (h d) -> p (k h) d", d=DA),
                                      AX, ALU.add).then_inc(norm2_ready.sem, 1)
                me.settle()
                me.did(dve.reciprocal(beta[:, :, :], beta[:, :, :]))
                if ahead:
                    take_moments(b + 1)
                me.settle()
                by_head = lambda k: ps[k][1][:, 0:3 * D].rearrange("p (h d) -> p h d", d=DA)
                for k in range(NT):
                    dve.wait_ge(stored[s][k], 16 * pair + 16)
                    dve.tensor_tensor(tiles[k].rhs[:, 0, :, :], by_head(k)[:, 2 * HA:, :], bc(beta[:, k, :], DA), ALU.mult)
                for k in range(NT):
                    dve.wait_ge(inv_norm_ready.sem, inv_norm_ready.made(b, k // (NT // 2)))
                    dve.tensor_tensor(tiles[k].q, by_head(k)[:, 0:HA, :], bc(inv_norm[:, k, 0:HA], DA), ALU.mult)
                    me.did(dve.tensor_tensor(tiles[k].k, by_head(k)[:, HA:2 * HA, :], bc(inv_norm[:, k, HA:], DA), ALU.mult))
                me.settle()
                for k in range(NT):
                    dve.tensor_tensor(tiles[k].rhs[:, 1, :, :], tiles[k].k, bc(beta[:, k, :], DA),
                                      ALU.mult).then_inc(normed.sem, 1)
                for k in range(NT):
                    dve.wait_ge(kqT_ps.sem, kqT_ps.made(b, k))
                    dve.tensor_tensor(bk_heads[:, k, :, :], ps[k][0][:, 2 * P:3 * P].unsqueeze(1).broadcast_to([P, HA, P]),
                                      bc(g.head_mask[:, :], P), ALU.mult).then_inc(bk_ready.sem, 1)
                if ahead:
                    normalise(b + 1)
                me.close()

            take_moments(0)
            normalise(0, first=True)
            with dve.Fori(0, B // 2 - 1) as pair:
                for s in range(2):
                    step(pair, s, True)
            step(B // 2 - 1, 0, True)
            step(B // 2 - 1, 1, False)

        @block.scalar
        def _(act):
            act.sem_inc(lt_sb.sem, NT)

            def transposed(b, k):
                act.wait_ge(xnT_ps.sem, xnT_ps.made(b, k))
                act.copy(xnT[:, k, :], ps[k][0][:, 0:P]).then_inc(xnT_sb.sem, 1)

            def step(pair, s, ahead):
                b = pair * 2 + s
                for k in range(NT):
                    act.wait_ge(proj_ps.sem, proj_ps.made(b, k))
                    act.activation(beta[:, k, :], ps[k][1][:, 3 * D:W_A], ACT.Exp, scale=-1.0).then_inc(beta_exp.sem, 1)
                    act.activation(squares[:, k, :], ps[k][1][:, 0:2 * D], ACT.Square).then_inc(squared.sem, 1)
                for k in range(NT):
                    tile = TilePack(pack, s, k)
                    act.wait_ge(bk_ready.sem, bk_ready.made(b, k))
                    act.copy(tile.kT, ps[k][0][:, P:2 * P]).then_inc(kT_sb.sem, 1)
                    act.copy(tile.qT, ps[k][0][:, 0:P]).then_inc(qT_sb.sem, 1)
                for k in range(NT):
                    act.wait_ge(lt_ps.sem, lt_ps.made(b, k))
                    act.copy(TilePack(pack, s, k).lt, ps[k][1][:, :].rearrange("p (h i) -> p h i", h=HA)).then_inc(lt_sb.sem, 1)
                    if ahead:
                        transposed(b + 1, k)

            for k in range(NT):
                transposed(0, k)
            with act.Fori(0, B // 2 - 1) as pair:
                for s in range(2):
                    step(pair, s, True)
            step(B // 2 - 1, 0, True)
            step(B // 2 - 1, 1, False)

        @block.gpsimd
        def _(pool):
            def reciprocal_std(b):
                pool.wait_ge(moments.sem, moments.made(b, 0))
                pool.tensor_tensor(rstd[:, :], var_eps[:, :], g.minus_half[:, 0:NT], ALU.pow).then_inc(rstd_ready.sem, 1)

            def step(pair, s, ahead):
                b = pair * 2 + s
                for half in range(2):
                    ks = slice(half * NT // 2, (half + 1) * NT // 2)
                    pool.wait_ge(norm2_ready.sem, norm2_ready.made(b, half))
                    pool.tensor_tensor(inv_norm[:, ks, :], norm2[:, ks, :],
                                       g.minus_half[:, 0:NT * HA].rearrange("p (k h) -> p k h", h=2 * HA), ALU.pow).then_inc(inv_norm_ready.sem, 1)
                    pool.wait_ge(inv_norm_ready.sem, inv_norm_ready.made(b, half))
                if ahead:
                    reciprocal_std(b + 1)
                for k in range(NT):
                    lt = TilePack(pack, s, k).lt
                    wait_ge(pool, lt_sb.sem, lt_sb.made(b, k), g.passed)
                    pool.affine_select(out=lt, in_=lt, compare_op=ALU.is_gt, fill=0.0, base=0,
                                       pattern=[[0, HA], [1, P]], channel_multiplier=-1).then_inc(lt_masked.sem, 1)
                for k in range(NT):
                    lt = TilePack(pack, s, k).lt
                    wait_ge(pool, lt_masked.sem, lt_masked.made(b, k), g.passed)
                    pool.affine_select(out=lt, in_=lt, compare_op=ALU.not_equal, fill=1.0, base=0,
                                       pattern=[[0, HA], [1, P]], channel_multiplier=-1).then_inc(lt_masked.sem, 1)

            reciprocal_std(0)
            with pool.Fori(0, B // 2 - 1) as pair:
                for s in range(2):
                    step(pair, s, True)
            step(B // 2 - 1, 0, True)
            step(B // 2 - 1, 1, False)

        @block.tensor
        def _(pe):
            pe.wait_ge(w_loaded, 64)

            def transpose_xn(b, k):
                pe.wait_ge(xn_ready.sem, xn_ready.made(b, k))
                pe.transpose(ps[k][0][:, 0:P], xn[:, k, :], g.ident[:, :]).then_inc(xnT_ps.sem, 1)

            def step(pair, s, ahead):
                b = pair * 2 + s
                for k in range(NT):
                    pe.wait_ge(xnT_sb.sem, xnT_sb.made(b, k))
                    pe.wait_ge(lt_sb.sem, lt_sb.made_before(b, k))
                    pe.matmul(ps[k][1][:, 0:W_A], xnT[:, k, :], w[:, :], start=True, stop=True).then_inc(proj_ps.sem, 1)
                for k in range(NT):
                    tile = TilePack(pack, s, k)
                    pe.wait_ge(normed.sem, normed.made(b, k))
                    pe.transpose(ps[k][0][:, 0:P], tile.q, g.ident[:, :])
                    pe.transpose(ps[k][0][:, P:2 * P], tile.k, g.ident[:, :])
                    pe.transpose(ps[k][0][:, 2 * P:3 * P], tile.rhs[:, 1, :, :], g.ident[:, :]).then_inc(kqT_ps.sem, 1)
                for k in range(NT):
                    pe.wait_ge(kT_sb.sem, kT_sb.made(b, k))
                    pe.matmul(ps[k][1][:, :], TilePack(pack, s, k).kT, bk_heads[:, k, :, :], start=True,
                              stop=True).then_inc(lt_ps.sem, 1)
                    if ahead:
                        pe.wait_ge(qT_sb.sem, qT_sb.made(b, k))
                        transpose_xn(b + 1, k)

            for k in range(NT):
                transpose_xn(0, k)
            with pe.Fori(0, B // 2 - 1) as pair:
                for s in range(2):
                    step(pair, s, True)
            step(B // 2 - 1, 0, True)
            step(B // 2 - 1, 1, False)


def delta_invert(nc, g, scratch):
    n_blocks = T * HA * GB // P
    assert T * HA == P and n_blocks == GB
    with ExitStack() as ctx:
        sb = lambda name, shape: ctx.enter_context(nc.sbuf_tensor(name, shape, F32))
        sem = phase_semaphores(nc, ctx, "_inv")
        ltb = sb("lt_blocks", [P, GB, LB, LB])
        inv = sb("inv_blocks", [P, GB, LB, LB])
        terms = sb("terms", [P, GB, LB, LB])
        loaded, own, stored, zeroed, eye = (
            sem("blocks_loaded"), sem("dve_own"), sem("blocks_stored"), sem("inv_zeroed"), sem("inv_eye"))
        block = ctx.enter_context(nc.Block())

        def load(eng, blocks):
            per_block = scratch.packs[:, :, LT_:].rearrange("t (g j) (h q) -> g t h j q", g=GB, h=HA)
            for n in blocks:
                for h in range(HA):
                    eng.dma_start(ltb[h::HA, n, :, :], per_block[n, :, h, :, n * LB:(n + 1) * LB]).then_inc(loaded, 16)

        @block.scalar
        def _(act):
            load(act, range(GB // 2, GB))

        @block.sync
        def _(sp):
            load(sp, range(GB // 2))
            sp.wait_ge(own, 2 * (LB - 1))
            sp.dma_start(scratch.inv, inv[:, :, :, :]).then_inc(stored, 16)
            sp.wait_ge(stored, 16)

        @block.gpsimd
        def _(pool):
            pool.memset(inv[:, :, :, :], 0.0).then_inc(zeroed, 1)

        @block.vector
        def _(dve):
            dve.wait_ge(zeroed, 1)
            dve.memset(inv[:, :, :, :].rearrange("p g i c -> p g (i c)")[:, :, 0::LB + 1], 1.0).then_inc(eye, 1)
            dve.wait_ge(eye, 1)
            dve.wait_ge(loaded, 16 * 4 * GB)
            for i in range(1, LB):
                for_j = bc(ltb[:, :, 0:i, i], i).rearrange("p g j c -> p g c j")
                dve.tensor_tensor(terms[:, :, 0:i, 0:i], for_j, inv[:, :, 0:i, 0:i].rearrange("p g j c -> p g c j"),
                                  ALU.mult).then_inc(own, 1)
                dve.wait_ge(own, 2 * i - 1)
                dve.tensor_reduce(inv[:, :, i, 0:i], terms[:, :, 0:i, 0:i], AX, ALU.add, negate=True).then_inc(own, 1)
                dve.wait_ge(own, 2 * i)


def delta_back(nc, g, ins, scratch):
    with ExitStack() as ctx:
        sb = lambda name, shape: ctx.enter_context(nc.sbuf_tensor(name, shape, F32))
        sem = phase_semaphores(nc, ctx, "_b")
        ps = [[ctx.enter_context(nc.psum_tensor(f"bps{k}{j}", [P, 512], F32)) for j in range(2)] for k in range(NT)]
        by_head = lambda bank: bank[:, :].rearrange("p (h i) -> p h i", h=HA)
        pack = sb("pack_b", [P, 2, NT, W_PACK])
        inv = sb("inv_b", [P, 2, NT, HA, P])
        invT = sb("invT_b", [P, NT, HA, P])
        resid = sb("newton_residual", [P, NT, HA, P])
        grown = sb("grown_b", [P, NT, HA, P])
        grownT = sb("grownT_b", [P, NT, HA, P])
        q_heads = sb("q_heads", [P, NT, HA, P])
        y0 = sb("y0", [P, NT, 2, HA, DA])
        err = sb("err", [P, NT, 2, HA, DA])
        uw = sb("uw", [P, NT, 2, HA, DA])
        within = sb("within", [P, NT, HA, DA])
        qt = sb("q_tilde", [P, NT, HA, DA])
        qtT = sb("q_tildeT", [P, NT, P])
        fg = sb("fg", [P, NT, 2, P])
        state = sb("state", [P, NT, P])
        o = sb("o_a", [P, NT, HA, DA])
        o2 = sb("o2_a", [P, NT, HA, DA])
        ms = sb("ms_a", [P, NT, HA])
        inv_rms = sb("inv_rms", [P, NT, HA])
        oT = sb("oT_a", [P, NT, P])
        wo = sb("wo_a", [P, P])
        g_col = sb("g_col", [P, 1])

        w_loaded, own, cleared, wo_ready = sem("wo_a_loaded"), sem("dve_own"), sem("inv_cleared"), sem("wo_a_ready")
        pack_in = [[sem(f"pack_in{s}{k}") for k in range(NT)] for s in range(2)]
        inv_in = [sem(f"inv_in{s}") for s in range(2)]
        made = lambda name, per=NT, credit=0: Product(sem(name), per, credit)
        q_heads_ready = made("q_heads_ready")
        qk_ps, qk_sb, qk_masked = made("qk_ps"), made("qk_sb"), made("qk_masked")
        invT_ready = made("invT_ready")
        lt0_ps, r0_ready = made("lt0_ps"), made("r0_ready")
        t1_ps, t1_sb = made("t1_ps"), made("t1_sb")
        t1T_ps, t1T_sb = made("t1T_ps"), made("t1T_sb")
        lt1_ps, r1_ready = made("lt1_ps"), made("r1_ready")
        t2T_ps, t2T_sb = made("t2T_ps"), made("t2T_sb")
        y0_ps, y0_sb = made("y0_ps"), made("y0_sb")
        ly_ps, err_ready = made("ly_ps"), made("err_ready")
        dy_ps, uw_ready = made("dy_ps"), made("uw_ready")
        muw_ps, qt_ready = made("muw_ps"), made("qt_ready")
        fg_ps, fg_masked = made("fg_ps"), made("fg_masked")
        qtT_ps, qtT_sb = made("qtT_ps"), made("qtT_sb")
        f_ready = made("f_ready")
        state_ps, state_ready = made("state_ps", NT - 2), made("state_ready", NT - 1)
        cross_ps, o_ready = made("cross_ps", NT - 1), made("o_ready")
        o2_ready, ms_ready, inv_rms_ready, on_ready = made("o2_ready"), made("ms_ready", 1), made("inv_rms_ready", 1), made("on_ready")
        oT_ps, oT_sb = made("oT_ps"), made("oT_sb")
        out_ps = made("out_ps", credit=2 * NT)
        added = made("added")

        def stream(eng, step, tail):
            step(0, 0, True)
            step(0, 1, False)
            with eng.Fori(1, B // 2) as pair:
                for s in range(2):
                    step(pair, s, False)
            for part in tail:
                part(B - 1)

        block = ctx.enter_context(nc.Block())

        @block.sync
        def _(sp):
            sp.dma_start(wo[:, :], ins["L0_attn_Wo"]).then_inc(w_loaded, 16)
            for h in range(HA):
                sp.dma_start(g_col[h * DA:(h + 1) * DA, :], ins["L0_attn_g_norm"].rearrange("(d a) -> d a", a=1)).then_inc(w_loaded, 16)
            sp.wait_ge(cleared, 2)
            blocks = scratch.inv.rearrange("th g i c -> g i th c")
            with sp.Fori(0, B // 2) as pair:
                for s in range(2):
                    b = pair * 2 + s
                    for k in range(NT):
                        sp.wait_ge(out_ps.sem, out_ps.made_before(b, k, 2))
                        sp.dma_start(pack[:, s, k, :], scratch.packs[b * NT + k]).then_inc(pack_in[s][k], 16)
                    for n in range(GB):
                        sp.dma_start(inv[n * LB:(n + 1) * LB, s, :, :, n * LB:(n + 1) * LB].rearrange("i k h c -> i (k h) c"),
                                     blocks[n, :, bass.ds(b * NT * HA, NT * HA), :]).then_inc(inv_in[s], 16)

        @block.gpsimd
        def _(pool):
            for s in range(2):
                pool.memset(inv[:, s, :, :, :], 0.0).then_inc(cleared, 1)
            pool.wait_ge(w_loaded, 16 * (1 + HA))
            pool.tensor_scalar(wo[:, :], wo[:, :], g_col[:, 0:1], None, ALU.mult).then_inc(wo_ready, 1)
            with pool.Fori(0, B // 2) as pair:
                for s in range(2):
                    b = pair * 2 + s
                    tiles = [TilePack(pack, s, k) for k in range(NT)]
                    for k in range(NT):
                        pool.wait_ge(pack_in[s][k], 16 * pair + 16)
                        pool.tensor_tensor(q_heads[:, k, :, :], tiles[k].qT.unsqueeze(1).broadcast_to([P, HA, P]),
                                           bc(g.head_mask[:, :], P), ALU.mult).then_inc(q_heads_ready.sem, 1)
                    for k in range(NT):
                        wait_ge(pool, qk_sb.sem, qk_sb.made(b, k), g.passed)
                        pool.affine_select(out=resid[:, k, :, :], in_=resid[:, k, :, :], compare_op=ALU.is_ge, fill=0.0,
                                           base=0, pattern=[[0, HA], [1, P]], channel_multiplier=-1).then_inc(qk_masked.sem, 1)
                    for k in range(NT):
                        pool.wait_ge(fg_masked.sem, fg_masked.made(b, k))
                        pool.tensor_tensor(fg[:, k, 0, :], fg[:, k, 0, :], g.ident[:, :], ALU.add).then_inc(f_ready.sem, 1)
                    for k in range(NT):
                        pool.wait_ge(o_ready.sem, o_ready.made(b, k))
                        pool.tensor_tensor(o2[:, k, :, :], o[:, k, :, :], o[:, k, :, :], ALU.mult).then_inc(o2_ready.sem, 1)
                    pool.wait_ge(ms_ready.sem, ms_ready.made(b, 0))
                    pool.tensor_tensor(inv_rms[:, :, :], ms[:, :, :], g.minus_half[:, 0:NT * HA].rearrange("p (k h) -> p k h", k=NT),
                                       ALU.pow).then_inc(inv_rms_ready.sem, 1)

        @block.vector
        def _(dve):
            def normalised(b):
                dve.wait_ge(inv_rms_ready.sem, inv_rms_ready.made(b, 0))
                for k in range(NT):
                    dve.tensor_tensor(o[:, k, :, :], o[:, k, :, :], bc(inv_rms[:, k, :], DA), ALU.mult).then_inc(on_ready.sem, 1)

            def add_projection(b):
                for k in range(NT):
                    dve.wait_ge(out_ps.sem, out_ps.made(b, k))
                    dve.tensor_tensor(g.x[:, b * NT + k, :], g.x[:, b * NT + k, :], ps[k][0][:, 0:P], ALU.add).then_inc(added.sem, 1)

            def step(pair, s, first):
                b = pair * 2 + s
                tiles = [TilePack(pack, s, k) for k in range(NT)]
                me = Own(dve, own, 1, b)
                dve.wait_ge(inv_in[s], (16 * GB) * pair + 16 * GB)
                for k in range(NT):
                    dve.transpose(invT[:, k, :, :], inv[:, s, k, :, :]).then_inc(invT_ready.sem, 1)
                if not first:
                    normalised(b - 1)
                for k in range(NT):
                    dve.wait_ge(lt0_ps.sem, lt0_ps.made(b, k))
                    dve.scalar_tensor_tensor(out=resid[:, k, :, :], in0=by_head(ps[k][0]), scalar=-1.0,
                                             in1=g.two_eye[:, :, :], op0=ALU.mult, op1=ALU.add).then_inc(r0_ready.sem, 1)
                if not first:
                    add_projection(b - 1)
                for k in range(NT):
                    dve.wait_ge(lt1_ps.sem, lt1_ps.made(b, k))
                    dve.scalar_tensor_tensor(out=resid[:, k, :, :], in0=by_head(ps[k][1]), scalar=-1.0,
                                             in1=g.two_eye[:, :, :], op0=ALU.mult, op1=ALU.add).then_inc(r1_ready.sem, 1)
                half = lambda bank: bank[:, 0:2 * D].rearrange("p (s h d) -> p s h d", s=2, d=DA)
                for k in range(NT):
                    dve.wait_ge(ly_ps.sem, ly_ps.made(b, k))
                    dve.tensor_tensor(err[:, k, :, :, :], tiles[k].rhs, half(ps[k][0]), ALU.subtract).then_inc(err_ready.sem, 1)
                for k in range(NT):
                    dve.wait_ge(dy_ps.sem, dy_ps.made(b, k))
                    dve.wait_ge(y0_sb.sem, y0_sb.made(b, k))
                    dve.tensor_tensor(uw[:, k, :, :, :], half(ps[k][1]), y0[:, k, :, :, :], ALU.add).then_inc(uw_ready.sem, 1)
                for k in range(NT):
                    dve.wait_ge(fg_ps.sem, fg_ps.made(b, k))
                    dve.tensor_tensor(fg[:, k, :, :], ps[k][1][:, 0:2 * P].rearrange("p (s c) -> p s c", s=2),
                                      g.fg_mask[:, :, :, :].rearrange("p s h d -> p s (h d)"), ALU.mult).then_inc(fg_masked.sem, 1)
                for k in range(NT):
                    dve.wait_ge(muw_ps.sem, muw_ps.made(b, k))
                    dve.tensor_copy(within[:, k, :, :], half(ps[k][0])[:, 0, :, :])
                    dve.tensor_tensor(qt[:, k, :, :], tiles[k].q, half(ps[k][0])[:, 1, :, :], ALU.subtract).then_inc(qt_ready.sem, 1)
                dve.wait_ge(fg_masked.sem, fg_masked.made(b, NT - 1))
                dve.wait_ge(qt_ready.sem, qt_ready.made(b, NT - 1))
                dve.tensor_copy(state[:, 1, :], fg[:, 0, 1, :]).then_inc(state_ready.sem, 1)
                dve.tensor_copy(o[:, 0, :, :], within[:, 0, :, :]).then_inc(o_ready.sem, 1)
                for k in range(1, NT):
                    if k < NT - 1:
                        dve.wait_ge(state_ps.sem, state_ps.made(b, k - 1))
                        dve.tensor_tensor(state[:, k + 1, :], ps[k][1][:, 0:P], fg[:, k, 1, :], ALU.add).then_inc(state_ready.sem, 1)
                    dve.wait_ge(cross_ps.sem, cross_ps.made(b, k - 1))
                    dve.tensor_tensor(o[:, k, :, :], ps[k][0][:, 0:P].rearrange("p (h d) -> p h d", d=DA), within[:, k, :, :],
                                      ALU.add).then_inc(o_ready.sem, 1)
                dve.wait_ge(o2_ready.sem, o2_ready.made(b, NT - 1))
                me.did(dve.tensor_reduce(ms[:, :, :], o2[:, :, :, :], AX, ALU.add))
                me.settle()
                dve.tensor_scalar(ms[:, :, :], ms[:, :, :], 1.0 / DA, RMS_EPS, ALU.mult, ALU.add).then_inc(ms_ready.sem, 1)
                me.close()

            stream(dve, step, (normalised, add_projection))

        @block.scalar
        def _(act):
            def evacuate(b, source, bank_of, target, ready):
                for k in range(NT):
                    act.wait_ge(source.sem, source.made(b, k))
                    act.copy(target(k), bank_of(k)).then_inc(ready.sem, 1)

            def output(b):
                evacuate(b, oT_ps, lambda k: ps[k][1][:, 0:P], lambda k: oT[:, k, :], oT_sb)

            def step(pair, s, first):
                b = pair * 2 + s
                if not first:
                    output(b - 1)
                evacuate(b, t1_ps, lambda k: by_head(ps[k][1]), lambda k: grown[:, k, :, :], t1_sb)
                evacuate(b, t1T_ps, lambda k: by_head(ps[k][0]), lambda k: grownT[:, k, :, :], t1T_sb)
                evacuate(b, t2T_ps, lambda k: by_head(ps[k][0]), lambda k: invT[:, k, :, :], t2T_sb)
                evacuate(b, y0_ps, lambda k: ps[k][1][:, 0:2 * D].rearrange("p (s h d) -> p s h d", s=2, d=DA),
                         lambda k: y0[:, k, :, :, :], y0_sb)
                evacuate(b, qk_ps, lambda k: by_head(ps[k][1]), lambda k: resid[:, k, :, :], qk_sb)
                evacuate(b, qtT_ps, lambda k: ps[k][0][:, 0:P], lambda k: qtT[:, k, :], qtT_sb)

            stream(act, step, (output,))

        @block.tensor
        def _(pe):
            pe.sem_inc(out_ps.sem, 2 * NT)
            pe.wait_ge(wo_ready, 1)

            def transpose_output(b):
                for k in range(NT):
                    pe.wait_ge(on_ready.sem, on_ready.made(b, k))
                    pe.transpose(ps[k][1][:, 0:P], o[:, k, :, :], g.ident[:, :]).then_inc(oT_ps.sem, 1)

            def project(b):
                for k in range(NT):
                    pe.wait_ge(oT_sb.sem, oT_sb.made(b, k))
                    pe.matmul(ps[k][0][:, 0:P], oT[:, k, :], wo[:, :], start=True, stop=True).then_inc(out_ps.sem, 1)

            def step(pair, s, first):
                b = pair * 2 + s
                tiles = [TilePack(pack, s, k) for k in range(NT)]

                def heads(bank, k, lhsT, rhs, ready):
                    for h in range(HA):
                        last = pe.matmul(bank(h), lhsT(h), rhs(h), start=True, stop=True)
                    last.then_inc(ready.sem, 1)

                full = lambda k, j: lambda h: by_head(ps[k][j])[:, h, :]
                pair_of = lambda k, j: lambda h: ps[k][j][:, 0:2 * D].rearrange("p (s h d) -> p s h d", s=2, d=DA)[:, :, h, :]
                for k in range(NT):
                    pe.wait_ge(pack_in[s][k], 16 * pair + 16)
                    if k == 0:
                        pe.wait_ge(inv_in[s], (16 * GB) * pair + 16 * GB)
                    if not first:
                        pe.wait_ge(o_ready.sem, o_ready.made(b - 1, k))
                    heads(full(k, 0), k, lambda h: tiles[k].lt[:, h, :], lambda h: inv[:, s, k, h, :], lt0_ps)
                if not first:
                    transpose_output(b - 1)
                for k in range(NT):
                    pe.wait_ge(invT_ready.sem, invT_ready.made(b, k))
                    pe.wait_ge(r0_ready.sem, r0_ready.made(b, k))
                    if not first:
                        pe.wait_ge(oT_sb.sem, oT_sb.made(b - 1, k))
                    heads(full(k, 1), k, lambda h: invT[:, k, h, :], lambda h: resid[:, k, h, :], t1_ps)
                if not first:
                    project(b - 1)
                for k in range(NT):
                    if not first:
                        pe.wait_ge(added.sem, added.made(b - 1, k))
                    heads(full(k, 0), k, lambda h: resid[:, k, h, :], lambda h: invT[:, k, h, :], t1T_ps)
                for k in range(NT):
                    pe.wait_ge(t1_sb.sem, t1_sb.made(b, k))
                    heads(full(k, 1), k, lambda h: tiles[k].lt[:, h, :], lambda h: grown[:, k, h, :], lt1_ps)
                for k in range(NT):
                    pe.wait_ge(t1T_sb.sem, t1T_sb.made(b, k))
                    pe.wait_ge(r1_ready.sem, r1_ready.made(b, k))
                    heads(full(k, 0), k, lambda h: resid[:, k, h, :], lambda h: grownT[:, k, h, :], t2T_ps)
                for k in range(NT):
                    pe.wait_ge(t2T_sb.sem, t2T_sb.made(b, k))
                    heads(pair_of(k, 1), k, lambda h: invT[:, k, h, :], lambda h: tiles[k].rhs[:, :, h, :], y0_ps)
                for k in range(NT):
                    pe.wait_ge(y0_sb.sem, y0_sb.made(b, k))
                    heads(pair_of(k, 0), k, lambda h: tiles[k].lt[:, h, :], lambda h: y0[:, k, :, h, :], ly_ps)
                for k in range(NT):
                    pe.wait_ge(q_heads_ready.sem, q_heads_ready.made(b, k))
                    pe.matmul(ps[k][1][:, :], tiles[k].kT, q_heads[:, k, :, :], start=True, stop=True).then_inc(qk_ps.sem, 1)
                for k in range(NT):
                    pe.wait_ge(err_ready.sem, err_ready.made(b, k))
                    pe.wait_ge(qk_sb.sem, qk_sb.made(b, k))
                    heads(pair_of(k, 1), k, lambda h: invT[:, k, h, :], lambda h: err[:, k, :, h, :], dy_ps)
                for k in range(NT):
                    pe.wait_ge(uw_ready.sem, uw_ready.made(b, k))
                    pe.wait_ge(qk_masked.sem, qk_masked.made(b, k))
                    heads(pair_of(k, 0), k, lambda h: resid[:, k, h, :], lambda h: uw[:, k, :, h, :], muw_ps)
                for k in range(NT):
                    pe.matmul(ps[k][1][:, 0:P], uw[:, k, 1, :, :], tiles[k].k, start=True, stop=True)
                    pe.matmul(ps[k][1][:, P:2 * P], tiles[k].k, uw[:, k, 0, :, :], start=True, stop=True).then_inc(fg_ps.sem, 1)
                for k in range(NT):
                    pe.wait_ge(qt_ready.sem, qt_ready.made(b, k))
                    pe.transpose(ps[k][0][:, 0:P], qt[:, k, :, :], g.ident[:, :]).then_inc(qtT_ps.sem, 1)
                for k in range(1, NT):
                    pe.wait_ge(state_ready.sem, state_ready.made(b, k - 1))
                    if k < NT - 1:
                        pe.wait_ge(f_ready.sem, f_ready.made(b, k))
                        pe.matmul(ps[k][1][:, 0:P], fg[:, k, 0, :], state[:, k, :], start=True, stop=True).then_inc(state_ps.sem, 1)
                    pe.wait_ge(qtT_sb.sem, qtT_sb.made(b, k))
                    pe.matmul(ps[k][0][:, 0:P], qtT[:, k, :], state[:, k, :], start=True, stop=True).then_inc(cross_ps.sem, 1)

            stream(pe, step, (transpose_output, project))


class Attention:

    def __init__(self, name, heads, width, pairs):
        self.name, self.heads, self.width, self.pairs = name, heads, width, pairs
        self.parts = 1 + max(max(p) for p in pairs)
        self.groups = heads // HG
        self.total = B * self.groups
        self.scale = float(width) ** -0.5
        assert len(pairs) * width <= SHIFT_ROW and HG * HEAD_ROWS == P and width <= HEAD_ROWS


HG = 4
HEAD_ROWS = P // HG
SHIFT_ROW = 96
RING = 4
EXP_LAG, PV_LAG, OUT_LAG = 2, 3, 4
TILES = HG * NT
L0_ATT = Attention("l0", 16, 8, ((0, 0), (0, 1), (0, 2), (1, 0), (1, 1), (2, 0)))
L1_ATT = Attention("l1", 32, 32, ((0, 0), (0, 1), (1, 0)))


def attention(nc, g, a, scratch, w_out, out, addend):
    W, M, U = a.width, a.total, a.groups
    with ExitStack() as ctx:
        sb = lambda name, shape, dt=F32: ctx.enter_context(nc.sbuf_tensor(f"{name}_{a.name}", shape, dt))
        sem = phase_semaphores(nc, ctx, "_" + a.name)
        pb = lambda name: ctx.enter_context(nc.psum_tensor(f"{name}_{a.name}", [P, N], F32))
        max_ps, exp_ps = [pb(f"max{i}") for i in range(2)], [pb(f"exp{i}") for i in range(3)]
        pv_bank, sums_bank, y_bank = pb("pv_bank"), pb("sums_bank"), pb("y_bank")
        qs, ks = sb("q_stack", [P, RING, HG, N], F16), sb("k_stack", [P, RING, HG, N], F16)
        vs = sb("v_ring", [P, RING, NT, HG, W])
        probs = sb("probs", [P, 2, HG, NT, N])
        part_sums = sb("part_sums", [P, 2, HG, 2, N])
        ones = sb("ones", [P, HEAD_ROWS])
        maxima = sb("maxima", [P, 2, NT, HG])
        shift = sb("shift", [TILES, 2, P], F16)
        sums, oT_raw, oT = sb("sums", [P, N]), sb("oT_raw", [P, N]), sb("oT", [P, 2, N])
        inv_sums, inv_rows = sb("inv_sums", [P, NT, HG]), sb("inv_rows", [P, NT, HG, HEAD_ROWS])

        cleared, shift_rows = sem("cleared"), sem("shift_rows")
        loaded = [sem(f"loaded{s}") for s in range(RING)]
        v_loaded = [sem(f"v_loaded{s}") for s in range(RING)]
        shifted = [sem(f"shifted{s}") for s in range(RING)]
        n_loads = 2 * len(a.pairs)
        made = lambda name, per=1: Product(sem(name), per)
        max_tile = made("max_tile", TILES)
        max_taken = made("max_taken", TILES)
        maxT_ps, shift_ready = made("maxT_ps"), made("shift_ready")
        score_tile = made("score_tile", TILES)
        prob_tile = made("prob_tile", TILES)
        pair_sum, key_sum, key_sum2 = made("pair_sum", HG), made("key_sum", HG // 2), made("key_sum2", HG // 2)
        sums_ps, sums_sb, sumsT_ps = made("sums_ps"), made("sums_sb"), made("sumsT_ps")
        inv_ready, inv_rows_ready, inv_ps = made("inv_ready"), made("inv_rows_ready"), made("inv_ps")
        pv_ps, pv_sb, oT_ready, y_ps, y_taken = made("pv_ps"), made("pv_sb"), made("oT_ready"), made("y_ps"), made("y_taken")

        def exists(turn, s, lag):
            return not isinstance(turn, int) or 0 <= turn * U + s - lag < M

        def stream(eng, step):
            for s in range(U):
                step(0, s)
            with eng.Fori(1, B) as turn:
                for s in range(U):
                    step(turn, s)
            for s in range(OUT_LAG):
                step(B, s)

        def nth(turn, s, unit):
            return (turn * (U // RING) + s // RING + 1) * unit

        def exp_bank(s, at):
            return (at + s % 2) % 3

        block = ctx.enter_context(nc.Block())

        @block.sync
        def _(sp):
            sp.wait_ge(cleared, 2)

            def load(turn, s):
                slot = s % RING
                if exists(turn, s, RING):
                    wait_ge(sp, score_tile.sem, score_tile.made(turn * U + s - RING, TILES - 1), g.passed)
                for r, parts in enumerate(a.pairs):
                    for side, stack in enumerate((qs, ks)):
                        sp.dma_start(stack[r * W:(r + 1) * W, slot, :, :],
                                     scratch.qk[side, parts[side], turn * U + s].rearrange("h d t -> d h t")).then_inc(loaded[slot], 16)

            def step(turn, s, more=True):
                if more:
                    load(turn, s + 1)
                if exists(turn, s, 0):
                    if exists(turn, s, RING):
                        wait_ge(sp, pv_ps.sem, pv_ps.made(turn * U + s - RING, 0), g.passed)
                    sp.dma_start(vs[:, s % RING, :, :, :], scratch.v[turn * U + s]).then_inc(v_loaded[s % RING], 16)
                if exists(turn, s, 1):
                    wait_ge(sp, shift_ready.sem, shift_ready.made(turn * U + s - 1, 0), g.passed)
                    for k in range(NT):
                        sp.dma_start(qs[SHIFT_ROW:SHIFT_ROW + HG, (s - 1) % RING, :, k * P:(k + 1) * P],
                                     shift[k * HG:(k + 1) * HG, (s - 1) % 2, :].unsqueeze(1).broadcast_to([HG, HG, P])
                                     ).then_inc(shifted[(s - 1) % RING], 16)

            load(0, 0)
            for s in range(U):
                step(0, s)
            with sp.Fori(1, B - 1) as turn:
                for s in range(U):
                    step(turn, s)
            for s in range(U):
                step(B - 1, s, s + 1 < U)
            step(B, 0, False)

        @block.gpsimd
        def _(pool):
            rows = ks[SHIFT_ROW:SHIFT_ROW + HG, :, :, :]
            pool.memset(rows, 0.0).then_inc(shift_rows, 1)
            pool.wait_ge(shift_rows, 1)
            pool.affine_select(out=rows, in_=rows, compare_op=ALU.not_equal, fill=1.0, base=0,
                               pattern=[[0, RING], [-1, HG], [0, N]], channel_multiplier=1).then_inc(cleared, 1)

            def step(turn, s):
                if not exists(turn, s, EXP_LAG):
                    return
                m, i = turn * U + s - EXP_LAG, (s - EXP_LAG) % 2
                for h in range(HG):
                    pool.wait_ge(prob_tile.sem, prob_tile.made(m, h * NT + NT - 1))
                    pool.tensor_tensor(part_sums[:, i, h, :, :], probs[:, i, h, 0:2, :], probs[:, i, h, 2:4, :],
                                       ALU.add).then_inc(pair_sum.sem, 1)
                    pool.wait_ge(pair_sum.sem, pair_sum.made(m, h))
                    if h < HG // 2:
                        both = part_sums[:, i, h, :, :]
                        pool.tensor_tensor(both[:, 0, :], both[:, 0, :], both[:, 1, :], ALU.add).then_inc(key_sum.sem, 1)
                        pool.wait_ge(key_sum.sem, key_sum.made(m, h))

            stream(pool, step)

        @block.vector
        def _(dve):
            if len(a.pairs) * W < SHIFT_ROW:
                dve.memset(qs[0:SHIFT_ROW, :, :, :], 0.0)
                dve.memset(ks[0:SHIFT_ROW, :, :, :], 0.0)
            dve.memset(ones[:, :], 1.0)
            dve.sem_inc(y_taken.sem, 1)
            dve.memset(pv_bank[:, :], 0.0).then_inc(cleared, 1)

            def step(turn, s):
                n = turn * U + s
                for at in range(TILES):
                    if exists(turn, s, 0):
                        dve.wait_ge(max_tile.sem, max_tile.made(n, at))
                        dve.reduce_max(maxima[:, s % 2, at % NT, at // NT:at // NT + 1], max_ps[at % 2][:, :],
                                       AX).then_inc(max_taken.sem, 1)
                    if at in (2, 5) and exists(turn, s, PV_LAG):
                        h = HG // 2 + at // 5
                        dve.wait_ge(pair_sum.sem, pair_sum.made(n - PV_LAG, h))
                        both = part_sums[:, (s - PV_LAG) % 2, h, :, :]
                        dve.tensor_tensor(both[:, 0, :], both[:, 0, :], both[:, 1, :], ALU.add).then_inc(key_sum2.sem, 1)
                    if at == 11 and exists(turn, s, PV_LAG):
                        dve.wait_ge(sumsT_ps.sem, sumsT_ps.made(n - PV_LAG, 0))
                        by_token = sums_bank[:, :].rearrange("p (k h r) -> p k h r", k=NT, h=HG)
                        dve.reciprocal(inv_sums[:, :, :], by_token[:, :, :, 0]).then_inc(inv_ready.sem, 1)
                        dve.wait_ge(inv_ready.sem, inv_ready.made(n - PV_LAG, 0))
                        dve.tensor_copy(inv_rows[:, :, :, :], bc(inv_sums[:, :, :], HEAD_ROWS)).then_inc(inv_rows_ready.sem, 1)
                    if at == 0 and exists(turn, s, OUT_LAG):
                        dve.wait_ge(inv_ps.sem, inv_ps.made(n - OUT_LAG, 0))
                        dve.wait_ge(pv_sb.sem, pv_sb.made(n - OUT_LAG, 0))
                        dve.tensor_tensor(oT[:, s % 2, :], oT_raw[:, :], sums_bank[:, :], ALU.mult).then_inc(oT_ready.sem, 1)
                    if at == TILES - 1 and s == OUT_LAG - 1 and exists(turn, s, OUT_LAG):
                        dve.wait_ge(y_ps.sem, y_ps.made(n - OUT_LAG, 0))
                        tiles = bass.ds((turn - 1) * NT, NT)
                        dve.tensor_tensor(out[:, tiles, :], y_bank[:, :].rearrange("p (k d) -> p k d", k=NT), addend(tiles),
                                          ALU.add).then_inc(y_taken.sem, 1)

            stream(dve, step)

        @block.scalar
        def _(act):
            def step(turn, s):
                n = turn * U + s
                for at in range(TILES):
                    if exists(turn, s, EXP_LAG):
                        m, i = n - EXP_LAG, (s - EXP_LAG) % 2
                        act.wait_ge(score_tile.sem, score_tile.made(m, at))
                        if at == 0 and exists(turn, s, EXP_LAG + 2):
                            act.wait_ge(pv_ps.sem, pv_ps.made(m - 2, 0))
                        act.activation(probs[:, i, at // NT, at % NT, :], exp_ps[exp_bank(s, at)][:, :], ACT.Exp,
                                       scale=a.scale).then_inc(prob_tile.sem, 1)
                    if at == 8 and exists(turn, s, PV_LAG):
                        act.wait_ge(sums_ps.sem, sums_ps.made(n - PV_LAG, 0))
                        act.copy(sums[:, :], sums_bank[:, :]).then_inc(sums_sb.sem, 1)
                    if at == 13 and exists(turn, s, PV_LAG):
                        act.wait_ge(pv_ps.sem, pv_ps.made(n - PV_LAG, 0))
                        if exists(turn, s, OUT_LAG):
                            act.wait_ge(oT_ready.sem, oT_ready.made(n - OUT_LAG, 0))
                        act.copy(oT_raw[:, :], pv_bank[:, :]).then_inc(pv_sb.sem, 1)
                    if at == 4 and exists(turn, s, 1):
                        act.wait_ge(maxT_ps.sem, maxT_ps.made(n - 1, 0))
                        act.activation(shift[:, (s - 1) % 2, :], sums_bank[0:TILES, 0:P], ACT.Copy,
                                       scale=-1.0).then_inc(shift_ready.sem, 1)

            stream(act, step)

        @block.tensor
        def _(pe):
            pe.wait_ge(cleared, 2)

            def step(turn, s):
                n = turn * U + s
                for at in range(TILES):
                    h, k = at // NT, at % NT
                    if exists(turn, s, 0):
                        if at == 0:
                            pe.wait_ge(loaded[s % RING], nth(turn, s, 16 * n_loads))
                        if at >= 2:
                            pe.wait_ge(max_taken.sem, max_taken.made(n, at - 2))
                        elif exists(turn, s, 1):
                            pe.wait_ge(max_taken.sem, max_taken.made(n - 1, TILES + at - 2))
                        pe.matmul(max_ps[at % 2][:, :], qs[0:SHIFT_ROW, s % RING, h, k * P:(k + 1) * P],
                                  ks[0:SHIFT_ROW, s % RING, h, :], start=True, stop=True).then_inc(max_tile.sem, 1)
                    if exists(turn, s, EXP_LAG):
                        m, slot = n - EXP_LAG, (s - EXP_LAG) % RING
                        if at == 0:
                            pe.wait_ge(shifted[slot], nth(turn, s - EXP_LAG, 16 * NT))
                        before = [t for t in range(at) if exp_bank(s, t) == exp_bank(s, at)]
                        if before:
                            pe.wait_ge(prob_tile.sem, prob_tile.made(m, before[-1]))
                        elif exists(turn, s, EXP_LAG + 1):
                            before = [t for t in range(TILES) if exp_bank(s - 1, t) == exp_bank(s, at)]
                            pe.wait_ge(prob_tile.sem, prob_tile.made(m - 1, before[-1]))
                        pe.matmul(exp_ps[exp_bank(s, at)][:, :], ks[0:SHIFT_ROW + HG, slot, h, k * P:(k + 1) * P],
                                  qs[0:SHIFT_ROW + HG, slot, h, :], start=True, stop=True).then_inc(score_tile.sem, 1)
                    if at == 3 and exists(turn, s, 1):
                        pe.wait_ge(max_taken.sem, max_taken.made(n - 1, TILES - 1))
                        if exists(turn, s, OUT_LAG):
                            pe.wait_ge(oT_ready.sem, oT_ready.made(n - OUT_LAG, 0))
                        pe.transpose(sums_bank[0:TILES, 0:P], maxima[:, (s - 1) % 2, :, :], g.ident[:, :]).then_inc(maxT_ps.sem, 1)
                    if at in (4, 15) and exists(turn, s, OUT_LAG):
                        group = (s - OUT_LAG) % U
                        if at == 4:
                            pe.wait_ge(oT_ready.sem, oT_ready.made(n - OUT_LAG, 0))
                            if group == 0:
                                pe.wait_ge(y_taken.sem, turn + (s - OUT_LAG) // U + 1)
                        for j in ((0, 1) if at == 4 else (2, 3)):
                            ins = pe.matmul(y_bank[:, j * D:(j + 1) * D], oT[:, s % 2, j * P:(j + 1) * P], w_out[:, group, :],
                                            start=(group == 0 and j == 0), stop=(group == U - 1 and j == NT - 1))
                        if at == 15:
                            ins.then_inc(y_ps.sem, 1)
                    if not exists(turn, s, PV_LAG):
                        continue
                    m, i, slot = n - PV_LAG, (s - PV_LAG) % 2, (s - PV_LAG) % RING
                    if at in (1, 5, 9, 12):
                        j = at // 4 if at < 12 else 3
                        if j == 0:
                            pe.wait_ge(v_loaded[slot], nth(turn, s - PV_LAG, 16))
                            pe.wait_ge(prob_tile.sem, prob_tile.made(m, TILES - 1))
                            if exists(turn, s, OUT_LAG):
                                pe.wait_ge(pv_sb.sem, pv_sb.made(m - 1, 0))
                        for hh in range(HG):
                            ins = pe.matmul(pv_bank[hh * HEAD_ROWS:hh * HEAD_ROWS + W, :], vs[:, slot, j, hh, :],
                                            probs[:, i, hh, j, :], start=(j == 0), stop=(j == NT - 1))
                        if j == NT - 1:
                            ins.then_inc(pv_ps.sem, 1)
                    if at == 7:
                        pe.wait_ge(key_sum.sem, key_sum.made(m, HG // 2 - 1))
                        pe.wait_ge(key_sum2.sem, key_sum2.made(m, HG // 2 - 1))
                        if exists(turn, s, 1):
                            pe.wait_ge(shift_ready.sem, shift_ready.made(n - 1, 0))
                        for hh in range(HG):
                            ins = pe.matmul(sums_bank[hh * HEAD_ROWS:(hh + 1) * HEAD_ROWS, :], ones[:, :], part_sums[:, i, hh, 0, :],
                                            start=True, stop=True)
                        ins.then_inc(sums_ps.sem, 1)
                    if at == 10:
                        pe.wait_ge(sums_sb.sem, sums_sb.made(m, 0))
                        for j in range(NT):
                            ins = pe.transpose(sums_bank[:, j * P:(j + 1) * P], sums[:, j * P:(j + 1) * P], g.ident[:, :])
                        ins.then_inc(sumsT_ps.sem, 1)
                    if at == 14:
                        pe.wait_ge(inv_rows_ready.sem, inv_rows_ready.made(m, 0))
                        for j in range(NT):
                            ins = pe.transpose(sums_bank[:, j * P:(j + 1) * P], inv_rows[:, j, :, :].rearrange("p h r -> p (h r)"),
                                               g.ident[:, :])
                        ins.then_inc(inv_ps.sem, 1)

            stream(pe, step)


def prep_l0(nc, g, ins, scratch):
    a = L0_ATT
    with ExitStack() as ctx:
        sb = lambda name, shape, dt=F32: ctx.enter_context(nc.sbuf_tensor(name + "_c", shape, dt))
        sem = phase_semaphores(nc, ctx, "_c")
        pb = lambda name: ctx.enter_context(nc.psum_tensor(name + "_ps_c", [P, N], F32))
        znT_bank, qk_bank, v_bank = pb("znT"), [pb("q"), pb("k")], pb("v")
        w = sb("w", [P, 3, D])
        col = sb("col", [P, 4])
        bv = sb("bv", [P, D])
        stats, mv, var_eps, rstd = sb("stats", [P, NT, 6]), sb("mv", [P, NT, 2]), sb("var_eps", [P, 2, NT]), sb("rstd", [P, 2, NT])
        zn, hT = sb("zn", [P, NT, D]), sb("hT", [P, N])
        qk = sb("qk", [P, 2, N])
        parts = sb("parts", [P, 2, 3, N], F16)
        v = sb("v", [P, a.groups, NT, HG, a.width])
        bo, wo_filled = sb("bo", [P, D]), sem("wo_filled")
        bo_added = Product(sem("bo_added"), NT)

        own, own_z, w_loaded = sem("own"), sem("own_z"), sem("w_loaded")
        made = lambda name, per=1, credit=0, unit=1: Product(sem(name), per, credit, unit)
        moments, rstd_ready = made("moments", 2), made("rstd_ready", 2)
        zn_ready, znT_ps, hT_ready = made("zn_ready", NT), made("znT_ps", 1), made("hT_ready", 1)
        qk_ps, v_ps = made("qk_ps", 2), made("v_ps", 1)
        qk_sb, part0, rest, part1, part2 = made("qk_sb", 2), made("part0"), made("rest"), made("part1"), made("part2")
        v_ready = made("v_ready", NT, NT)
        parts_stored, v_stored = made("parts_stored", 2, 2, 16), made("v_stored", 1, 1, 16)
        block = ctx.enter_context(nc.Block())

        @block.sync
        def _(sp):
            for n, name in enumerate(("wq", "wk", "wv")):
                sp.dma_start(w[:, n, :], ins["L0_ffn_" + name]).then_inc(w_loaded, 16)
            for n, name in enumerate(("ln1_g", "ln1_b", "bq", "bk")):
                sp.dma_start(col[:, n:n + 1], ins["L0_ffn_" + name].rearrange("(p a) -> p a", a=1)).then_inc(w_loaded, 16)
            sp.dma_start(bv[:, :], ins["L0_ffn_bv"].partition_broadcast(P)).then_inc(w_loaded, 16)
            sp.dma_start(bo[:, :], ins["L0_ffn_bo"].partition_broadcast(P)).then_inc(w_loaded, 16)
            sp.wait_ge(wo_filled, 1)
            wo = ins["L0_ffn_wo"].rearrange("(g h d) c -> h d g c", h=HG, d=a.width)
            for h in range(HG):
                sp.dma_start(g.wo[h * HEAD_ROWS:h * HEAD_ROWS + a.width, :, :], wo[h]).then_inc(wo_filled, 16)
            sp.sem_inc(parts_stored.sem, 32)
            sp.sem_inc(v_stored.sem, 16)
            with sp.Fori(0, B) as b:
                sp.wait_ge(v_ready.sem, v_ready.made(b, NT - 1))
                sp.dma_start(scratch.v.rearrange("(b g) p k h c -> b p g (k h c)", b=B)[b],
                             v[:, :, :, :, :].rearrange("p g k h c -> p g (k h c)")).then_inc(v_stored.sem, 16)
                wait_ge(sp, part2.sem, part2.made(b, 0), g.passed)
                for s in range(2):
                    sp.dma_start(scratch.qk[s].rearrange("r (b g) h d t -> b (g h d) r t", b=B)[b],
                                 parts[:, s, :, :]).then_inc(parts_stored.sem, 16)
            sp.wait_ge(wo_filled, 16 * HG + 1)
            sp.wait_ge(v_stored.sem, v_stored.made(B - 1, 0))
            sp.wait_ge(parts_stored.sem, parts_stored.made(B - 1, 1))

        @block.gpsimd
        def _(pool):
            pool.memset(g.wo[:, :, :], 0.0).then_inc(wo_filled, 1)
            pool.wait_ge(w_loaded, 16 * 9)
            with pool.Fori(0, B) as b:
                for i in range(2):
                    pool.wait_ge(moments.sem, moments.made(b, i))
                    pool.tensor_tensor(rstd[:, i, :], var_eps[:, i, :], g.minus_half[:, 0:NT], ALU.pow).then_inc(rstd_ready.sem, 1)
                for k in range(NT):
                    pool.wait_ge(zn_ready.sem, zn_ready.made(b, k))
                    pool.tensor_tensor(g.z[:, b * NT + k, :], g.z[:, b * NT + k, :], bo[:, :], ALU.add).then_inc(bo_added.sem, 1)
                    pool.wait_ge(bo_added.sem, bo_added.made(b, k))

        @block.vector
        def _(dve):
            dve.wait_ge(w_loaded, 16 * 9)
            dve.sem_inc(v_ready.sem, NT)

            def moments_of(rows, me, i):
                for k in range(NT):
                    me.did(dve.bn_stats(stats[:, k, :], rows(k)))
                me.settle(g.passed)
                for k in range(NT):
                    me.did(dve.bn_aggr(mv[:, k, :], stats[:, k, :]))
                me.settle()
                dve.tensor_scalar(var_eps[:, i, :], mv[:, :, 1], LN_EPS, None, ALU.add).then_inc(moments.sem, 1)
                me.close()

            def moments_of_x(b):
                moments_of(lambda k: g.x[:, b * NT + k, :], Own(dve, own, 2 * NT, b), 0)

            def normalise_x(b):
                me = Own(dve, own_z, 3 * NT, b)
                dve.wait_ge(rstd_ready.sem, rstd_ready.made(b, 0))
                for k in range(NT):
                    me.did(dve.tensor_scalar(g.z[:, b * NT + k, :], g.x[:, b * NT + k, :], mv[:, k, 0:1], rstd[:, 0, k:k + 1],
                                             ALU.subtract, ALU.mult))
                me.settle(g.passed)
                moments_of(lambda k: g.z[:, b * NT + k, :], me, 1)

            def normalise_z(b, first=False):
                dve.wait_ge(rstd_ready.sem, rstd_ready.made(b, 1))
                if not first:
                    dve.wait_ge(znT_ps.sem, znT_ps.made(b - 1, 0))
                for k in range(NT):
                    dve.tensor_scalar(zn[:, k, :], g.z[:, b * NT + k, :], mv[:, k, 0:1], rstd[:, 1, k:k + 1],
                                      ALU.subtract, ALU.mult).then_inc(zn_ready.sem, 1)

            def step(b, ahead):
                dve.wait_ge(znT_ps.sem, znT_ps.made(b, 0))
                dve.tensor_scalar(hT[:, :], znT_bank[:, :], col[:, 0:1], col[:, 1:2], ALU.mult, ALU.add).then_inc(hT_ready.sem, 1)
                if ahead:
                    normalise_x(b + 1)
                for s in range(2):
                    dve.wait_ge(qk_ps.sem, qk_ps.made(b, s))
                    dve.tensor_scalar(qk[:, s, :], qk_bank[s][:, :], col[:, 2 + s:3 + s], None, ALU.add).then_inc(qk_sb.sem, 1)
                dve.wait_ge(v_ps.sem, v_ps.made(b, 0))
                dve.wait_ge(v_stored.sem, v_stored.made_before(b, 0))
                for k in range(NT):
                    split = lambda ap: ap.rearrange("p (g h d) -> p g h d", h=HG, d=a.width)
                    dve.tensor_tensor(v[:, :, k, :, :], split(v_bank[:, k * D:(k + 1) * D]), split(bv[:, :]),
                                      ALU.add).then_inc(v_ready.sem, 1)
                if ahead:
                    normalise_z(b + 1)
                dve.wait_ge(part0.sem, part0.made(b, 0))
                dve.tensor_tensor(qk[:, :, :], qk[:, :, :], parts[:, :, 0, :], ALU.subtract).then_inc(rest.sem, 1)
                if ahead > 1:
                    moments_of_x(b + 2)
                dve.wait_ge(part1.sem, part1.made(b, 0))
                dve.tensor_tensor(parts[:, :, 2, :], qk[:, :, :], parts[:, :, 1, :], ALU.subtract).then_inc(part2.sem, 1)

            moments_of_x(0)
            normalise_x(0)
            normalise_z(0, first=True)
            moments_of_x(1)
            with dve.Fori(0, B - 2) as b:
                step(b, 2)
            step(B - 2, 1)
            step(B - 1, 0)

        @block.scalar
        def _(act):
            with act.Fori(0, B) as b:
                act.wait_ge(qk_sb.sem, qk_sb.made(b, 1))
                act.wait_ge(parts_stored.sem, parts_stored.made_before(b, 1))
                act.copy(parts[:, :, 0, :], qk[:, :, :]).then_inc(part0.sem, 1)
                act.wait_ge(rest.sem, rest.made(b, 0))
                act.copy(parts[:, :, 1, :], qk[:, :, :]).then_inc(part1.sem, 1)

        @block.tensor
        def _(pe):
            pe.wait_ge(w_loaded, 16 * 9)

            def transposes(b):
                for k in range(NT):
                    pe.wait_ge(zn_ready.sem, zn_ready.made(b, k))
                    ins = pe.transpose(znT_bank[:, k * P:(k + 1) * P], zn[:, k, :], g.ident[:, :])
                ins.then_inc(znT_ps.sem, 1)

            def projections(b):
                pe.wait_ge(hT_ready.sem, hT_ready.made(b, 0))
                for s in range(2):
                    pe.matmul(qk_bank[s][:, :], w[:, s, :], hT[:, :], start=True, stop=True).then_inc(qk_ps.sem, 1)
                pe.wait_ge(v_ready.sem, v_ready.made_before(b, NT - 1))
                for k in range(NT):
                    ins = pe.matmul(v_bank[:, k * D:(k + 1) * D], hT[:, k * P:(k + 1) * P], w[:, 2, :], start=True, stop=True)
                ins.then_inc(v_ps.sem, 1)

            transposes(0)
            with pe.Fori(0, B - 1) as b:
                projections(b)
                transposes(b + 1)
            projections(B - 1)


E_, F_ = 8, 512
FT = F_ // P


def moe(nc, g, ins):
    M = B * E_
    with ExitStack() as ctx:
        sb = lambda name, shape, dt=F32: ctx.enter_context(nc.sbuf_tensor(name + "_e", shape, dt))
        sem = phase_semaphores(nc, ctx, "_e")
        pb = lambda name: ctx.enter_context(nc.psum_tensor(name + "_ps_e", [P, N], F32))
        mid_bank, y_bank = [pb(f"mid{i}") for i in range(4)], [pb(f"y{i}") for i in range(2)]
        znT_bank, gate_bank = pb("znT"), pb("gate")
        w1, w2, b1 = sb("w1", [P, E_, F_]), sb("w2", [P, E_, FT, D]), sb("b1", [P, E_, FT])
        b1_rows = sb("b1_rows", [E_ * FT, P])
        gate_w, gate_b, b2, col = sb("gate_w", [P, E_]), sb("gate_b", [P, E_]), sb("b2", [E_, D]), sb("col", [P, 2])
        rank, ranks_built = sb("rank", [P, NT, E_]), sem("ranks_built")
        stats, mv, var_eps, rstd = sb("stats", [P, NT, 6]), sb("mv", [P, NT, 2]), sb("var_eps", [P, NT]), sb("rstd", [P, NT])
        zn, hT, hT_all = sb("zn", [P, NT, D]), sb("hT", [P, N]), sb("hT_all", [P, B, N])
        logits, best = sb("logits", [P, NT, E_]), sb("best", [P, NT])
        choice, choiceT, choice_all = sb("choice", [P, NT, E_]), sb("choiceT", [E_, N]), sb("choice_all", [P, T, E_])
        mid = sb("mid", [P, 2, FT, N])
        own, w_loaded, b1_loaded, experts_in, b1T_ps, b1_kept = (
            sem("own"), sem("w_loaded"), sem("b1_loaded"), sem("experts_in"), sem("b1T_ps"), sem("b1_kept"))
        made = lambda name, per=1, credit=0: Product(sem(name), per, credit)
        moments, rstd_ready, zn_ready = made("moments"), made("rstd_ready"), made("zn_ready", NT)
        znT_ps, hT_ready = made("znT_ps"), made("hT_ready")
        hT_kept = made("hT_kept", 1, 1)
        logits_ps, chosen, b2_ps = made("logits_ps"), made("chosen"), made("b2_ps")
        choiceT_ps, choiceT_sb = made("choiceT_ps"), made("choiceT_sb")
        x_added = made("x_added", NT, NT)
        mid_ps, mid_sb, y_ps, y_added = made("mid_ps", FT), made("mid_sb", FT), made("y_ps"), made("y_added", NT)

        def stream(eng, prepare, expert, prepare_first=False):
            prepare(0, range(E_))

            def batch(b, ahead):
                for e in range(E_):
                    if ahead and prepare_first:
                        prepare(b + 1, [e])
                    expert(b, e)
                    if ahead and not prepare_first:
                        prepare(b + 1, [e])

            batch(0, True)
            with eng.Fori(1, B - 1) as b:
                batch(b, True)
            batch(B - 1, False)

        block = ctx.enter_context(nc.Block())

        @block.sync
        def _(sp):
            sp.dma_start(gate_w[:, :], ins["L0_ffn_gate_w"]).then_inc(w_loaded, 16)
            sp.dma_start(gate_b[:, :], ins["L0_ffn_gate_b"].partition_broadcast(P)).then_inc(w_loaded, 16)
            sp.dma_start(b2[:, :], ins["L0_ffn_b2"]).then_inc(w_loaded, 16)
            for n, name in enumerate(("ln2_g", "ln2_b")):
                sp.dma_start(col[:, n:n + 1], ins["L0_ffn_" + name].rearrange("(p a) -> p a", a=1)).then_inc(w_loaded, 16)
            sp.dma_start(b1_rows[:, :], ins["L0_ffn_b1"].rearrange("e (f p) -> (e f) p", p=P)).then_inc(b1_loaded, 16)
            sp.dma_start(w1[:, :, :], ins["L0_ffn_w1"].rearrange("e p f -> p e f")).then_inc(experts_in, 16)
            sp.dma_start(w2[:, :, :, :], ins["L0_ffn_w2"].rearrange("e (f p) d -> p e f d", p=P)).then_inc(experts_in, 16)

        @block.gpsimd
        def _(pool):
            for e in range(E_):
                pool.memset(rank[:, :, e:e + 1], float(E_ - e)).then_inc(ranks_built, 1)
                pool.wait_ge(ranks_built, e + 1)
            with pool.Fori(0, B) as b:
                pool.wait_ge(moments.sem, moments.made(b, 0))
                pool.tensor_tensor(rstd[:, :], var_eps[:, :], g.minus_half[:, 0:NT], ALU.pow).then_inc(rstd_ready.sem, 1)

        @block.vector
        def _(dve):
            dve.wait_ge(w_loaded, 16 * 5)
            dve.wait_ge(ranks_built, E_)
            dve.sem_inc(x_added.sem, NT)
            mine = [None]

            def prepare(b, parts):
                if 0 in parts:
                    me = mine[0] = Own(dve, own, 3 * NT + 5, b)
                    for k in range(NT):
                        me.did(dve.bn_stats(stats[:, k, :], g.z[:, b * NT + k, :]))
                    me.settle(g.passed)
                    for k in range(NT):
                        me.did(dve.bn_aggr(mv[:, k, :], stats[:, k, :]))
                    me.settle()
                    dve.tensor_scalar(var_eps[:, :], mv[:, :, 1], LN_EPS, None, ALU.add).then_inc(moments.sem, 1)
                me = mine[0]
                if 1 in parts:
                    dve.wait_ge(rstd_ready.sem, rstd_ready.made(b, 0))
                    for k in range(NT):
                        dve.tensor_scalar(zn[:, k, :], g.z[:, b * NT + k, :], mv[:, k, 0:1], rstd[:, k:k + 1],
                                          ALU.subtract, ALU.mult).then_inc(zn_ready.sem, 1)
                    for k in range(NT):
                        me.did(dve.tensor_tensor(g.x[:, b * NT + k, :], g.x[:, b * NT + k, :], g.z[:, b * NT + k, :], ALU.add))
                if 2 in parts:
                    dve.wait_ge(znT_ps.sem, znT_ps.made(b, 0))
                    dve.wait_ge(hT_kept.sem, hT_kept.made_before(b, 0))
                    dve.tensor_scalar(hT[:, :], znT_bank[:, :], col[:, 0:1], col[:, 1:2], ALU.mult, ALU.add).then_inc(hT_ready.sem, 1)
                if 3 in parts:
                    dve.wait_ge(logits_ps.sem, logits_ps.made(b, 0))
                    gate_b4 = gate_b[:, :].unsqueeze(1).broadcast_to([P, NT, E_])
                    logits_ps4 = gate_bank[:, 0:NT * E_].rearrange("p (k e) -> p k e", k=NT)
                    me.did(dve.tensor_tensor(logits[:, :, :], logits_ps4, gate_b4, ALU.add))
                    me.settle()
                    me.did(dve.tensor_reduce(best[:, :], logits[:, :, :], AX, ALU.max))
                    me.settle()
                    me.did(dve.tensor_tensor(logits[:, :, :], logits[:, :, :], bc(best[:, :], E_), ALU.is_equal))
                    me.settle()
                    me.did(dve.tensor_tensor(logits[:, :, :], logits[:, :, :], rank[:, :, :], ALU.mult))
                    me.settle()
                    me.did(dve.tensor_reduce(best[:, :], logits[:, :, :], AX, ALU.max))
                    me.settle()
                    dve.tensor_tensor(choice_all[:, bass.ds(b * NT, NT), :], logits[:, :, :], bc(best[:, :], E_), ALU.is_equal)
                    dve.tensor_tensor(choice[:, :, :], logits[:, :, :], bc(best[:, :], E_), ALU.is_equal).then_inc(chosen.sem, 1)
                    me.close()
                if 4 in parts:
                    dve.wait_ge(choiceT_ps.sem, choiceT_ps.made(b, 0))
                    dve.tensor_copy(choiceT[:, :], gate_bank[0:E_, :]).then_inc(choiceT_sb.sem, 1)
                if 5 in parts:
                    dve.wait_ge(b2_ps.sem, b2_ps.made(b, 0))
                    for k in range(NT):
                        dve.tensor_tensor(g.x[:, b * NT + k, :], g.x[:, b * NT + k, :], gate_bank[:, k * D:(k + 1) * D],
                                          ALU.add).then_inc(x_added.sem, 1)

            def expert(b, e):
                n = b * E_ + e
                dve.wait_ge(y_ps.sem, y_ps.made(n, 0))
                if e == 0:
                    dve.wait_ge(chosen.sem, chosen.made(b, 0))
                    dve.wait_ge(x_added.sem, x_added.made(b, NT - 1))
                for k in range(NT):
                    if e:
                        dve.wait_ge(y_added.sem, y_added.made(n - 1, k))
                    dve.scalar_tensor_tensor(out=g.x[:, b * NT + k, :], in0=y_bank[e % 2][:, k * D:(k + 1) * D],
                                             scalar=choice_all[:, b * NT + k, e:e + 1], in1=g.x[:, b * NT + k, :],
                                             op0=ALU.mult, op1=ALU.add).then_inc(y_added.sem, 1)

            stream(dve, prepare, expert, prepare_first=True)

        @block.scalar
        def _(act):
            act.sem_inc(hT_kept.sem, 1)
            act.wait_ge(b1T_ps, 1)
            act.copy(b1[:, :, :], gate_bank[:, 0:E_ * FT].rearrange("p (e f) -> p e f", e=E_)).then_inc(b1_kept, 1)

            def prepare(b, parts):
                if 3 in parts:
                    act.wait_ge(hT_ready.sem, hT_ready.made(b, 0))
                    act.copy(hT_all[:, b, :], hT[:, :]).then_inc(hT_kept.sem, 1)

            def expert(b, e):
                n = b * E_ + e
                for f in range(FT):
                    act.wait_ge(mid_ps.sem, mid_ps.made(n, f))
                    if f == 0 and (e >= 2 or not isinstance(b, int) or b):
                        act.wait_ge(y_ps.sem, y_ps.made(n - 2, 0))
                    if f == 0 and e == 0 and isinstance(b, int) and b == 0:
                        act.wait_ge(b1_kept, 1)
                    act.activation(mid[:, e % 2, f, :], mid_bank[f][:, :], ACT.Relu, bias=b1[:, e, f:f + 1]).then_inc(mid_sb.sem, 1)

            stream(act, prepare, expert)

        @block.tensor
        def _(pe):
            pe.wait_ge(b1_loaded, 16)
            pe.transpose(gate_bank[:, 0:E_ * FT], b1_rows[:, :], g.ident[0:E_ * FT, 0:E_ * FT]).then_inc(b1T_ps, 1)
            pe.wait_ge(w_loaded, 16 * 5)
            pe.wait_ge(b1_kept, 1)

            def prepare(b, parts):
                if 2 in parts:
                    for k in range(NT):
                        pe.wait_ge(zn_ready.sem, zn_ready.made(b, k))
                        ins_ = pe.transpose(znT_bank[:, k * P:(k + 1) * P], zn[:, k, :], g.ident[:, :])
                    ins_.then_inc(znT_ps.sem, 1)
                if 3 in parts:
                    pe.wait_ge(hT_ready.sem, hT_ready.made(b, 0))
                    pe.wait_ge(x_added.sem, x_added.made_before(b, NT - 1))
                    for k in range(NT):
                        ins_ = pe.matmul(gate_bank[:, k * E_:(k + 1) * E_], hT[:, k * P:(k + 1) * P], gate_w[:, :], start=True, stop=True)
                    ins_.then_inc(logits_ps.sem, 1)
                if 4 in parts:
                    pe.wait_ge(chosen.sem, chosen.made(b, 0))
                    for k in range(NT):
                        ins_ = pe.transpose(gate_bank[0:E_, k * P:(k + 1) * P], choice[:, k, :], g.ident[:, :])
                    ins_.then_inc(choiceT_ps.sem, 1)
                if 5 in parts:
                    pe.wait_ge(choiceT_sb.sem, choiceT_sb.made(b, 0))
                    for k in range(NT):
                        ins_ = pe.matmul(gate_bank[:, k * D:(k + 1) * D], choiceT[:, k * P:(k + 1) * P], b2[:, :], start=True, stop=True)
                    ins_.then_inc(b2_ps.sem, 1)

            def second_product(n, e, reuse):
                pe.wait_ge(mid_sb.sem, mid_sb.made(n, FT - 1))
                if reuse:
                    pe.wait_ge(y_added.sem, y_added.made(n - 2, NT - 1))
                for k in range(NT):
                    for f in range(FT):
                        ins = pe.matmul(y_bank[e % 2][:, k * D:(k + 1) * D], mid[:, e % 2, f, k * P:(k + 1) * P], w2[:, e, f, :],
                                        start=(f == 0), stop=(f == FT - 1))
                ins.then_inc(y_ps.sem, 1)

            def expert(b, e):
                n, very_first = b * E_ + e, isinstance(b, int) and b == 0
                if e == 0:
                    pe.wait_ge(hT_kept.sem, hT_kept.made(b, 0))
                    if very_first:
                        pe.wait_ge(experts_in, 32)
                for f in range(FT):
                    if e or not very_first:
                        pe.wait_ge(mid_sb.sem, mid_sb.made(n - 1, f))
                    pe.matmul(mid_bank[f][:, :], w1[:, e, f * P:(f + 1) * P], hT_all[:, b, :], start=True,
                              stop=True).then_inc(mid_ps.sem, 1)
                if e or not very_first:
                    second_product(n - 1, (e - 1) % E_, e >= 3 or not very_first)

            stream(pe, prepare, expert)
            second_product(M - 1, E_ - 1, True)


QK_TILES = 2 * L1_ATT.heads * L1_ATT.width // P
V_HALVES = L1_ATT.heads * L1_ATT.width // N


def prep_l1(nc, g, ins, scratch):
    a = L1_ATT
    with ExitStack() as ctx:
        sb = lambda name, shape, dt=F32: ctx.enter_context(nc.sbuf_tensor(name + "_g", shape, dt))
        sem = phase_semaphores(nc, ctx, "_g")
        pb = lambda name: ctx.enter_context(nc.psum_tensor(name + "_ps_g", [P, N], F32))
        xnT_bank, bank = pb("xnT"), [pb(f"ring{i}") for i in range(4)]
        w = sb("w", [P, 3 * a.heads * a.width])
        stats, mv, var_eps, rstd = sb("stats", [P, NT, 6]), sb("mv", [P, NT, 2]), sb("var_eps", [P, NT]), sb("rstd", [P, NT])
        xn, xnT = sb("xn", [P, NT, D]), sb("xnT", [P, 2, N])
        parts = sb("parts", [P, QK_TILES, 2, N], F16)
        v = sb("v", [P, a.groups, NT, HG, a.width])
        v_cols = NT * V_HALVES
        own, w_loaded, out_loaded = sem("own"), sem("w_loaded"), sem("out_loaded")
        made = lambda name, per=1, credit=0, unit=1: Product(sem(name), per, credit, unit)
        moments, rstd_ready, zn_ready = made("moments"), made("rstd_ready"), made("xn_ready", NT, NT)
        xnT_ps, xnT_sb = made("xnT_ps", 1, 1), made("xnT_sb")
        tile_ps, part0, part1 = made("tile_ps", QK_TILES), made("part0", QK_TILES), made("part1", QK_TILES, QK_TILES)
        v_ps, v_sb = made("v_ps", v_cols), made("v_sb", v_cols, v_cols)
        parts_stored = [made(f"parts_stored{i}", 1, 1, 16) for i in range(QK_TILES)]
        v_stored = made("v_stored", NT, NT, 16)
        block = ctx.enter_context(nc.Block())

        @block.sync
        def _(sp):
            sp.dma_start(w[:, :], ins["L1_attn_w_qkv"]).then_inc(w_loaded, 16)
            sp.dma_start(g.w_out[:, :, :], ins["L1_attn_w_out"].rearrange("(c p) d -> p c d", p=P)).then_inc(out_loaded, 16)
            sp.dma_start(g.b_out[:, :], ins["L1_attn_b_out"].partition_broadcast(P)).then_inc(out_loaded, 16)
            for i in range(QK_TILES):
                sp.sem_inc(parts_stored[i].sem, 16)
            sp.sem_inc(v_stored.sem, 16 * NT)
            with sp.Fori(0, B) as b:
                for i in range(QK_TILES):
                    sp.wait_ge(part1.sem, part1.made(b, i))
                    s, j = i // (QK_TILES // 2), i % (QK_TILES // 2)
                    per = P // (HG * a.width)
                    sp.dma_start(scratch.qk[s].rearrange("r (b j g) h d t -> b j (g h d) r t", b=B, g=per)[b, j],
                                 parts[:, i, :, :]).then_inc(parts_stored[i].sem, 16)
                for k in range(NT):
                    wait_ge(sp, v_sb.sem, v_sb.made(b, (k + 1) * V_HALVES - 1), g.passed)
                    sp.dma_start(scratch.v.rearrange("(b g) p k h c -> b k p g (h c)", b=B)[b, k],
                                 v[:, :, k, :, :].rearrange("p g h c -> p g (h c)")).then_inc(v_stored.sem, 16)
            for i in range(QK_TILES):
                sp.wait_ge(parts_stored[i].sem, parts_stored[i].made(B - 1, 0))
            sp.wait_ge(v_stored.sem, v_stored.made(B - 1, NT - 1))
            sp.wait_ge(out_loaded, 32)

        @block.gpsimd
        def _(pool):
            with pool.Fori(0, B) as b:
                pool.wait_ge(moments.sem, moments.made(b, 0))
                pool.tensor_tensor(rstd[:, :], var_eps[:, :], g.minus_half[:, 0:NT], ALU.pow).then_inc(rstd_ready.sem, 1)

        @block.vector
        def _(dve):
            dve.sem_inc(part1.sem, QK_TILES)

            def normalise(b, it):
                me = Own(dve, own, 2 * NT, it)
                for k in range(NT):
                    me.did(dve.bn_stats(stats[:, k, :], g.x[:, b * NT + k, :]))
                me.settle(g.passed)
                for k in range(NT):
                    me.did(dve.bn_aggr(mv[:, k, :], stats[:, k, :]))
                me.settle()
                dve.tensor_scalar(var_eps[:, :], mv[:, :, 1], LN_EPS, None, ALU.add).then_inc(moments.sem, 1)
                dve.wait_ge(rstd_ready.sem, rstd_ready.made(it, 0))
                dve.wait_ge(xnT_ps.sem, xnT_ps.made_before(it, 0))
                for k in range(NT):
                    dve.tensor_scalar(xn[:, k, :], g.x[:, b * NT + k, :], mv[:, k, 0:1], rstd[:, k:k + 1],
                                      ALU.subtract, ALU.mult).then_inc(zn_ready.sem, 1)

            with dve.Fori(0, B) as b:
                normalise(b, b)
                for i in range(QK_TILES):
                    dve.wait_ge(part0.sem, part0.made(b, i))
                    dve.tensor_tensor(parts[:, i, 1, :], bank[i % 4][:, :], parts[:, i, 0, :], ALU.subtract).then_inc(part1.sem, 1)

        @block.scalar
        def _(act):
            act.sem_inc(v_sb.sem, v_cols)
            with act.Fori(0, B) as b:
                act.wait_ge(xnT_ps.sem, xnT_ps.made(b, 0))
                act.copy(xnT[:, 0, :], xnT_bank[:, :]).then_inc(xnT_sb.sem, 1)
                for i in range(QK_TILES):
                    act.wait_ge(tile_ps.sem, tile_ps.made(b, i))
                    act.wait_ge(parts_stored[i].sem, parts_stored[i].made_before(b, 0))
                    act.copy(parts[:, i, 0, :], bank[i % 4][:, :]).then_inc(part0.sem, 1)
                act.wait_ge(v_stored.sem, v_stored.made_before(b, NT - 1))
                for i in range(v_cols):
                    k, half = i // V_HALVES, i % V_HALVES
                    gs = slice(half * a.groups // V_HALVES, (half + 1) * a.groups // V_HALVES)
                    act.wait_ge(v_ps.sem, v_ps.made(b, i))
                    act.copy(v[:, gs, k, :, :],
                             bank[i % 4][:, :].rearrange("p (g h d) -> p g h d", h=HG, d=a.width)).then_inc(v_sb.sem, 1)

        @block.tensor
        def _(pe):
            pe.wait_ge(w_loaded, 16)
            pe.sem_inc(xnT_ps.sem, 1)
            with pe.Fori(0, B) as b:
                pe.wait_ge(zn_ready.sem, b * NT + NT)
                for k in range(NT):
                    ins_ = pe.transpose(xnT_bank[:, k * P:(k + 1) * P], xn[:, k, :], g.ident[:, :])
                ins_.then_inc(xnT_ps.sem, 1)
                pe.wait_ge(xnT_sb.sem, xnT_sb.made(b, 0))
                for i in range(QK_TILES):
                    if i < 4:
                        pe.wait_ge(v_sb.sem, v_sb.made_before(b, v_cols - 4 + i))
                    else:
                        pe.wait_ge(part1.sem, part1.made(b, i - 4))
                    pe.matmul(bank[i % 4][:, :], w[:, i * P:(i + 1) * P], xnT[:, 0, :], start=True, stop=True).then_inc(tile_ps.sem, 1)
                for i in range(v_cols):
                    k, half = i // V_HALVES, i % V_HALVES
                    if i < 4:
                        pe.wait_ge(part1.sem, part1.made(b, QK_TILES - 4 + i))
                    else:
                        pe.wait_ge(v_sb.sem, v_sb.made(b, i - 4))
                    at = QK_TILES * P + half * N
                    pe.matmul(bank[i % 4][:, :], xnT[:, 0, k * P:(k + 1) * P], w[:, at:at + N], start=True,
                              stop=True).then_inc(v_ps.sem, 1)


L1_EPS = 1e-6


def post_l1(nc, g, ins, out):
    with ExitStack() as ctx:
        sb = lambda name, shape, dt=F32: ctx.enter_context(nc.sbuf_tensor(name + "_h", shape, dt))
        sem = phase_semaphores(nc, ctx, "_h")
        pb = lambda name: ctx.enter_context(nc.psum_tensor(name + "_ps_h", [P, N], F32))
        xnT_bank, f_bank, filter_bank = [pb(f"xnT{s}") for s in range(2)], [pb(f"f{s}") for s in range(2)], pb("filter")
        rows = sb("rows", [P, 3, D])
        fourier, wf, filt, half = sb("fourier", [P, 3, D]), sb("wf", [P, 2, D]), sb("filter", [P, D]), sb("half", [P, 2, D])
        stats, mv = sb("stats", [P, 2, NT, 6]), sb("mv", [P, 2, NT, 2])
        var_eps, rstd = sb("var_eps", [P, 2, NT]), sb("rstd", [P, 2, NT])
        xn, xnT, res = sb("xn", [P, 2, NT, D]), sb("xnT", [P, 2, N]), sb("res", [P, 2, NT, D])
        own, w_loaded = sem("own"), sem("w_loaded")
        half_ps, half_sb, filt_ps, filt_sb = sem("half_ps"), sem("half_sb"), sem("filt_ps"), sem("filt_sb")
        made = lambda name, per=1, credit=0: Product(sem(name), per, credit)
        moments, rstd_ready = made("moments", 4), made("rstd_ready", 4)
        x_beta, y_bias, y_whole = made("x_beta", 2), made("y_bias", 2), made("y_whole", 2)
        xn_ready, xnT_ps, xnT_sb = made("xn_ready", 2 * NT), made("xnT_ps", 2), made("xnT_sb", 2)
        f_ps, res_ready = made("f_ps", 2), made("res_ready", 2, 2)
        stored = [sem(f"stored{s}") for s in range(2)]
        row = lambda n: rows[:, n, :].unsqueeze(1).broadcast_to([P, NT, D])
        of_batch = lambda buf, pair, s: buf[:, bass.ds((pair * 2 + s) * NT, NT), :]
        block = ctx.enter_context(nc.Block())

        @block.sync
        def _(sp):
            for n, name in enumerate(("L1_attn_ln_gamma", "L1_attn_ln_beta", "L1_ffn_bias")):
                sp.dma_start(rows[:, n, :], ins[name].partition_broadcast(P)).then_inc(w_loaded, 16)
            for n, name in enumerate(("L1_ffn_w_freq_real", "L1_ffn_w_freq_imag")):
                sp.dma_start(wf[:, n, :], ins[name]).then_inc(w_loaded, 16)
            sp.dma_start(fourier[:, :, :], ins["fourier"]).then_inc(w_loaded, 16)
            for s in range(2):
                sp.sem_inc(stored[s], 16)
            with sp.Fori(0, B // 2) as pair:
                for s in range(2):
                    sp.wait_ge(res_ready.sem, res_ready.made(pair, s))
                    sp.dma_start(out.rearrange("b (k p) d -> b p k d", p=P)[pair * 2 + s], res[:, s, :, :]).then_inc(stored[s], 16)
            for s in range(2):
                sp.wait_ge(stored[s], 16 * (B // 2 + 1))

        @block.gpsimd
        def _(pool):
            pool.wait_ge(w_loaded, 16 * 6)
            with pool.Fori(0, B // 2) as pair:
                def reciprocal_std(i, s):
                    pool.wait_ge(moments.sem, moments.made(pair, 2 * i + s))
                    pool.tensor_tensor(rstd[:, s, :], var_eps[:, s, :], g.minus_half[:, 0:NT], ALU.pow).then_inc(rstd_ready.sem, 1)

                reciprocal_std(0, 0)
                reciprocal_std(0, 1)
                for s in range(2):
                    pool.tensor_tensor(of_batch(g.x, pair, s), of_batch(g.x, pair, s), row(1), ALU.add).then_inc(x_beta.sem, 1)
                    pool.wait_ge(x_beta.sem, x_beta.made(pair, s))
                reciprocal_std(1, 0)
                reciprocal_std(1, 1)
                for s in range(2):
                    pool.wait_ge(xn_ready.sem, xn_ready.made(pair, s * NT + NT - 1))
                    pool.tensor_tensor(of_batch(g.y, pair, s), of_batch(g.y, pair, s), row(2), ALU.add).then_inc(y_bias.sem, 1)
                    pool.wait_ge(y_bias.sem, y_bias.made(pair, s))

        @block.vector
        def _(dve):
            dve.wait_ge(w_loaded, 16 * 6)
            dve.wait_ge(half_ps, 1)
            dve.tensor_copy(half[:, :, :], filter_bank[:, 0:2 * D].rearrange("p (s d) -> p s d", s=2)).then_inc(half_sb, 1)
            dve.wait_ge(filt_ps, 1)
            dve.tensor_scalar(filt[:, :], filter_bank[:, 0:D], 1.0 / D, None, ALU.mult).then_inc(filt_sb, 1)
            dve.sem_inc(res_ready.sem, 2)
            with dve.Fori(0, B // 2) as pair:
                me = Own(dve, own, 2 * (5 * NT + 1), pair)
                y = lambda s, k: g.y[:, (pair * 2 + s) * NT + k, :]

                def moments_of(i, s, eps):
                    for k in range(NT):
                        me.did(dve.bn_stats(stats[:, s, k, :], y(s, k)))
                    me.settle(g.passed)
                    for k in range(NT):
                        me.did(dve.bn_aggr(mv[:, s, k, :], stats[:, s, k, :]))
                    me.settle()
                    dve.tensor_scalar(var_eps[:, s, :], mv[:, s, :, 1], eps, None, ALU.add).then_inc(moments.sem, 1)

                for s in range(2):
                    moments_of(0, s, L1_EPS)
                for s in range(2):
                    dve.wait_ge(rstd_ready.sem, rstd_ready.made(pair, s))
                    for k in range(NT):
                        me.did(dve.tensor_scalar(y(s, k), y(s, k), mv[:, s, k, 0:1], rstd[:, s, k:k + 1], ALU.subtract, ALU.mult))
                    me.settle()
                    whole = of_batch(g.y, pair, s)
                    me.did(dve.tensor_tensor(whole, whole, row(0), ALU.mult))
                    me.settle()
                    dve.wait_ge(x_beta.sem, x_beta.made(pair, s))
                    dve.tensor_tensor(whole, whole, of_batch(g.x, pair, s), ALU.add).then_inc(y_whole.sem, 1)
                    wait_ge(dve, y_whole.sem, y_whole.made(pair, s), g.passed)
                    moments_of(1, s, LN_EPS)
                for s in range(2):
                    dve.wait_ge(rstd_ready.sem, rstd_ready.made(pair, 2 + s))
                    for k in range(NT):
                        dve.tensor_scalar(xn[:, s, k, :], y(s, k), mv[:, s, k, 0:1], rstd[:, s, k:k + 1],
                                          ALU.subtract, ALU.mult).then_inc(xn_ready.sem, 1)
                for s in range(2):
                    dve.wait_ge(f_ps.sem, f_ps.made(pair, s))
                    dve.wait_ge(y_bias.sem, y_bias.made(pair, s))
                    dve.wait_ge(stored[s], 16 * pair + 16)
                    dve.tensor_tensor(res[:, s, :, :], f_bank[s][:, :].rearrange("p (k d) -> p k d", k=NT), of_batch(g.y, pair, s),
                                      ALU.add).then_inc(res_ready.sem, 1)
                me.close()

        @block.scalar
        def _(act):
            with act.Fori(0, B // 2) as pair:
                for s in range(2):
                    act.wait_ge(xnT_ps.sem, xnT_ps.made(pair, s))
                    act.copy(xnT[:, s, :], xnT_bank[s][:, :]).then_inc(xnT_sb.sem, 1)

        @block.tensor
        def _(pe):
            pe.wait_ge(w_loaded, 16 * 6)
            cos, sin, msin = (fourier[:, i, :] for i in range(3))
            pe.matmul(filter_bank[:, 0:D], wf[:, 0, :], cos, start=True, stop=False)
            pe.matmul(filter_bank[:, 0:D], wf[:, 1, :], sin, start=False, stop=True)
            pe.matmul(filter_bank[:, D:2 * D], wf[:, 1, :], cos, start=True, stop=False)
            pe.matmul(filter_bank[:, D:2 * D], wf[:, 0, :], msin, start=False, stop=True).then_inc(half_ps, 1)
            pe.wait_ge(half_sb, 1)
            pe.matmul(filter_bank[:, 0:D], half[:, 0, :], cos, start=True, stop=False)
            pe.matmul(filter_bank[:, 0:D], half[:, 1, :], msin, start=False, stop=True).then_inc(filt_ps, 1)
            pe.wait_ge(filt_sb, 1)
            with pe.Fori(0, B // 2) as pair:
                for s in range(2):
                    for k in range(NT):
                        pe.wait_ge(xn_ready.sem, xn_ready.made(pair, s * NT + k))
                        ins_ = pe.transpose(xnT_bank[s][:, k * P:(k + 1) * P], xn[:, s, k, :], g.ident[:, :])
                    ins_.then_inc(xnT_ps.sem, 1)
                for s in range(2):
                    pe.wait_ge(xnT_sb.sem, xnT_sb.made(pair, s))
                    pe.wait_ge(res_ready.sem, res_ready.made_before(pair, s))
                    for k in range(NT):
                        ins_ = pe.matmul(f_bank[s][:, k * D:(k + 1) * D], xnT[:, s, k * P:(k + 1) * P], filt[:, :], start=True, stop=True)
                    ins_.then_inc(f_ps.sem, 1)


def program(nc, ins, out):
    with ExitStack() as ctx:
        g = Shared()
        sb = lambda name, shape: ctx.enter_context(nc.sbuf_tensor(name, shape, F32))
        dram = lambda name, shape, dt=F32: nc.dram_tensor("scratch_" + name, shape, dt, kind="Internal").ap()
        g.x = sb("x_res", [P, T, D])
        g.ident = sb("ident", [P, P])
        g.minus_half = sb("minus_half", [P, 64])
        g.passed = ctx.enter_context(nc.semaphore("passed"))
        with ExitStack() as delta:
            sb_delta = lambda name, shape: delta.enter_context(nc.sbuf_tensor(name, shape, F32))
            g.head_mask = sb_delta("head_mask", [P, HA])
            g.two_eye = sb_delta("two_eye", [P, HA, P])
            g.fg_mask = sb_delta("fg_mask", [P, 2, HA, DA])
            scratch = Shared()
            scratch.packs, scratch.inv = dram("packs", (T, P, W_PACK)), dram("inv", (P, GB, LB, LB))
            setup(nc, g, ins)
            delta_front(nc, g, ins, scratch)
            delta_invert(nc, g, scratch)
            delta_back(nc, g, ins, scratch)

        def att_scratch(a):
            s = Shared()
            s.qk = dram("qk_" + a.name, (2, a.parts, a.total, HG, a.width, N), F16)
            s.v = dram("v_" + a.name, (a.total, P, NT, HG, a.width))
            return s

        with ExitStack() as ffn:
            sb_ffn = lambda name, shape: ffn.enter_context(nc.sbuf_tensor(name, shape, F32))
            g.z = sb_ffn("z_res", [P, T, D])
            g.wo = sb_ffn("wo", [P, L0_ATT.groups, D])
            scratch = att_scratch(L0_ATT)
            prep_l0(nc, g, ins, scratch)
            attention(nc, g, L0_ATT, scratch, g.wo, g.z, lambda tiles: g.z[:, tiles, :])
            moe(nc, g, ins)
        scratch = att_scratch(L1_ATT)
        g.y = sb("y", [P, T, D])
        g.w_out, g.b_out = sb("w_out", [P, L1_ATT.groups, D]), sb("b_out", [P, D])
        prep_l1(nc, g, ins, scratch)
        attention(nc, g, L1_ATT, scratch, g.w_out, g.y, lambda tiles: g.b_out[:, :].unsqueeze(1).broadcast_to([P, NT, D]))
        post_l1(nc, g, ins, out)


_INS = ['L0_attn_x', 'L0_attn_Wq', 'L0_attn_Wk', 'L0_attn_Wv', 'L0_attn_Wbeta', 'L0_attn_Wo', 'L0_attn_g_norm',
        'L0_ffn_ln1_g', 'L0_ffn_ln1_b', 'L0_ffn_ln2_g', 'L0_ffn_ln2_b', 'L0_ffn_wq', 'L0_ffn_bq', 'L0_ffn_wk',
        'L0_ffn_bk', 'L0_ffn_wv', 'L0_ffn_bv', 'L0_ffn_wo', 'L0_ffn_bo', 'L0_ffn_gate_w', 'L0_ffn_gate_b',
        'L0_ffn_w1', 'L0_ffn_b1', 'L0_ffn_w2', 'L0_ffn_b2', 'L1_attn_w_qkv', 'L1_attn_w_out', 'L1_attn_b_out',
        'L1_attn_ln_gamma', 'L1_attn_ln_beta', 'L1_ffn_w_freq_real', 'L1_ffn_w_freq_imag', 'L1_ffn_bias']


def fourier_rows():
    angle = 2.0 * np.pi * (np.outer(np.arange(D), np.arange(D)) % D) / D
    return np.ascontiguousarray(np.stack([np.cos(angle), np.sin(angle), -np.sin(angle)], axis=1).astype(np.float32))


def kernel(**inputs):
    import concourse.bacc as _bacc
    from concourse.bass_utils import run_bass_kernel_spmd as _run

    nc = _bacc.Bacc("TRN2", target_bir_lowering=False, num_devices=1)
    arrays = {f"in_{name}_dram": np.ascontiguousarray(inputs[name]) for name in _INS}
    arrays["in_fourier_dram"] = fourier_rows()
    ins = {name: nc.dram_tensor(f"in_{name}_dram", arrays[f"in_{name}_dram"].shape, F32, kind="ExternalInput").ap()
           for name in _INS + ["fourier"]}
    out = nc.dram_tensor("out_0_dram", (B, N, D), F32, kind="ExternalOutput").ap()
    program(nc, ins, out)
    r = _run(nc, [arrays], core_ids=[0])
    return r.results[0]["out_0_dram"]
```
